# Optimizing a Trainium2 kernel written in Bass

```python
import numpy as np
import jax
import jax.numpy as jnp

def _softmax(x, axis=-1):
    return jax.nn.softmax(x, axis=axis)

def _gelu(x):
    return jax.nn.gelu(x, approximate=True)

def _silu(x):
    return jax.nn.silu(x)

def _sigmoid(x):
    return jax.nn.sigmoid(x)

def _layernorm(x, axis=-1, eps=1e-05):
    m = jnp.mean(x, axis=axis, keepdims=True)
    v = jnp.var(x, axis=axis, keepdims=True)
    return (x - m) / jnp.sqrt(v + eps)

def _scatter_add(tgt, idx, src, axis=0):
    return tgt.at[idx].add(src)

def _segment_sum(src, seg, n):
    return jax.ops.segment_sum(src, seg, n)
kernel_name = 'mk_gps_d1_gnn_r8_e48662'

def setup_inputs(seed: int=0):
    np.random.seed(seed)
    _w = jnp.asarray

    def _rec_inputs():
        import jax
        import jax.numpy as jnp
        _gk = jax.random.key(seed)
        x = -0.0003713 + 1 * jax.random.normal(jax.random.fold_in(_gk, 1), (6250, 256), jnp.float32)
        src = jax.random.randint(jax.random.fold_in(_gk, 2), (200000,), 0, 6250, jnp.int32)
        dst = jax.random.randint(jax.random.fold_in(_gk, 3), (200000,), 0, 6250, jnp.int32)
        _o = jnp.argsort(dst, stable=True)
        src = src[_o]
        dst = dst[_o]
        edge_weight = 0.00107675 + 0.999702 * jax.random.normal(jax.random.fold_in(_gk, 12), (200000,), jnp.float32)
        node_vec1 = 0.00452826 + 1.00397 * jax.random.normal(jax.random.fold_in(_gk, 13), (6250, 1), jnp.float32)
        return (x, src, dst, edge_weight, node_vec1)
    x, src, dst, edge_weight, node_vec1 = _rec_inputs()

    def _L0_gnn_setup():
        import jax, jax.numpy as jnp
        import numpy as np
        IN_FEATURES = 6250
        OUT_FEATURES = 6250
        NNZ = 100000
        BATCH = 256
        key = jax.random.key(seed)
        k_x, k_row, k_col, k_val, k_b = jax.random.split(key, 5)
        x = jax.random.normal(k_x, (IN_FEATURES, BATCH), dtype=jnp.float32)
        row = jax.random.randint(k_row, (NNZ,), 0, OUT_FEATURES, dtype=jnp.int64)
        col = jax.random.randint(k_col, (NNZ,), 0, IN_FEATURES, dtype=jnp.int64)
        indices = jnp.stack([row, col], axis=0)
        values = jax.random.normal(k_val, (NNZ,), dtype=jnp.float32)
        bias = jax.random.normal(k_b, (OUT_FEATURES, 1), dtype=jnp.float32)
        return {'x': x, 'indices': indices, 'values': values, 'bias': bias}
    _L0_gnn_all = _L0_gnn_setup()
    _L0_gnn_in = {k: v for k, v in _L0_gnn_all.items() if k in ()}
    del _L0_gnn_all

    def _L0_mix_setup():
        import jax, jax.numpy as jnp
        import numpy as np
        import math
        EMBED = 256
        HEADS = 4
        HEAD_DIM = EMBED // HEADS
        OUT_DIM = 256
        LN_EPS = 1e-05

        def _qkv_init(key):
            spread = math.sqrt(3.0 / EMBED)
            gain, delta = (0.01, 0.01)
            w = jax.random.uniform(key, (EMBED, EMBED), minval=-spread, maxval=spread) * gain
            return w + delta * jnp.eye(EMBED, dtype=w.dtype)

        def _layer_norm(x, g, b):
            mu = jnp.mean(x, axis=-1, keepdims=True)
            var = jnp.mean(jnp.square(x - mu), axis=-1, keepdims=True)
            return (x - mu) * jax.lax.rsqrt(var + LN_EPS) * g + b

        def _split_heads(x, B, S):
            return x.reshape(B, S, HEADS, HEAD_DIM).transpose(0, 2, 1, 3)
        key = jax.random.key(seed)
        ks = jax.random.split(key, 6)
        seq = jax.random.normal(ks[0], (4, 1024, EMBED), dtype=jnp.float32)
        wq = _qkv_init(ks[1])
        wk = _qkv_init(ks[2])
        wv = _qkv_init(ks[3])
        bound = 1.0 / math.sqrt(EMBED)
        wo = jax.random.uniform(ks[4], (OUT_DIM, EMBED), minval=-bound, maxval=bound)
        bo = jax.random.uniform(ks[5], (OUT_DIM,), minval=-bound, maxval=bound)
        ln_k_g = jnp.ones((HEAD_DIM,), jnp.float32)
        ln_k_b = jnp.zeros((HEAD_DIM,), jnp.float32)
        ln_v_g = jnp.ones((HEAD_DIM,), jnp.float32)
        ln_v_b = jnp.zeros((HEAD_DIM,), jnp.float32)
        return {'seq': seq, 'wq': wq, 'wk': wk, 'wv': wv, 'wo': wo, 'bo': bo, 'ln_k_g': ln_k_g, 'ln_k_b': ln_k_b, 'ln_v_g': ln_v_g, 'ln_v_b': ln_v_b}
    _L0_mix_all = _L0_mix_setup()
    _L0_mix_in = {k: v for k, v in _L0_mix_all.items() if k in ('wq', 'wk', 'wv', 'wo', 'bo', 'ln_k_g', 'ln_k_b', 'ln_v_g', 'ln_v_b')}
    del _L0_mix_all

    def _L0_ffn_setup():
        import jax, jax.numpy as jnp
        import numpy as np
        D_MODEL = 256
        EXPERT_DIM = 512
        NUM_EXPERTS = 8
        TOP_K = 2
        SEQ_LEN = 256
        BATCH = 2
        key = jax.random.key(seed)
        ks = jax.random.split(key, 8)
        s = 0.02
        x = jax.random.normal(ks[0], (SEQ_LEN, BATCH, D_MODEL), dtype=jnp.float32)
        Wg = jax.random.normal(ks[1], (D_MODEL, NUM_EXPERTS), dtype=jnp.float32) * s
        bg = jax.random.normal(ks[2], (NUM_EXPERTS,), dtype=jnp.float32) * s
        bias = jnp.zeros((NUM_EXPERTS,), dtype=jnp.float32)
        W1 = jax.random.normal(ks[3], (NUM_EXPERTS, D_MODEL, EXPERT_DIM), dtype=jnp.float32) * s
        b1 = jax.random.normal(ks[4], (NUM_EXPERTS, EXPERT_DIM), dtype=jnp.float32) * s
        W2 = jax.random.normal(ks[5], (NUM_EXPERTS, EXPERT_DIM, D_MODEL), dtype=jnp.float32) * s
        b2 = jax.random.normal(ks[6], (NUM_EXPERTS, D_MODEL), dtype=jnp.float32) * s
        return {'x': x, 'Wg': Wg, 'bg': bg, 'bias': bias, 'W1': W1, 'b1': b1, 'W2': W2, 'b2': b2}
    _L0_ffn_all = _L0_ffn_setup()
    _L0_ffn_in = {k: v for k, v in _L0_ffn_all.items() if k in ('Wg', 'bg', 'bias', 'W1', 'b1', 'W2', 'b2')}
    del _L0_ffn_all
    return {'x': x, 'src': src, 'dst': dst, 'edge_weight': edge_weight, 'node_vec1': node_vec1, 'L0_mix_wq': _L0_mix_in['wq'], 'L0_mix_wk': _L0_mix_in['wk'], 'L0_mix_wv': _L0_mix_in['wv'], 'L0_mix_wo': _L0_mix_in['wo'], 'L0_mix_bo': _L0_mix_in['bo'], 'L0_mix_ln_k_g': _L0_mix_in['ln_k_g'], 'L0_mix_ln_k_b': _L0_mix_in['ln_k_b'], 'L0_mix_ln_v_g': _L0_mix_in['ln_v_g'], 'L0_mix_ln_v_b': _L0_mix_in['ln_v_b'], 'L0_ffn_Wg': _L0_ffn_in['Wg'], 'L0_ffn_bg': _L0_ffn_in['bg'], 'L0_ffn_bias': _L0_ffn_in['bias'], 'L0_ffn_W1': _L0_ffn_in['W1'], 'L0_ffn_b1': _L0_ffn_in['b1'], 'L0_ffn_W2': _L0_ffn_in['W2'], 'L0_ffn_b2': _L0_ffn_in['b2']}

def reference(x, src, dst, edge_weight, node_vec1, L0_mix_wq, L0_mix_wk, L0_mix_wv, L0_mix_wo, L0_mix_bo, L0_mix_ln_k_g, L0_mix_ln_k_b, L0_mix_ln_v_g, L0_mix_ln_v_b, L0_ffn_Wg, L0_ffn_bg, L0_ffn_bias, L0_ffn_W1, L0_ffn_b1, L0_ffn_W2, L0_ffn_b2):
    import jax
    import jax.numpy as jnp

    def _L0_gnn_ref(x, indices, values, bias):
        import jax, jax.numpy as jnp
        import numpy as np
        IN_FEATURES = 6250
        OUT_FEATURES = 6250
        NNZ = 100000
        BATCH = 256
        row, col = (indices[0], indices[1])
        gathered = values[:, None] * x[col]
        out = jax.ops.segment_sum(gathered, row, num_segments=OUT_FEATURES)
        out = out + bias
        return out

    def _L0_mix_ref(seq, wq, wk, wv, wo, bo, ln_k_g, ln_k_b, ln_v_g, ln_v_b):
        import jax, jax.numpy as jnp
        import numpy as np
        import math
        EMBED = 256
        HEADS = 4
        HEAD_DIM = EMBED // HEADS
        OUT_DIM = 256
        LN_EPS = 1e-05

        def _qkv_init(key):
            spread = math.sqrt(3.0 / EMBED)
            gain, delta = (0.01, 0.01)
            w = jax.random.uniform(key, (EMBED, EMBED), minval=-spread, maxval=spread) * gain
            return w + delta * jnp.eye(EMBED, dtype=w.dtype)

        def _layer_norm(x, g, b):
            mu = jnp.mean(x, axis=-1, keepdims=True)
            var = jnp.mean(jnp.square(x - mu), axis=-1, keepdims=True)
            return (x - mu) * jax.lax.rsqrt(var + LN_EPS) * g + b

        def _split_heads(x, B, S):
            return x.reshape(B, S, HEADS, HEAD_DIM).transpose(0, 2, 1, 3)
        B, S, _ = seq.shape
        q = _split_heads(seq @ wq.T, B, S)
        k = _split_heads(seq @ wk.T, B, S)
        v = _split_heads(seq @ wv.T, B, S)
        k = _layer_norm(k, ln_k_g, ln_k_b)
        v = _layer_norm(v, ln_v_g, ln_v_b)
        kv = jnp.einsum('bhsd,bhse->bhde', k, v) / S
        ga = jnp.einsum('bhsd,bhde->bhse', q, kv)
        ga = ga.transpose(0, 2, 1, 3).reshape(B, S, EMBED)
        return ga @ wo.T + bo

    def _L0_ffn_ref(x, Wg, bg, bias, W1, b1, W2, b2):
        import jax, jax.numpy as jnp
        import numpy as np
        D_MODEL = 256
        EXPERT_DIM = 512
        NUM_EXPERTS = 8
        TOP_K = 2
        SEQ_LEN = 256
        BATCH = 2
        x_flat = x.reshape(-1, D_MODEL)
        gate_logits = x_flat @ Wg + bg + bias
        topk_vals, topk_idx = jax.lax.top_k(gate_logits, TOP_K)
        topk_w = jax.nn.softmax(topk_vals, axis=-1)
        combine = (jax.nn.one_hot(topk_idx, NUM_EXPERTS, dtype=x.dtype) * topk_w[..., None]).sum(axis=1)
        h = jax.nn.relu(jnp.einsum('td,edh->teh', x_flat, W1) + b1)
        y = jnp.einsum('teh,ehd->ted', h, W2) + b2
        out = jnp.einsum('ted,te->td', y, combine)
        return out.reshape(x.shape)
    edge_index = jnp.stack([src, dst])
    xn = _layernorm(x, axis=-1)
    x = x + _L0_gnn_ref(xn, edge_index, edge_weight, node_vec1) + _L0_mix_ref(xn[None], L0_mix_wq, L0_mix_wk, L0_mix_wv, L0_mix_wo, L0_mix_bo, L0_mix_ln_k_g, L0_mix_ln_k_b, L0_mix_ln_v_g, L0_mix_ln_v_b)[0]
    x = x + _L0_ffn_ref(_layernorm(x, axis=-1)[None], L0_ffn_Wg, L0_ffn_bg, L0_ffn_bias, L0_ffn_W1, L0_ffn_b1, L0_ffn_W2, L0_ffn_b2)[0]
    return x

_drawn_inputs = setup_inputs


def setup_inputs(seed=0):
    import zlib

    import numpy as np

    out = dict(_drawn_inputs(seed))
    spreads = {'L0_mix_ln_k_g': (1.0, 0.6),
     'L0_mix_ln_k_b': (0.0, 0.8),
     'L0_mix_ln_v_g': (1.0, 0.6),
     'L0_mix_ln_v_b': (0.0, 0.8),
     'L0_ffn_bias': (0.0, 0.8)}
    factors = {'L0_mix_wq': 8.0,
     'L0_mix_wk': 8.0,
     'L0_mix_wv': 8.0,
     'L0_mix_wo': 8.0,
     'L0_mix_bo': 8.0,
     'L0_ffn_Wg': 5.237,
     'L0_ffn_bg': 8.0,
     'L0_ffn_W1': 5.474,
     'L0_ffn_b1': 8.0,
     'L0_ffn_W2': 4.491,
     'L0_ffn_b2': 23.792}
    for name, (base, spread) in spreads.items():
        noise = np.random.default_rng([zlib.crc32(name.encode()), seed]).standard_normal(out[name].shape)
        drawn = base * np.exp(spread * noise) if base else spread * noise
        out[name] = jnp.asarray(drawn.astype(out[name].dtype))
    for name, factor in factors.items():
        out[name] = (out[name] * factor).astype(out[name].dtype)
    return out
```

```python
from contextlib import ExitStack

import numpy as np

import concourse.bass as bass
from concourse import mybir

P = 128
F32 = mybir.dt.float32
F32R = mybir.dt.float32r
I32 = mybir.dt.int32
BF16 = mybir.dt.bfloat16
ALU = mybir.AluOpType
ACT = mybir.ActivationFunctionType
AX = mybir.AxisListType
EPS = 1e-5

CH = 28
SW = CH + 1
GRP = 7
BU = 7
NB = 50


def gps_layer(nc, x, src, dst, edge_weight, node_vec1, wq, wk, wv, wo, bo, kg, kb, vg, vb,
         Wg, bg, bias, W1, b1, W2, b2, out):
    N, D = x.shape
    E = src.shape[0]
    SC = CH * P
    G = -(-E // SC)
    NT = -(-N // P)
    TAIL = N - (NT - 1) * P
    NG = G // GRP
    assert D == 2 * P and G == NG * GRP and NT == GRP * BU and NG % 2 == 0 and NB == NT + 1
    HD = kg.shape[0]
    H = D // HD
    FULL = E - (G - 1) * SC
    TP = FULL // CH
    TR = FULL - TP * CH

    xn_dram = nc.dram_tensor("xn_dram", (NT * P, D), F32, kind="Internal").ap()

    rows_dram = nc.dram_tensor("rows_dram", (NT * P, D), F32, kind="Internal").ap()

    with ExitStack() as ctx:
        def sb(name, shape, dt=F32, c=ctx):
            return c.enter_context(nc.sbuf_tensor(name, shape, dt))

        ident = sb("ident", [P, P])
        iota = sb("iota", [P, P])
        iota1 = sb("iota1", [P, P])
        ones_row = sb("ones_row", [1, P])
        before = sb("before", [P, P], F32R)
        banks = [ctx.enter_context(nc.psum_tensor(f"bank{i}", [P, 512], F32)) for i in range(8)]
        with ExitStack() as c1:
            acc = sb("acc", [P, NT, D], F32, c1)
            shared = (banks, acc, ident, iota, iota1, ones_row, before)
            constants(nc, shared)
            with ExitStack() as c2:
                edges = edge_lists(nc, c2, shared, src, dst, edge_weight, E, G, TP, TR, N)
                attention(nc, shared, x, node_vec1, wq, wk, wv, wo, bo, kg, kb, vg, vb, xn_dram, NT, TAIL, N, D, H, HD)
                edge_sum(nc, shared, edges, xn_dram, G, NG, NT, D)
                stragglers(nc, shared, edges, src, dst, xn_dram, E, G, TP, TR, NT, D)
            put_rows(nc, shared, rows_dram, NT)
        experts(nc, banks, rows_dram, ident, iota, ones_row, Wg, bg, bias, W1, b1, W2, b2, out, NT, TAIL, N, D)


def constants(nc, shared):
    banks, acc, ident, iota, iota1, ones_row, before = shared
    with ExitStack() as ctx:
        ints = ctx.enter_context(nc.sbuf_tensor("ints", [P, 2, P], I32))
        iota_done = ctx.enter_context(nc.semaphore("iota_done"))
        cast_done = ctx.enter_context(nc.semaphore("cast_done"))
        block = ctx.enter_context(nc.Block())

        @block.gpsimd
        def _(pool):
            pool.iota(ints[:, 0, :], [[1, P]], base=0, channel_multiplier=0).then_inc(iota_done, 1)
            pool.iota(ints[:, 1, :], [[1, P]], base=0, channel_multiplier=-1).then_inc(iota_done, 1)

        @block.vector
        def _(dve):
            dve.memset(ones_row[:, :], 1.0)
            dve.wait_ge(iota_done, 2)
            dve.tensor_copy(iota[:, :], ints[:, 0, :]).then_inc(cast_done, 1)
            dve.tensor_scalar(ident[:, :], ints[:, 1, :], 0.0, None, ALU.is_equal)
            dve.tensor_scalar(before[:, :], ints[:, 1, :], 0.0, None, ALU.is_gt)
            dve.wait_ge(cast_done, 1)
            dve.tensor_scalar(iota1[:, :], iota[:, :], 1.0, None, ALU.add)


def edge_lists(nc, keep, shared, src, dst, edge_weight, E, G, TP, TR, N):
    banks, acc, ident, iota, iota1, ones_row, before = shared
    SC = CH * P

    def kb(name, shape, dt=F32):
        return keep.enter_context(nc.sbuf_tensor(name, shape, dt))

    bucket = kb("bucket", [P, G, CH])
    weight = kb("weight", [P, G, CH])
    packed = kb("packed", [P, G, CH])
    inside = kb("inside", [P, G, CH], BF16)
    w_left = kb("w_left", [P, G, CH])
    n_left = kb("n_left", [P, G])
    rows_i = kb("rows_i", [P, G], I32)
    with ExitStack() as ctx:
        def sb(name, shape, dt=F32):
            return ctx.enter_context(nc.sbuf_tensor(name, shape, dt))

        dst_i = sb("dst_i", [P, G, CH], I32)
        local = sb("local", [P, G, CH])
        src_i = sb("src_i", [P, G, CH], I32)
        tmp_i = sb("tmp_i", [P, G, CH], I32)
        off = sb("off", [P, G, CH])
        first_i = sb("first_i", [1, G], I32)
        first = sb("first", [1, G])
        start = sb("start", [P, G])
        lane_i = sb("lane_i", [P, 1], I32)
        lane = sb("lane", [P, 1])
        padded = ctx.enter_context(nc.semaphore("padded"))
        loaded = ctx.enter_context(nc.semaphore("loaded"))
        lane_done = ctx.enter_context(nc.semaphore("lane_done"))
        first_done = ctx.enter_context(nc.semaphore("first_done"))
        start_done = ctx.enter_context(nc.semaphore("start_done"))
        step = ctx.enter_context(nc.semaphore("step"))
        block = ctx.enter_context(nc.Block())
        NL = 3 * 3 + 1

        @block.sync
        def _(sp):
            sp.wait_ge(padded, 3)
            for arr, to in ((dst, dst_i), (src, src_i), (edge_weight, weight)):
                body = arr[0:(G - 1) * SC].rearrange("(g p c) -> p g c", p=P, c=CH)
                sp.dma_start(to[:, 0:G - 1, :], body).then_inc(loaded, 16)
                tail = arr[(G - 1) * SC:(G - 1) * SC + TP * CH].rearrange("(p c) -> p c", c=CH)
                sp.dma_start(to[0:TP, G - 1, :], tail).then_inc(loaded, 16)
                rest = arr[E - TR:E].rearrange("(a c) -> a c", a=1)
                sp.dma_start(to[TP:TP + 1, G - 1, 0:TR], rest).then_inc(loaded, 16)
            with nc.allow_non_contiguous_dma(reason="one element per superchunk"):
                sp.dma_start(first_i[0:1, 0:G - 1], dst[0:(G - 1) * SC].rearrange("(a g s) -> a g s", a=1, s=SC)[:, :, 0]).then_inc(loaded, 16)
                sp.dma_start(first_i[0:1, G - 1:G], dst[(G - 1) * SC:(G - 1) * SC + 1].rearrange("(a b) -> a b", a=1)).then_inc(loaded, 16)

        @block.gpsimd
        def _(pool):
            pool.iota(lane_i[:, :], [[0, 1]], base=0, channel_multiplier=1).then_inc(lane_done, 1)

        @block.tensor
        def _(pe):
            pe.wait_ge(first_done, 1)
            pe.matmul(banks[0][:, 0:G], ones_row[:, :], first[:, :], start=True, stop=True).then_inc(start_done, 1)

        @block.vector
        def _(dve):
            n = [0]

            def then(ins):
                n[0] += 1
                ins.then_inc(step, 1)
                dve.wait_ge(step, n[0])

            dve.memset(src_i[:, G - 1, :], NB * P).then_inc(padded, 1)
            dve.memset(dst_i[:, G - 1, :], 0).then_inc(padded, 1)
            dve.memset(weight[:, G - 1, :], 0.0).then_inc(padded, 1)
            dve.wait_ge(loaded, 16 * (NL + 1))
            dve.tensor_scalar(first[:, :], first_i[:, :], float(N - P), None, ALU.min).then_inc(first_done, 1)
            then(dve.tensor_scalar(tmp_i[:, :, :], src_i[:, :, :], 7, None, ALU.logical_shift_right))
            then(dve.tensor_copy(bucket[:, :, :], tmp_i[:, :, :]))
            then(dve.tensor_scalar(tmp_i[:, :, :], src_i[:, :, :], P - 1, None, ALU.bitwise_and))
            then(dve.tensor_copy(local[:, :, :], tmp_i[:, :, :]))
            dve.wait_ge(start_done, 1)
            then(dve.tensor_copy(start[:, :], banks[0][:, 0:G]))
            then(dve.tensor_tensor(off[:, :, :], dst_i[:, :, :], start[:, :].unsqueeze(2).broadcast_to([P, G, CH]), ALU.subtract))
            then(dve.scalar_tensor_tensor(out=packed[:, :, :], in0=off[:, :, :], scalar=float(P), in1=local[:, :, :], op0=ALU.mult, op1=ALU.add))
            then(dve.tensor_scalar(inside[:, :, :], off[:, :, :], 0.0, None, ALU.is_ge))
            then(dve.scalar_tensor_tensor(out=inside[:, :, :], in0=off[:, :, :], scalar=float(P), in1=inside[:, :, :], op0=ALU.is_lt, op1=ALU.mult))
            then(dve.scalar_tensor_tensor(out=inside[:, :, :], in0=bucket[:, :, :], scalar=float(NB), in1=inside[:, :, :], op0=ALU.is_equal, op1=ALU.max))
            dve.wait_ge(lane_done, 1)
            then(dve.tensor_copy(lane[:, :], lane_i[:, :]))
            then(dve.tensor_scalar(rows_i[:, :], start[:, :], lane[:, 0:1], None, ALU.add))
    return bucket, weight, packed, inside, w_left, n_left, rows_i


def merge_stats(dve, then, stats, mv, D):
    even, odd = stats[:, :, 1], stats[:, :, 4]
    then(dve.tensor_tensor(mv[:, 1, :], even, odd, ALU.subtract))
    then(dve.tensor_tensor(mv[:, 1, :], mv[:, 1, :], mv[:, 1, :], ALU.mult))
    then(dve.tensor_scalar(mv[:, 1, :], mv[:, 1, :], D / 4.0, None, ALU.mult))
    then(dve.tensor_tensor(mv[:, 0, :], stats[:, :, 2], stats[:, :, 5], ALU.add))
    then(dve.tensor_tensor(mv[:, 1, :], mv[:, 0, :], mv[:, 1, :], ALU.add))
    then(dve.tensor_scalar(mv[:, 1, :], mv[:, 1, :], 1.0 / D, None, ALU.mult))
    then(dve.tensor_tensor(mv[:, 0, :], even, odd, ALU.add))
    then(dve.tensor_scalar(mv[:, 0, :], mv[:, 0, :], 0.5, None, ALU.mult))


def attention(nc, shared, x, node_vec1, wq, wk, wv, wo, bo, kg, kb, vg, vb, xn_dram, NT, TAIL, N, D, H, HD):
    banks, acc, ident, iota, iota1, ones_row, before = shared
    KV = 2 * D
    HH = 2 * H
    with ExitStack() as ctx:
        def sb(name, shape, dt=F32):
            return ctx.enter_context(nc.sbuf_tensor(name, shape, dt))

        def sem(name):
            return ctx.enter_context(nc.semaphore(name))

        xn = [sb(f"xn{i}", [P, D]) for i in range(2)]
        xT = [sb(f"xT{i}", [P, 2, P]) for i in range(2)]
        xT_all = sb("xT_all", [P, NT, 2, P])
        sq = sb("sq", [P, KV])
        hat = [sb(f"hat{i}", [P, KV]) for i in range(2)]
        kvn = [sb(f"kvn{i}", [P, KV]) for i in range(2)]
        w_nat = sb("w_nat", [P, 4, 2, D])
        wkvT = sb("wkvT", [P, 2, KV])
        woT = sb("woT", [P, 2, D])
        vecs = sb("vecs", [1, D + 4 * HD])
        gain = sb("gain", [P, KV])
        shift = sb("shift", [P, KV])
        bo_b = sb("bo_b", [P, D])
        nv = sb("nv", [P, NT])
        stats = sb("stats", [P, NT, 6])
        mv = sb("mv", [P, 2, NT])
        dev = sb("dev", [P, NT])
        rstd = sb("rstd", [P, NT])
        hsum = sb("hsum", [P, 2, HH])
        ss = sb("ss", [P, HH])
        hdev = sb("hdev", [P, HH])
        hinv = sb("hinv", [P, HH])
        kvT = sb("kvT", [P, 2, P])
        R = sb("R", [P, 2, D])
        M = sb("M", [P, 2, D])
        eps = sb("eps", [P, 1])
        turn_ps, proj_ps, kv_ps, mix_ps = banks[0:2], banks[2:4], banks[4:6], banks[6:8]

        x_in = sem("x_in"); w_in = sem("w_in"); nv_in = sem("nv_in")
        cleared = sem("cleared")
        w_turned = sem("w_turned"); spread = sem("spread"); w_ready = sem("w_ready")
        var_done = sem("var_done"); dev_done = sem("dev_done")
        xn_done = sem("xn_done"); stored = sem("stored"); xn_free = sem("xn_free")
        turned = sem("turned"); xT_done = sem("xT_done"); proj = sem("proj")
        squared = sem("squared"); summed = sem("summed"); rooted = sem("rooted"); inverted = sem("inverted")
        hat_done = sem("hat_done"); gained = sem("gained"); kvn_done = sem("kvn_done"); kv_used = sem("kv_used")
        kvT_done = sem("kvT_done"); R_made = sem("R_made"); R_done = sem("R_done")
        M_made = sem("M_made"); M_done = sem("M_done"); copied = sem("copied")
        xT_back = sem("xT_back"); mixed = sem("mixed"); added = sem("added")
        step = sem("step"); aggr = sem("aggr")
        block = ctx.enter_context(nc.Block())
        NW = 4 + 5
        LAST = NT - 1

        def tiles(eng, one):
            one(0, 0)
            with eng.Fori(0, (NT - 3) // 2) as h:
                one(2 * h + 1, 1)
                one(2 * h + 2, 0)
            one(NT - 2, 1)
            one(NT - 1, 0)

        def pairs(eng, one):
            with eng.Fori(0, NT // 2) as h:
                one(2 * h, 0)
                one(2 * h + 1, 1)
            one(NT - 1, 0)

        @block.sync
        def _(sp):
            sp.wait_ge(cleared, 2)
            for i, w in enumerate((wq, wk, wv, wo)):
                sp.dma_start(w_nat[:, i, :, :], w.rearrange("(m p) d -> p m d", p=P)).then_inc(w_in, 16)
            sp.dma_start(vecs[:, 0:D], bo.rearrange("(a d) -> a d", a=1)).then_inc(w_in, 16)
            for i, v in enumerate((kg, vg, kb, vb)):
                sp.dma_start(vecs[:, D + i * HD:D + (i + 1) * HD], v.rearrange("(a d) -> a d", a=1)).then_inc(w_in, 16)
            sp.dma_start(acc[0:TAIL, LAST, :], x[LAST * P:N, :]).then_inc(x_in, 16)
            sp.dma_start(acc[:, 0:LAST, :], x[0:LAST * P, :].rearrange("(t p) d -> p t d", p=P)).then_inc(x_in, 16)
            with nc.allow_non_contiguous_dma(reason="one value per node"):
                sp.dma_start(nv[:, 0:LAST], node_vec1[0:LAST * P, :].rearrange("(t p) a -> p (t a)", p=P)).then_inc(nv_in, 16)
                sp.dma_start(nv[0:TAIL, LAST:NT], node_vec1[LAST * P:N, :]).then_inc(nv_in, 16)
            sp.sem_inc(xn_free, 2)

            def store(t, i):
                sp.wait_ge(xn_done, t + 1)
                sp.dma_start(xn_dram[bass.ds(t * P, P), :], xn[i][:, :]).then_inc(stored, 16)
                sp.wait_ge(stored, (t + 1) * 16)
                sp.sem_inc(xn_free, 1)

            pairs(sp, store)

        @block.gpsimd
        def _(pool):
            pool.sem_inc(kvn_done, 2)
            pool.wait_ge(w_ready, 1)

            def affine(t, i):
                pool.wait_ge(hat_done, t + 3)
                pool.wait_ge(kv_used, t + 1)
                pool.tensor_tensor(kvn[i][:, :], hat[i][:, :], gain[:, :], ALU.mult).then_inc(gained, 1)
                pool.wait_ge(gained, t + 1)
                pool.tensor_tensor(kvn[i][:, :], kvn[i][:, :], shift[:, :], ALU.add).then_inc(kvn_done, 1)

            pairs(pool, affine)

        @block.scalar
        def _(act):
            act.sem_inc(xT_done, 2)
            act.wait_ge(var_done, 1)
            act.activation(dev[:, :], mv[:, 1, :], ACT.Sqrt, bias=eps[:, 0:1], scale=1.0).then_inc(dev_done, 1)

            def take_xT(t, i):
                act.wait_ge(turned, t + 3)
                act.wait_ge(proj, t + 1)
                act.copy(xT[i][:, :, :], turn_ps[i][:, 0:2 * P].rearrange("p (k c) -> p k c", k=2)).then_inc(xT_done, 1)
                act.wait_ge(xT_done, t + 3)
                act.copy(xT_all[:, bass.ds(t, 1), :, :].rearrange("p a k c -> p (a k) c"), xT[i][:, :, :]).then_inc(copied, 1)

            def heads(t, i):
                act.wait_ge(proj, t + 3)
                act.activation(sq[:, :], proj_ps[i][:, :], ACT.Square).then_inc(squared, 1)
                act.wait_ge(summed, t + 1)
                act.activation(hdev[:, :], ss[:, :], ACT.Sqrt, bias=eps[:, 0:1], scale=1.0 / HD).then_inc(rooted, 1)

            def one(t, i):
                heads(t, i)
                if not isinstance(t, int) or t + 2 < NT:
                    take_xT(t + 2, i)

            take_xT(0, 0)
            take_xT(1, 1)
            tiles(act, one)

            def give_xT(t, i):
                act.wait_ge(mixed, t + 1)
                act.copy(xT[i][:, :, :], xT_all[:, bass.ds(t, 1), :, :].rearrange("p a k c -> p (a k) c")).then_inc(xT_back, 1)

            act.wait_ge(copied, NT)
            act.wait_ge(proj, NT + 2)
            pairs(act, give_xT)

        @block.tensor
        def _(pe):
            pe.sem_inc(turned, 2)
            pe.sem_inc(proj, 2)
            pe.sem_inc(kv_used, 2)
            pe.sem_inc(mixed, 2)
            pe.wait_ge(w_in, 16 * NW)
            for s in range(2):
                for j in range(2):
                    at = D + (2 * s + j) * HD
                    pe.matmul(proj_ps[s][:, j * D:(j + 1) * D], ones_row[:, :],
                              vecs[:, at:at + HD].unsqueeze(1).broadcast_to([1, H, HD]), start=True, stop=True)
            pe.matmul(turn_ps[0][:, 0:D], ones_row[:, :], vecs[:, 0:D], start=True, stop=True).then_inc(spread, 1)
            for k in range(2):
                for m in range(2):
                    pe.transpose(kv_ps[k][:, m * P:(m + 1) * P], w_nat[:, 3, m, k * P:(k + 1) * P], ident[:, :])
                for w in range(2):
                    for m in range(2):
                        last = pe.transpose(mix_ps[k][:, w * D + m * P:w * D + (m + 1) * P],
                                            w_nat[:, 1 + w, m, k * P:(k + 1) * P], ident[:, :])
            last.then_inc(w_turned, 1)
            pe.wait_ge(w_ready, 1)

            def turn(t, i):
                pe.wait_ge(xn_done, t + 1)
                pe.wait_ge(xT_done, t + 1)
                for k in range(2):
                    tr = pe.transpose(turn_ps[i][:, k * P:(k + 1) * P], xn[i][:, k * P:(k + 1) * P], ident[:, :])
                tr.then_inc(turned, 1)

            def project(t, i):
                pe.wait_ge(xT_done, t + 3)
                pe.wait_ge(hat_done, t + 1)
                for k in range(2):
                    mm = pe.matmul(proj_ps[i][:, :], xT[i][:, k, :], wkvT[:, k, :], start=(k == 0), stop=(k == 1))
                mm.then_inc(proj, 1)

            def kv_product(t, i, rows):
                pe.wait_ge(kvn_done, t + 3)
                first = isinstance(t, int) and t == 0
                final = isinstance(t, int) and t == LAST
                for c in range(2):
                    mm = pe.matmul(kv_ps[c][:, 0:P], kvn[i][0:rows, D + c * P:D + (c + 1) * P],
                                   kvn[i][0:rows, c * P:(c + 1) * P], start=first, stop=final, skip_group_check=True)
                mm.then_inc(kv_used, 1)

            def one(t, i):
                fixed = isinstance(t, int)
                if not fixed or t + 2 < NT:
                    turn(t + 2, i)
                if not fixed or t + 1 < NT:
                    project(t + 1, 1 - i)
                if not fixed or t > 0:
                    kv_product(t - 1, 1 - i, P)

            turn(0, 0)
            turn(1, 1)
            project(0, 0)
            one(0, 0)
            one(1, 1)
            with pe.Fori(0, (NT - 5) // 2) as h:
                one(2 * h + 2, 0)
                one(2 * h + 3, 1)
            one(NT - 3, 0)
            one(NT - 2, 1)
            one(NT - 1, 0)
            kv_product(LAST, 0, TAIL)

            pe.wait_ge(kvT_done, 1)
            for c in range(2):
                mm = pe.matmul(mix_ps[c][:, 0:D], kvT[:, c, :], woT[:, c, :], start=True, stop=True)
            mm.then_inc(R_made, 1)
            pe.wait_ge(R_done, 1)
            for m in range(2):
                for c in range(2):
                    mm = pe.matmul(proj_ps[m][:, 0:D], w_nat[:, 0, c, m * P:(m + 1) * P], R[:, c, :], start=(c == 0), stop=(c == 1))
            mm.then_inc(M_made, 1)
            pe.wait_ge(M_done, 1)

            def mix(t, i):
                pe.wait_ge(xT_back, t + 1)
                pe.wait_ge(added, t + 1)
                for k in range(2):
                    mm = pe.matmul(mix_ps[i][:, 0:D], xT[i][:, k, :], M[:, k, :], start=(k == 0), stop=(k == 1))
                mm.then_inc(mixed, 1)

            pairs(pe, mix)

        @block.vector
        def _(dve):
            n = [0]

            def then(ins):
                n[0] += 1
                ins.then_inc(step, 1)
                dve.wait_ge(step, n[0])

            dve.sem_inc(hat_done, 2)
            dve.sem_inc(added, 2)
            dve.memset(acc[:, LAST, :], 0.0).then_inc(cleared, 1)
            dve.memset(nv[:, LAST:NT], 0.0).then_inc(cleared, 1)
            then(dve.memset(kvT[:, :, :], 0.0))
            then(dve.memset(eps[:, :], EPS))
            dve.wait_ge(w_turned, 1)
            for k in range(2):
                heads = mix_ps[k][:, :].rearrange("p (h d) -> p h d", d=HD)
                then(dve.tensor_reduce(hsum[:, k, :], heads, AX.X, ALU.add))
                then(dve.tensor_scalar(hsum[:, k, :], hsum[:, k, :], 1.0 / HD, None, ALU.mult))
                then(dve.tensor_tensor(wkvT[:, k, :].rearrange("p (h d) -> p h d", d=HD), heads,
                                       hsum[:, k, :].unsqueeze(2).broadcast_to([P, HH, HD]), ALU.subtract))
                then(dve.tensor_copy(woT[:, k, :], kv_ps[k][:, 0:D]))
            dve.wait_ge(spread, 1)
            dve.tensor_copy(gain[:, :], proj_ps[0][:, :])
            then(dve.tensor_copy(shift[:, :], proj_ps[1][:, :]))
            then(dve.tensor_copy(bo_b[:, :], turn_ps[0][:, 0:D]))
            dve.wait_ge(x_in, 32)
            with dve.Fori(0, NT) as t:
                dve.bn_stats(stats[:, bass.ds(t, 1), :].rearrange("p a d -> p (a d)"),
                             acc[:, bass.ds(t, 1), :].rearrange("p a d -> p (a d)")).then_inc(aggr, 1)
            dve.wait_ge(aggr, NT)
            merge_stats(dve, then, stats, mv, D)
            dve.sem_inc(var_done, 1)
            dve.wait_ge(dev_done, 1)
            then(dve.reciprocal(rstd[:, :], dev[:, :]))
            dve.wait_ge(nv_in, 32)
            dve.sem_inc(w_ready, 1)

            def normalize(t, i):
                row = acc[:, bass.ds(t, 1), :].rearrange("p a d -> p (a d)")
                dve.wait_ge(xn_free, t + 1)
                dve.wait_ge(turned, t + 1)
                dve.tensor_scalar(xn[i][:, :], row, mv[:, 0, bass.ds(t, 1)], rstd[:, bass.ds(t, 1)],
                                  ALU.subtract, ALU.mult).then_inc(xn_done, 1)
                dve.scalar_tensor_tensor(out=row, in0=row, scalar=nv[:, bass.ds(t, 1)], in1=bo_b[:, :], op0=ALU.add, op1=ALU.add)

            def one(t, i):
                dve.wait_ge(squared, t + 1)
                dve.tensor_reduce(ss[:, :], sq[:, :].rearrange("p (h d) -> p h d", d=HD), AX.X, ALU.add).then_inc(summed, 1)
                if not isinstance(t, int) or t + 2 < NT:
                    normalize(t + 2, i)
                dve.wait_ge(rooted, t + 1)
                dve.reciprocal(hinv[:, :], hdev[:, :]).then_inc(inverted, 1)
                dve.wait_ge(inverted, t + 1)
                dve.wait_ge(kvn_done, t + 1)
                dve.tensor_tensor(hat[i][:, :].rearrange("p (h d) -> p h d", d=HD),
                                  proj_ps[i][:, :].rearrange("p (h d) -> p h d", d=HD),
                                  hinv[:, :].unsqueeze(2).broadcast_to([P, HH, HD]), ALU.mult).then_inc(hat_done, 1)

            normalize(0, 0)
            normalize(1, 1)
            tiles(dve, one)

            dve.wait_ge(kv_used, NT + 2)
            for c in range(2):
                for h in range(2):
                    part = slice(h * HD, (h + 1) * HD)
                    last = dve.tensor_scalar(kvT[part, c, part], kv_ps[c][part, part], 1.0 / N, None, ALU.mult)
            last.then_inc(kvT_done, 1)
            dve.wait_ge(R_made, 1)
            dve.tensor_copy(R[:, 0, :], mix_ps[0][:, 0:D])
            dve.tensor_copy(R[:, 1, :], mix_ps[1][:, 0:D]).then_inc(R_done, 1)
            dve.wait_ge(M_made, 1)
            dve.tensor_copy(M[:, 0, :], proj_ps[0][:, 0:D])
            dve.tensor_copy(M[:, 1, :], proj_ps[1][:, 0:D]).then_inc(M_done, 1)

            def add(t, i):
                row = acc[:, bass.ds(t, 1), :].rearrange("p a d -> p (a d)")
                dve.wait_ge(mixed, t + 3)
                dve.tensor_tensor(row, row, mix_ps[i][:, 0:D], ALU.add).then_inc(added, 1)

            pairs(dve, add)


def edge_sum(nc, shared, edges, xn_dram, G, NG, NT, D):
    banks, acc, ident, iota, iota1, ones_row, before = shared
    bucket, weight, packed, inside, w_left, n_left, rows_i = edges
    BUF = [0, 1, 0, 1, 0, 1, 2]
    LINKS = 14
    with ExitStack() as ctx:
        def sb(name, shape, dt=F32):
            return ctx.enter_context(nc.sbuf_tensor(name, shape, dt))

        def sem(name):
            return ctx.enter_context(nc.semaphore(name))

        tiles = sb("tiles", [P, NB, SW], F32R)
        keep = sb("keep", [P, NB, SW])
        ranks = sb("ranks", [P, NB, SW])
        rank1 = sb("rank1", [P, CH])
        far = sb("far", [P, CH])
        slot = sb("slot", [P, CH, P])
        vals = sb("vals", [P, 2, NB, CH])
        t_int = sb("t_int", [P, NB], I32)
        t_loc = sb("t_loc", [P, NB], I32)
        t_off = sb("t_off", [P, NB], I32)
        w_hi = sb("w_hi", [P, NB], F32R)
        table = [sb(f"table{i}", [P, 4, GRP, NB]) for i in range(2)]
        cur_s = sb("cur_s", [P, 3, GRP, BU])
        cur_d = sb("cur_d", [P, GRP, BU])
        hot_d = [sb(f"hot_d{i}", [P, GRP, P], F32R) for i in range(3)]
        hot_w = [sb(f"hot_w{i}", [P, 2, GRP, P], F32R) for i in range(3)]
        block_sb = [sb(f"block_sb{i}", [P, GRP, P]) for i in range(3)]
        window = [sb(f"window{i}", [P, GRP, D]) for i in range(2)]
        row_of = sb("row_of", [P, 1], I32)
        landing = sb("landing", [P, D])
        SRC, DST, WHI, WLO = range(4)

        def block_ps(i, j):
            return banks[2 * (i % 2) + j // 4][:, (j % 4) * P:(j % 4 + 1) * P]

        sum_ps = [banks[4 + i][:, 0:D] for i in range(2)]
        base_ps = banks[6][:, 0:NB]
        table_ps = banks[7][:, 0:2 * NB]

        keep_set = sem("keep_set"); tiles_done = sem("tiles_done"); base_done = sem("base_done")
        chain = sem("chain"); slot_done = sem("slot_done"); vals_done = sem("vals_done"); table_made = sem("table_made")
        row_done = sem("row_done"); gathered = sem("gathered"); window_in = sem("window_in"); pcur = sem("pcur"); passed = sem("passed")
        dcur = sem("dcur")
        d_done = sem("d_done"); w_done = sem("w_done"); a_done = sem("a_done"); a_copied = sem("a_copied")
        o_done = sem("o_done"); o_added = sem("o_added"); unit_read = sem("unit_read")
        block = ctx.enter_context(nc.Block())

        def schedule(eng, sort, unit):
            sort(0)
            with eng.Fori(1, GRP) as s:
                sort(s)
            with eng.Fori(0, NG // 2 - 1) as h:
                for par in range(2):
                    with eng.Fori(0, GRP) as k:
                        unit(2 * h + par, k, par, True)
            for g in (NG - 2, NG - 1):
                with eng.Fori(0, GRP) as k:
                    unit(g, k, g % 2, g < NG - 1)

        @block.gpsimd
        def _(pool):
            pool.sem_inc(d_done, 1)

            def values(s):
                if not isinstance(s, int):
                    pool.wait_ge(table_made, s)
                pool.wait_ge(tiles_done, s + 1)
                one_hot = tiles[:, :, 1:SW].bitcast(F32)
                for f, v in enumerate((packed, weight)):
                    ins = pool.tensor_tensor(vals[:, f, :, :], one_hot, v[:, bass.ds(s, 1), :].broadcast_to([P, NB, CH]), ALU.mult)
                ins.then_inc(vals_done, 1)

            def fetch(s, k, par):
                pool.tensor_copy(row_of[:, :], rows_i[:, bass.ds(s, 1)]).then_inc(row_done, 1)
                pool.wait_ge(row_done, s + 1)
                pool.sem_inc(passed, 1)
                pool.indirect_dma_start(out=landing[:, :], out_offset=None, in_=xn_dram,
                                        in_offset=bass.IndirectOffsetOnAxis(ap=row_of[:, 0:1], axis=0)).then_inc(gathered, 16)
                pool.wait_ge(gathered, (s + 1) * 16)
                pool.tensor_copy(window[par][:, bass.ds(k, 1), :].rearrange("p a d -> p (a d)"), landing[:, :]).then_inc(window_in, 1)

            def sort(s):
                values(s)
                fetch(s, s, 0)

            def unit(g, k, par, more):
                u = g * GRP + k
                pool.wait_ge(chain, (g + 1) * (GRP * LINKS))
                pool.wait_ge(d_done, u * BU + 1)
                pool.tensor_copy(cur_d[:, :, :], table[par][:, DST, :, bass.ds(k * BU, BU)]).then_inc(pcur, 1)
                pool.wait_ge(pcur, u + 1)
                for i in range(BU):
                    it = u * BU + i
                    pool.wait_ge(a_done, it + 1)
                    pool.sem_inc(passed, 1)
                    for j in range(GRP):
                        ins = pool.tensor_scalar(hot_d[BUF[i]][:, j, :], iota[:, :], cur_d[:, j, i:i + 1], None, ALU.is_equal)
                    ins.then_inc(d_done, 1)
                    if more and i == 2:
                        values(u + GRP)
                if more:
                    pool.wait_ge(o_done, g * (GRP * BU) + 2)
                    fetch(u + GRP, k, 1 - par)

            schedule(pool, sort, unit)

        @block.tensor
        def _(pe):
            pe.sem_inc(a_done, 2)
            pe.sem_inc(o_done, 2)

            def base(s):
                pe.wait_ge(tiles_done, s + 1)
                for c in range(CH):
                    mm = pe.matmul(base_ps, before[:, :], tiles[:, :, 1 + c], start=(c == 0), stop=(c == CH - 1))
                mm.then_inc(base_done, 1)

            def make_table(s):
                pe.wait_ge(vals_done, s + 1)
                pe.wait_ge(slot_done, s + 1)
                for c in range(CH):
                    mm = pe.matmul(table_ps, slot[:, c, :], vals[:, :, :, c], start=(c == 0), stop=(c == CH - 1))
                mm.then_inc(table_made, 1)

            def sort(s):
                base(s)
                make_table(s)

            def blocks(it, i):
                pe.wait_ge(d_done, it + 2)
                pe.wait_ge(w_done, it + 2)
                pe.wait_ge(a_copied, it + 1 if i == 0 else it)
                for j in range(GRP):
                    for part in range(2):
                        mm = pe.matmul(block_ps(i, j), hot_d[BUF[i]][:, j, :], hot_w[BUF[i]][:, part, j, :],
                                       start=(part == 0), stop=(part == 1))
                mm.then_inc(a_done, 1)

            def rows(it, i, par):
                pe.wait_ge(a_copied, it + 2)
                pe.wait_ge(o_added, it + 1 if i == 0 else it)
                for j in range(GRP):
                    mm = pe.matmul(sum_ps[i % 2], block_sb[BUF[i]][:, j, :], window[par][:, j, :], start=(j == 0), stop=(j == GRP - 1))
                mm.then_inc(o_done, 1)

            def unit(g, k, par, more):
                u = g * GRP + k
                pe.wait_ge(window_in, (g + 1) * GRP)
                blocks(u * BU, 0)
                for i in range(1, BU):
                    blocks(u * BU + i, i)
                    rows(u * BU + i - 1, i - 1, par)
                    if more and i == 2:
                        base(u + GRP)
                if more:
                    make_table(u + GRP)
                rows(u * BU + BU - 1, BU - 1, par)

            schedule(pe, sort, unit)

        @block.scalar
        def _(act):
            act.sem_inc(a_copied, 1)

            def unit(g, k):
                u = g * GRP + k
                for i in range(BU):
                    it = u * BU + i
                    act.wait_ge(a_done, it + 3)
                    act.wait_ge(o_done, it + 1)
                    for j, m in ((0, 4), (4, GRP - 4)):
                        ins = act.copy(block_sb[BUF[i]][:, j:j + m, :].rearrange("p m c -> p (m c)"),
                                       banks[2 * (i % 2) + j // 4][:, 0:m * P])
                    ins.then_inc(a_copied, 1)

            with act.Fori(0, NG) as g:
                with act.Fori(0, GRP) as k:
                    unit(g, k)

        @block.vector
        def _(dve):
            dve.sem_inc(o_added, 1)
            dve.sem_inc(w_done, 1)
            dve.memset(keep[:, :, :], 1.0).then_inc(keep_set, 1)
            dve.wait_ge(keep_set, 1)
            dve.memset(keep[:, :, 0:1], 0.0).then_inc(keep_set, 1)
            dve.wait_ge(keep_set, 2)
            links = [0]

            def link(s, ins):
                links[0] += 1
                ins.then_inc(chain, 1)
                dve.wait_ge(chain, s * LINKS + links[0])

            def hot_tiles(s):
                if not isinstance(s, int):
                    dve.wait_ge(vals_done, s)
                dve.tensor_tensor(tiles[:, :, 1:SW], iota[:, 0:NB].unsqueeze(2).broadcast_to([P, NB, CH]),
                                  bucket[:, bass.ds(s, 1), :].broadcast_to([P, NB, CH]), ALU.is_equal).then_inc(tiles_done, 1)

            def scan(s):
                links[0] = 0
                dve.wait_ge(tiles_done, s + 1)
                dve.wait_ge(base_done, s + 1)
                link(s, dve.tensor_copy(tiles[:, :, 0], base_ps))
                link(s, dve.tensor_tensor_scan(ranks[:, :, :].rearrange("p b c -> p (b c)"), keep[:, :, :].rearrange("p b c -> p (b c)"),
                                               tiles[:, :, :].bitcast(F32).rearrange("p b c -> p (b c)"), 0.0, ALU.mult, ALU.add))

            def rank(s):
                one_hot = tiles[:, :, 1:SW].bitcast(F32)
                link(s, dve.tensor_tensor(ranks[:, :, 1:SW], ranks[:, :, 1:SW], one_hot, ALU.mult))
                if not isinstance(s, int):
                    dve.wait_ge(slot_done, s)
                link(s, dve.tensor_reduce(rank1[:, :], ranks[:, :, 1:SW].rearrange("p b c -> p c b"), AX.X, ALU.add))
                link(s, dve.scalar_tensor_tensor(out=far[:, :], in0=rank1[:, :], scalar=P + 0.5,
                                                 in1=inside[:, bass.ds(s, 1), :].rearrange("p a c -> p (a c)"), op0=ALU.is_lt, op1=ALU.mult))
                link(s, dve.tensor_scalar(far[:, :], far[:, :], 0.5, None, ALU.is_lt))
                dve.tensor_tensor(w_left[:, bass.ds(s, 1), :].rearrange("p a c -> p (a c)"), far[:, :],
                                  weight[:, bass.ds(s, 1), :].rearrange("p a c -> p (a c)"), ALU.mult)
                dve.tensor_reduce(n_left[:, bass.ds(s, 1)], far[:, :], AX.X, ALU.add)

            def slots(s):
                if not isinstance(s, int):
                    dve.wait_ge(table_made, s)
                for c in range(CH):
                    ins = dve.tensor_scalar(slot[:, c, :], iota1[:, :], rank1[:, c:c + 1], None, ALU.is_equal)
                ins.then_inc(slot_done, 1)

            def unpack(s, k, par):
                place = lambda f: table[par][:, f, bass.ds(k, 1), :].rearrange("p a b -> p (a b)")
                dve.wait_ge(table_made, s + 1)
                link(s, dve.tensor_copy(t_int[:, :], table_ps[:, 0:NB]))
                link(s, dve.tensor_copy(w_hi[:, :], table_ps[:, NB:2 * NB]))
                link(s, dve.tensor_copy(place(WHI), w_hi[:, :].bitcast(F32)))
                link(s, dve.tensor_tensor(place(WLO), table_ps[:, NB:2 * NB], w_hi[:, :].bitcast(F32), ALU.subtract))
                link(s, dve.tensor_scalar(t_loc[:, :], t_int[:, :], P - 1, None, ALU.bitwise_and))
                link(s, dve.tensor_scalar(t_off[:, :], t_int[:, :], 7, None, ALU.arith_shift_right))
                link(s, dve.tensor_copy(place(SRC), t_loc[:, :]))
                link(s, dve.tensor_copy(place(DST), t_off[:, :]))
                assert links[0] == LINKS

            def sort(s):
                hot_tiles(s)
                scan(s)
                rank(s)
                slots(s)
                unpack(s, s, 0)

            def unit(g, k, par, more):
                u = g * GRP + k
                s = u + GRP
                dve.wait_ge(w_done, u * BU + 1)
                dve.tensor_copy(cur_s[:, 0, :, :], table[par][:, SRC, :, bass.ds(k * BU, BU)])
                dve.tensor_copy(cur_s[:, 1, :, :], table[par][:, WHI, :, bass.ds(k * BU, BU)])
                dve.tensor_copy(cur_s[:, 2, :, :], table[par][:, WLO, :, bass.ds(k * BU, BU)]).then_inc(dcur, 1)
                dve.wait_ge(dcur, u + 1)

                def hot(i):
                    dve.wait_ge(a_done, u * BU + i + 1)
                    for j in range(GRP):
                        for part in range(2):
                            ins = dve.tensor_scalar(hot_w[BUF[i]][:, part, j, :], iota[:, :], cur_s[:, 0, j, i:i + 1],
                                                    cur_s[:, 1 + part, j, i:i + 1], ALU.is_equal, ALU.mult)
                    ins.then_inc(w_done, 1)

                def add(i):
                    row = acc[:, bass.ds(k * BU + i, 1), :].rearrange("p a d -> p (a d)")
                    dve.wait_ge(o_done, u * BU + i + 3)
                    dve.tensor_tensor(row, row, sum_ps[i % 2], ALU.add).then_inc(o_added, 1)

                hot(0)
                hot(1)
                if more:
                    hot_tiles(s)
                hot(2)
                add(0)
                hot(3)
                add(1)
                if more:
                    scan(s)
                hot(4)
                add(2)
                if more:
                    rank(s)
                hot(5)
                add(3)
                if more:
                    slots(s)
                hot(6)
                add(4)
                add(5)
                if more:
                    dve.wait_ge(pcur, u + 1)
                    unpack(s, k, 1 - par)
                add(6)

            schedule(dve, sort, unit)


def stragglers(nc, shared, edges, src, dst, xn_dram, E, G, TP, TR, NT, D):
    banks, acc, ident, iota, iota1, ones_row, before = shared
    bucket, weight, packed, inside, w_left, n_left, rows_i = edges
    SC = CH * P
    with ExitStack() as ctx:
        def sb(name, shape, dt=F32):
            return ctx.enter_context(nc.sbuf_tensor(name, shape, dt))

        def sem(name):
            return ctx.enter_context(nc.semaphore(name))

        ones_col = sb("ones_col", [P, 1])
        left = sb("left", [P, 1])
        total = sb("total", [1, 1], I32)
        src_l = sb("src_l", [P, G * CH], I32)
        dst_l = sb("dst_l", [P, G * CH], I32)
        w_flat = w_left[:, :, :].rearrange("p g c -> p (g c)")
        idx = sb("idx", [P, 1], I32)
        rows = sb("rows", [P, D])
        rel = sb("rel", [P, 1])
        w_one = sb("w_one", [P, 1])
        hot = sb("hot", [P, P])
        left_done = sem("left_done"); total_ps = sem("total_ps"); total_done = sem("total_done")
        padded = sem("padded"); loaded = sem("loaded"); idx_done = sem("idx_done"); rows_in = sem("rows_in")
        rel_done = sem("rel_done"); hot_done = sem("hot_done"); made = sem("made"); added = sem("added")
        passed = sem("passed")
        block = ctx.enter_context(nc.Block())
        Q = G * CH

        def some_left(eng):
            eng.wait_ge(total_done, 1)
            return eng.If(eng.value_load(total[0:1, 0:1], min_val=0, max_val=Q * P) > 0)

        @block.sync
        def _(sp):
            with some_left(sp):
                sp.wait_ge(padded, 2)
                for arr, to in ((dst, dst_l), (src, src_l)):
                    at = to[:, :].rearrange("p (g c) -> p g c", c=CH)
                    body = arr[0:(G - 1) * SC].rearrange("(g p c) -> p g c", p=P, c=CH)
                    sp.dma_start(at[:, 0:G - 1, :], body).then_inc(loaded, 16)
                    tail = arr[(G - 1) * SC:(G - 1) * SC + TP * CH].rearrange("(p c) -> p c", c=CH)
                    sp.dma_start(at[0:TP, G - 1, :], tail).then_inc(loaded, 16)
                    rest = arr[E - TR:E].rearrange("(a c) -> a c", a=1)
                    sp.dma_start(at[TP:TP + 1, G - 1, 0:TR], rest).then_inc(loaded, 16)

        @block.gpsimd
        def _(pool):
            with some_left(pool):
                pool.wait_ge(loaded, 6 * 16)
                with pool.Fori(0, Q) as q:
                    pool.tensor_copy(idx[:, :], dst_l[:, bass.ds(q, 1)]).then_inc(idx_done, 1)
                    pool.wait_ge(idx_done, q + 1)
                    pool.wait_ge(made, q * NT + 1)
                    pool.sem_inc(passed, 1)
                    pool.indirect_dma_start(out=rows[:, :], out_offset=None, in_=xn_dram,
                                            in_offset=bass.IndirectOffsetOnAxis(ap=idx[:, 0:1], axis=0)).then_inc(rows_in, 16)
                    pool.wait_ge(rows_in, (q + 1) * 16)

        @block.tensor
        def _(pe):
            pe.sem_inc(made, 1)
            pe.wait_ge(left_done, 2)
            pe.matmul(banks[0][0:1, 0:1], left[:, :], ones_col[:, :], start=True, stop=True).then_inc(total_ps, 1)
            with some_left(pe):
                with pe.Fori(0, Q) as q:
                    pe.wait_ge(rows_in, (q + 1) * 16)
                    pe.sem_inc(passed, 1)
                    with pe.Fori(0, NT) as b:
                        pe.wait_ge(hot_done, q * NT + b + 1)
                        pe.wait_ge(added, q * NT + b + 1)
                        pe.matmul(banks[1][:, 0:D], hot[:, :], rows[:, :], start=True, stop=True).then_inc(made, 1)

        @block.vector
        def _(dve):
            dve.sem_inc(added, 1)
            dve.memset(ones_col[:, :], 1.0).then_inc(left_done, 1)
            dve.tensor_reduce(left[:, :], n_left[:, :], AX.X, ALU.add).then_inc(left_done, 1)
            dve.wait_ge(total_ps, 1)
            dve.tensor_copy(total[:, :], banks[0][0:1, 0:1]).then_inc(total_done, 1)
            with some_left(dve):
                dve.memset(src_l[:, (G - 1) * CH:Q], NB * P).then_inc(padded, 1)
                dve.memset(dst_l[:, (G - 1) * CH:Q], 0).then_inc(padded, 1)
                dve.wait_ge(loaded, 6 * 16)
                with dve.Fori(0, Q) as q:
                    dve.wait_ge(added, q * NT + 1)
                    dve.tensor_copy(rel[:, :], src_l[:, bass.ds(q, 1)]).then_inc(rel_done, 1)
                    dve.tensor_copy(w_one[:, :], w_flat[:, bass.ds(q, 1)]).then_inc(rel_done, 1)
                    with dve.Fori(0, NT) as b:
                        dve.wait_ge(rel_done, q * (NT + 2) + b + 2)
                        dve.wait_ge(made, q * NT + b + 1)
                        dve.tensor_scalar(hot[:, :], iota[:, :], rel[:, 0:1], w_one[:, 0:1], ALU.is_equal, ALU.mult).then_inc(hot_done, 1)
                        dve.wait_ge(hot_done, q * NT + b + 1)
                        dve.tensor_scalar(rel[:, :], rel[:, :], float(-P), None, ALU.add).then_inc(rel_done, 1)
                        dve.wait_ge(made, q * NT + b + 2)
                        row = acc[:, bass.ds(b, 1), :].rearrange("p a d -> p (a d)")
                        dve.tensor_tensor(row, row, banks[1][:, 0:D], ALU.add).then_inc(added, 1)


def put_rows(nc, shared, rows_dram, NT):
    acc = shared[1]
    with ExitStack() as ctx:
        rows_out = ctx.enter_context(nc.semaphore("rows_out"))
        block = ctx.enter_context(nc.Block())

        @block.sync
        def _(sp):
            sp.dma_start(rows_dram.rearrange("(t p) d -> p t d", p=P), acc[:, :, :]).then_inc(rows_out, 16)
            sp.wait_ge(rows_out, 16)


def experts(nc, banks, rows_dram, ident, iota, ones_row, Wg, bg, bias, W1, b1, W2, b2, out, NT, TAIL, N, D):
    X, F = W1.shape[0], W1.shape[2]
    FC = F // P
    QG = NT // 2
    TOK = 2 * P
    with ExitStack() as ctx:
        def sb(name, shape, dt=F32):
            return ctx.enter_context(nc.sbuf_tensor(name, shape, dt))

        def sem(name):
            return ctx.enter_context(nc.semaphore(name))

        w1 = [sb(f"w1_{i}", [P, X, 2, F], F32R) for i in range(2)]
        w2 = [sb(f"w2_{i}", [P, X, FC, D], F32R) for i in range(2)]
        wg_f = sb("wg_f", [P, 2, X])
        wg = [sb(f"wg_{i}", [P, 2, X], F32R) for i in range(2)]
        b1_s = sb("b1_s", [P, X, FC])
        b2_s = sb("b2_s", [X, D])
        gb_row = sb("gb_row", [1, 2 * X])
        gb = sb("gb", [P, X])
        eps = sb("eps2", [P, 1])
        r_in = sb("r_in", [P, 2, D])
        res = sb("res", [P, 2, D])
        z = sb("z", [P, 2, D])
        zT = [sb(f"zT{i}", [P, 2, TOK], F32R) for i in range(2)]
        stats = sb("stats2", [P, 2, 6])
        mv = sb("mv2", [P, 2, 2])
        dev = sb("dev2", [P, 2])
        rstd = sb("rstd2", [P, 2])
        logits = sb("logits", [P, 2, X])
        best = sb("best", [P, 2, 8])
        where = sb("where", [P, 2, 8], mybir.dt.uint32)
        where_f = sb("where_f", [P, 2, 2])
        gap = sb("gap", [P, 2])
        ex = sb("ex", [P, 2])
        den = sb("den", [P, 2])
        share = sb("share", [P, 2, 2])
        gate_a = sb("gate_a", [P, 2, X])
        gate = sb("gate", [P, 2, X])
        gateT = sb("gateT", [X, 2, P])
        hf = [sb(f"hf{i}", [P, FC, TOK]) for i in range(2)]
        hh = [sb(f"hh{i}", [P, FC, TOK], F32R) for i in range(2)]
        hl = [sb(f"hl{i}", [P, FC, TOK], F32R) for i in range(2)]

        def hid_ps(e, c):
            return banks[2 * (e % 2) + c // 2][:, (c % 2) * TOK:(c % 2 + 1) * TOK]

        y_ps = banks[4:6]
        turn_ps, small_ps = banks[6], banks[7]

        w_in = [sem(f"w_in{i}") for i in range(2)]
        small_in = sem("small_in"); row_in = sem("row_in"); out_done = sem("out_done")
        w_split = sem("w_split"); gb_ps = sem("gb_ps"); w_ready = sem("w_ready")
        var_done = sem("var_done"); dev_done = sem("dev_done"); z_done = sem("z_done"); z_turned = sem("z_turned")
        zh_done = sem("zh_done"); zl_done = sem("zl_done"); logit_ps = sem("logit_ps")
        gap_done = sem("gap_done"); ex_done = sem("ex_done"); gate_done = sem("gate_done")
        gateT_ps = sem("gateT_ps"); gateT_done = sem("gateT_done"); shift_ps = sem("shift_ps"); res_set = sem("res_set")
        hid = sem("hid"); relu_done = sem("relu_done"); split_done = sem("split_done")
        y_made = sem("y_made"); y_added = sem("y_added"); chain = sem("chain"); hi_done = sem("hi_done"); half_done = sem("half_done"); res_free = sem("res_free"); passed = sem("passed")
        block = ctx.enter_context(nc.Block())
        LINKS = 10

        def groups(eng, group):
            with eng.Fori(0, QG - 1) as q:
                group(q, 2, 2)
            group(QG - 1, 2, 1)
            group(QG, 1, 0)

        @block.sync
        def _(sp):
            for n in range(2 * X):
                if n >= 2:
                    sp.wait_ge(w_split, n - 1)
                e = n % X
                if n < X:
                    sp.dma_start(hf[n % 2][:, :, :].rearrange("p c t -> p (c t)").rearrange("p (k h) -> p k h", k=2),
                                 W1[e].rearrange("(k p) h -> p k h", p=P)).then_inc(w_in[n % 2], 16)
                else:
                    sp.dma_start(hf[n % 2][:, :, :], W2[e].rearrange("(c p) d -> p c d", p=P)).then_inc(w_in[n % 2], 16)

            def load(q, n):
                sp.dma_start(r_in[:, 0:n, :], rows_dram[bass.ds(q * TOK, n * P), :].rearrange("(t p) d -> p t d", p=P)).then_inc(row_in, 16)

            def group(q, n, nxt):
                if nxt:
                    sp.wait_ge(res_set, q + 1)
                    load(q + 1, nxt)
                sp.wait_ge(y_added, q * X + X + 2)
                if n == 2:
                    sp.dma_start(out[bass.ds(q * TOK, TOK), :].rearrange("(t p) d -> p t d", p=P), res[:, :, :]).then_inc(out_done, 16)
                else:
                    sp.dma_start(out[N - TAIL:N, :], res[0:TAIL, 0, :]).then_inc(out_done, 16)
                sp.wait_ge(out_done, (q + 1) * 16)
                sp.sem_inc(res_free, 1)

            sp.sem_inc(res_free, 1)
            groups(sp, group)

        @block.scalar
        def _(act):
            act.sem_inc(relu_done, 2)
            act.dma_start(wg_f[:, :, :], Wg.rearrange("(k p) e -> p k e", p=P)).then_inc(small_in, 16)
            with nc.allow_non_contiguous_dma(reason="bias of each hidden unit on its partition"):
                act.dma_start(b1_s[:, :, :], b1.rearrange("e (c p) -> p e c", p=P)).then_inc(small_in, 16)
            act.dma_start(b2_s[:, :], b2).then_inc(small_in, 16)
            act.dma_start(gb_row[:, 0:X], bg.rearrange("(a e) -> a e", a=1)).then_inc(small_in, 16)
            act.dma_start(gb_row[:, X:2 * X], bias.rearrange("(a e) -> a e", a=1)).then_inc(small_in, 16)
            act.dma_start(r_in[:, :, :], rows_dram[0:TOK, :].rearrange("(t p) d -> p t d", p=P)).then_inc(row_in, 16)
            for n in range(2 * X):
                act.wait_ge(w_in[n % 2], 16 * (n // 2 + 1))
                if n < X:
                    to = w1[0][:, n % X, :, :].rearrange("p k h -> p (k h)")
                else:
                    to = w2[0][:, n % X, :, :].rearrange("p c d -> p (c d)")
                act.copy(to, hf[n % 2][:, :, :].rearrange("p c t -> p (c t)")).then_inc(hi_done, 1)

            def deviation(q, n):
                act.wait_ge(var_done, q + 1)
                act.activation(dev[:, 0:n], mv[:, 0:n, 1], ACT.Sqrt, bias=eps[:, 0:1], scale=1.0).then_inc(dev_done, 1)

            def high_z(q, n):
                act.wait_ge(z_turned, q + 1)
                src = turn_ps[:, :].rearrange("p (k t) -> p k t", k=2)[:, :, 0:n * P]
                act.copy(zT[0][:, :, 0:n * P], src).then_inc(zh_done, 1)

            def exponent(q, n):
                act.wait_ge(gap_done, q + 1)
                act.activation(ex[:, 0:n], gap[:, 0:n], ACT.Exp).then_inc(ex_done, 1)

            def relu(q, e, n):
                act.wait_ge(hid, q * X + e + 1)
                act.wait_ge(split_done, q * X + e + 1)
                for c in range(FC):
                    ins = act.activation(hf[e % 2][:, c, 0:n * P], hid_ps(e, c)[:, 0:n * P], ACT.Relu, bias=b1_s[:, e, c:c + 1])
                ins.then_inc(relu_done, 1)

            def group(q, n, nxt):
                for e in range(X):
                    if e == 4 and nxt:
                        deviation(q + 1, nxt)
                    if e == X - 1 and nxt:
                        act.wait_ge(hid, q * X + X)
                        high_z(q + 1, nxt)
                    relu(q, e, n)
                if nxt:
                    exponent(q + 1, nxt)

            deviation(0, 2)
            high_z(0, 2)
            exponent(0, 2)
            groups(act, group)

        @block.tensor
        def _(pe):
            pe.sem_inc(y_made, 2)
            pe.wait_ge(small_in, 16 * 5)
            pe.matmul(small_ps[:, 0:2 * X], ones_row[:, :], gb_row[:, :], start=True, stop=True).then_inc(gb_ps, 1)

            THREE = ((0, 0), (0, 1), (1, 0))

            def turn(q, n):
                pe.wait_ge(z_done, q + 1)
                for t in range(n):
                    for k in range(2):
                        tr = pe.transpose(turn_ps[:, k * TOK + t * P:k * TOK + (t + 1) * P], z[:, t, k * P:(k + 1) * P], ident[:, :])
                tr.then_inc(z_turned, 1)

            def logit(q, n):
                pe.wait_ge(zh_done, q + 1)
                pe.wait_ge(zl_done, q + 1)
                for t in range(n):
                    m = 0
                    for k in range(2):
                        for a, b in THREE:
                            mm = pe.matmul(small_ps[:, t * X:(t + 1) * X], zT[a][:, k, t * P:(t + 1) * P], wg[b][:, k, :], start=(m == 0), stop=(m == 5))
                            m += 1
                mm.then_inc(logit_ps, 1)

            def turn_gate(q, n):
                pe.wait_ge(gate_done, q + 1)
                for t in range(n):
                    tr = pe.transpose(small_ps[0:X, t * P:(t + 1) * P], gate[:, t, :], ident[:, :])
                tr.then_inc(gateT_ps, 1)

            def shifts(q, n):
                pe.wait_ge(gateT_done, q + 1)
                for t in range(n):
                    mm = pe.matmul(small_ps[:, t * D:(t + 1) * D], gateT[:, t, :], b2_s[:, :], start=True, stop=True)
                mm.then_inc(shift_ps, 1)

            def hidden(q, e, n):
                pe.wait_ge(relu_done, q * X + e + 1)
                for c in range(FC):
                    m = 0
                    for k in range(2):
                        for a, b in THREE:
                            mm = pe.matmul(hid_ps(e, c)[:, 0:n * P], w1[a][:, e, k, c * P:(c + 1) * P], zT[b][:, k, 0:n * P],
                                           start=(m == 0), stop=(m == 5))
                            m += 1
                mm.then_inc(hid, 1)

            def second(q, e, n):
                pe.wait_ge(split_done, q * X + e + 3)
                pe.wait_ge(y_added, q * X + e + 1)
                parts = (hh, hl)
                for t in range(n):
                    m = 0
                    for c in range(FC):
                        for a, b in THREE:
                            mm = pe.matmul(y_ps[e % 2][:, t * D:(t + 1) * D], parts[a][e % 2][:, c, t * P:(t + 1) * P], w2[b][:, e, c, :],
                                           start=(m == 0), stop=(m == 3 * FC - 1))
                            m += 1
                mm.then_inc(y_made, 1)

            def group(q, n, nxt):
                hidden(q, 0, n)
                turn_gate(q, n)
                hidden(q, 1, n)
                shifts(q, n)
                second(q, 0, n)
                for e in range(2, X):
                    hidden(q, e, n)
                    second(q, e - 1, n)
                    if e == 5 and nxt:
                        turn(q + 1, nxt)
                if nxt:
                    logit(q + 1, nxt)
                second(q, X - 1, n)

            turn(0, 2)
            pe.wait_ge(w_ready, 1)
            logit(0, 2)
            groups(pe, group)

        @block.vector
        def _(dve):
            dve.memset(eps[:, :], EPS)
            dve.sem_inc(y_added, 2)
            dve.sem_inc(split_done, 2)
            links = [0]

            def link(q, ins):
                links[0] += 1
                ins.then_inc(chain, 1)
                dve.wait_ge(chain, q * LINKS + links[0])

            def statistics(q, n):
                links[0] = 0
                dve.wait_ge(row_in, (q + 1) * 16)
                for t in range(n):
                    ins = dve.bn_stats(stats[:, t, :], r_in[:, t, :])
                link(q, ins)
                dve.sem_inc(passed, 1)
                for t in range(n):
                    ins = dve.bn_aggr(mv[:, t, :], stats[:, t, :])
                ins.then_inc(var_done, 1)

            def normalize(q, n):
                dve.wait_ge(dev_done, q + 1)
                link(q, dve.reciprocal(rstd[:, 0:n], dev[:, 0:n]))
                for t in range(n):
                    ins = dve.tensor_scalar(z[:, t, :], r_in[:, t, :], mv[:, t, 0:1], rstd[:, t:t + 1], ALU.subtract, ALU.mult)
                ins.then_inc(z_done, 1)

            def low_z(q, n):
                dve.wait_ge(zh_done, q + 1)
                src = turn_ps[:, :].rearrange("p (k t) -> p k t", k=2)[:, :, 0:n * P]
                dve.tensor_tensor(zT[1][:, :, 0:n * P], src, zT[0][:, :, 0:n * P].bitcast(F32), ALU.subtract).then_inc(zl_done, 1)

            def gates(q, n):
                dve.wait_ge(logit_ps, q + 1)
                for t in range(n):
                    ins = dve.tensor_tensor(logits[:, t, :], small_ps[:, t * X:(t + 1) * X], gb[:, :], ALU.add)
                link(q, ins)
                dve.sem_inc(passed, 1)
                for t in range(n):
                    ins = dve.max(best[:, t, :], logits[:, t, :])
                link(q, ins)
                dve.sem_inc(passed, 1)
                for t in range(n):
                    dve.max_index(where[:, t, :], best[:, t, :], logits[:, t, :])
                dve.tensor_tensor(gap[:, 0:n], best[:, 0:n, 1], best[:, 0:n, 0], ALU.subtract).then_inc(gap_done, 1)
                dve.wait_ge(ex_done, q + 1)
                link(q, dve.tensor_copy(where_f[:, 0:n, :], where[:, 0:n, 0:2]))
                link(q, dve.tensor_scalar(den[:, 0:n], ex[:, 0:n], 1.0, None, ALU.add))
                link(q, dve.reciprocal(share[:, 0:n, 0], den[:, 0:n]))
                link(q, dve.tensor_tensor(share[:, 0:n, 1], ex[:, 0:n], share[:, 0:n, 0], ALU.mult))
                for s, to in enumerate((gate_a, gate)):
                    for t in range(n):
                        ins = dve.tensor_scalar(to[:, t, :], iota[:, 0:X], where_f[:, t, s:s + 1], share[:, t, s:s + 1], ALU.is_equal, ALU.mult)
                link(q, ins)
                link(q, dve.tensor_tensor(gate[:, 0:n, :], gate[:, 0:n, :], gate_a[:, 0:n, :], ALU.add))
                assert links[0] == LINKS, links[0]
                dve.sem_inc(gate_done, 1)

            def take_gateT(q, n):
                dve.wait_ge(gateT_ps, q + 1)
                dve.tensor_copy(gateT[:, 0:n, :], small_ps[0:X, 0:n * P].rearrange("p (t c) -> p t c", t=n)).then_inc(gateT_done, 1)

            def set_res(q, n):
                dve.wait_ge(shift_ps, q + 1)
                dve.wait_ge(res_free, q + 1)
                dve.tensor_tensor(res[:, 0:n, :], r_in[:, 0:n, :], small_ps[:, 0:n * D].rearrange("p (t d) -> p t d", t=n), ALU.add).then_inc(res_set, 1)

            def split(q, e, n):
                dve.wait_ge(relu_done, q * X + e + 3)
                dve.wait_ge(y_made, q * X + e + 1)
                dve.tensor_copy(hh[e % 2][:, :, 0:n * P], hf[e % 2][:, :, 0:n * P]).then_inc(half_done, 1)
                dve.wait_ge(half_done, q * X + e + 1)
                dve.tensor_tensor(hl[e % 2][:, :, 0:n * P], hf[e % 2][:, :, 0:n * P], hh[e % 2][:, :, 0:n * P].bitcast(F32), ALU.subtract).then_inc(split_done, 1)

            def add(q, e, n):
                dve.wait_ge(y_added, q * X + e + 2) if e else dve.wait_ge(res_set, q + 1)
                dve.wait_ge(y_made, q * X + e + 3)
                for t in range(n):
                    ins = dve.scalar_tensor_tensor(out=res[:, t, :], in0=y_ps[e % 2][:, t * D:(t + 1) * D], scalar=gate[:, t, e:e + 1],
                                                   in1=res[:, t, :], op0=ALU.mult, op1=ALU.add)
                ins.then_inc(y_added, 1)

            def group(q, n, nxt):
                take_gateT(q, n)
                split(q, 0, n)
                split(q, 1, n)
                set_res(q, n)
                add(q, 0, n)
                for e in range(2, X):
                    split(q, e, n)
                    add(q, e - 1, n)
                    if e == 3 and nxt:
                        statistics(q + 1, nxt)
                    if e == 4 and nxt:
                        normalize(q + 1, nxt)
                if nxt:
                    low_z(q + 1, nxt)
                add(q, X - 1, n)
                if nxt:
                    gates(q + 1, nxt)

            statistics(0, 2)
            for n in range(2 * X):
                dve.wait_ge(hi_done, n + 1)
                if n < X:
                    hi, lo = (w1[i][:, n % X, :, :].rearrange("p k h -> p (k h)") for i in range(2))
                else:
                    hi, lo = (w2[i][:, n % X, :, :].rearrange("p c d -> p (c d)") for i in range(2))
                dve.tensor_tensor(lo, hf[n % 2][:, :, :].rearrange("p c t -> p (c t)"), hi.bitcast(F32), ALU.subtract).then_inc(w_split, 1)
            dve.wait_ge(small_in, 16 * 5)
            dve.tensor_copy(wg[0][:, :, :], wg_f[:, :, :]).then_inc(w_split, 1)
            dve.wait_ge(w_split, 2 * X + 1)
            dve.tensor_tensor(wg[1][:, :, :], wg_f[:, :, :], wg[0][:, :, :].bitcast(F32), ALU.subtract)
            dve.wait_ge(gb_ps, 1)
            dve.tensor_copy(gb[:, :], small_ps[:, 0:X]).then_inc(w_split, 1)
            dve.wait_ge(w_split, 2 * X + 2)
            dve.tensor_tensor(gb[:, :], gb[:, :], small_ps[:, X:2 * X], ALU.add).then_inc(w_ready, 1)
            normalize(0, 2)
            low_z(0, 2)
            gates(0, 2)
            groups(dve, group)


_INS = ['x', 'src', 'dst', 'edge_weight', 'node_vec1', 'L0_mix_wq', 'L0_mix_wk', 'L0_mix_wv', 'L0_mix_wo', 'L0_mix_bo',
        'L0_mix_ln_k_g', 'L0_mix_ln_k_b', 'L0_mix_ln_v_g', 'L0_mix_ln_v_b', 'L0_ffn_Wg', 'L0_ffn_bg', 'L0_ffn_bias',
        'L0_ffn_W1', 'L0_ffn_b1', 'L0_ffn_W2', 'L0_ffn_b2']
_OUTS = [((6250, 256), 'float32')]


def kernel(**inputs):
    import numpy as _np
    import concourse.bacc as _bacc
    from concourse import mybir as _mybir
    from concourse.bass_utils import run_bass_kernel_spmd as _run

    nc = _bacc.Bacc("TRN2", target_bir_lowering=False, num_devices=1)
    arrays, args = {}, []
    for name in _INS:
        a = _np.ascontiguousarray(inputs[name])
        arrays[f"in_{name}_dram"] = a
        args.append(nc.dram_tensor(f"in_{name}_dram", a.shape, _mybir.dt.from_np(a.dtype), kind="ExternalInput").ap())
    for i, (shape, dtype) in enumerate(_OUTS):
        dt = _mybir.dt.from_np(_np.dtype(dtype))
        args.append(nc.dram_tensor(f"out_{i}_dram", shape, dt, kind="ExternalOutput").ap())
    gps_layer(nc, *args)
    r = _run(nc, [arrays], core_ids=[0])
    got = tuple(r.results[0][f"out_{i}_dram"] for i in range(len(_OUTS)))
    return got[0]
```

```python
from contextlib import ExitStack

import numpy as np

import concourse.bass as bass
from concourse import mybir

P = 128
F32 = mybir.dt.float32
F32R = mybir.dt.float32r
I32 = mybir.dt.int32
BF16 = mybir.dt.bfloat16
ALU = mybir.AluOpType
ACT = mybir.ActivationFunctionType
AX = mybir.AxisListType
EPS = 1e-5

CH = 28
SW = CH + 2
GRP = 8
BU = 6
NB = 50
FIELDS = 5
SRC, DST, W = 0, 1, 2


def gps_layer(nc, x, src, dst, edge_weight, node_vec1, wq, wk, wv, wo, bo, kg, kb, vg, vb,
         Wg, bg, bias, W1, b1, W2, b2, out):
    N, D = x.shape
    E = src.shape[0]
    SC = CH * P
    G = -(-E // SC)
    NT = -(-N // P)
    TAIL = N - (NT - 1) * P
    NG = G // GRP
    assert D == 2 * P and G == NG * GRP and NT == GRP * BU + 1 and NG % 2 == 1 and NB == NT + 1
    HD = kg.shape[0]
    H = D // HD
    FULL = E - (G - 1) * SC
    TP = FULL // CH
    TR = FULL - TP * CH

    xn_dram = nc.dram_tensor("xn_dram", (NT * P, D), F32, kind="Internal").ap()

    rows_dram = nc.dram_tensor("rows_dram", (NT * P, D), F32, kind="Internal").ap()

    with ExitStack() as ctx:
        def sb(name, shape, dt=F32, c=ctx):
            return c.enter_context(nc.sbuf_tensor(name, shape, dt))

        ident = sb("ident", [P, P])
        iota = sb("iota", [P, P])
        iota1_c = sb("iota1_c", [P, P, CH], BF16)
        iota_j = sb("iota_j", [P, P, GRP], BF16)
        ones_row = sb("ones_row", [1, P])
        before = sb("before", [P, P], BF16)
        banks = [ctx.enter_context(nc.psum_tensor(f"bank{i}", [P, 512], F32)) for i in range(8)]
        with ExitStack() as c1:
            acc = sb("acc", [P, NT, D], F32, c1)
            shared = (banks, acc, ident, iota, iota1_c, iota_j, ones_row, before)
            constants(nc, shared)
            with ExitStack() as c2:
                edges = edge_lists(nc, c2, shared, src, dst, edge_weight, E, G, TP, TR, N)
                attention(nc, shared, x, node_vec1, wq, wk, wv, wo, bo, kg, kb, vg, vb, xn_dram, NT, TAIL, N, D, H, HD)
                edge_sum(nc, shared, edges, xn_dram, G, NG, NT, D)
                stragglers(nc, shared, edges, src, dst, edge_weight, xn_dram, E, G, TP, TR, NT, D)
            put_rows(nc, shared, rows_dram, NT)
        experts(nc, banks, rows_dram, ident, iota, ones_row, Wg, bg, bias, W1, b1, W2, b2, out, NT, TAIL, N, D)


def constants(nc, shared):
    banks, acc, ident, iota, iota1_c, iota_j, ones_row, before = shared
    with ExitStack() as ctx:
        ints = ctx.enter_context(nc.sbuf_tensor("ints", [P, 2, P], I32))
        iota_done = ctx.enter_context(nc.semaphore("iota_done"))
        cast_done = ctx.enter_context(nc.semaphore("cast_done"))
        block = ctx.enter_context(nc.Block())

        @block.gpsimd
        def _(pool):
            pool.iota(ints[:, 0, :], [[1, P]], base=0, channel_multiplier=0).then_inc(iota_done, 1)
            pool.iota(ints[:, 1, :], [[1, P]], base=0, channel_multiplier=-1).then_inc(iota_done, 1)

        @block.vector
        def _(dve):
            dve.memset(ones_row[:, :], 1.0)
            dve.wait_ge(iota_done, 2)
            dve.tensor_copy(iota[:, :], ints[:, 0, :]).then_inc(cast_done, 1)
            dve.tensor_scalar(ident[:, :], ints[:, 1, :], 0.0, None, ALU.is_equal)
            dve.tensor_scalar(before[:, :], ints[:, 1, :], 0.0, None, ALU.is_gt)
            dve.wait_ge(cast_done, 1)
            dve.tensor_copy(iota_j[:, :, :], iota[:, :].unsqueeze(2).broadcast_to([P, P, GRP]))
            dve.tensor_scalar(iota1_c[:, :, :], iota[:, :].unsqueeze(2).broadcast_to([P, P, CH]), 1.0, None, ALU.add)


def edge_lists(nc, keep, shared, src, dst, edge_weight, E, G, TP, TR, N):
    banks, acc, ident, iota, iota1_c, iota_j, ones_row, before = shared
    SC = CH * P

    def kb(name, shape, dt=F32):
        return keep.enter_context(nc.sbuf_tensor(name, shape, dt))

    tile1 = kb("tile1", [P, G + 1, CH], BF16)
    fields = kb("fields", [P, FIELDS, G + 1, CH], BF16)
    inside = kb("inside", [P, G, CH], BF16)
    left = kb("left", [P, G, CH], BF16)
    n_left = kb("n_left", [P, G])
    rows_i = kb("rows_i", [P, G], I32)
    with ExitStack() as ctx:
        def sb(name, shape, dt=F32):
            return ctx.enter_context(nc.sbuf_tensor(name, shape, dt))

        dst_i = sb("dst_i", [P, G, CH], I32)
        weight = sb("weight", [P, G, CH])
        bucket = sb("bucket", [P, G, CH])
        src_i = sb("src_i", [P, G, CH], I32)
        tmp_i = sb("tmp_i", [P, G, CH], I32)
        off = sb("off", [P, G, CH])
        first_i = sb("first_i", [1, G], I32)
        first = sb("first", [1, G])
        start = sb("start", [P, G])
        lane_i = sb("lane_i", [P, 1], I32)
        lane = sb("lane", [P, 1])
        padded = ctx.enter_context(nc.semaphore("padded"))
        loaded = ctx.enter_context(nc.semaphore("loaded"))
        lane_done = ctx.enter_context(nc.semaphore("lane_done"))
        first_done = ctx.enter_context(nc.semaphore("first_done"))
        start_done = ctx.enter_context(nc.semaphore("start_done"))
        step = ctx.enter_context(nc.semaphore("step"))
        block = ctx.enter_context(nc.Block())
        NL = 3 * 3 + 1

        @block.sync
        def _(sp):
            sp.wait_ge(padded, 3)
            for arr, to in ((dst, dst_i), (src, src_i), (edge_weight, weight)):
                body = arr[0:(G - 1) * SC].rearrange("(g p c) -> p g c", p=P, c=CH)
                sp.dma_start(to[:, 0:G - 1, :], body).then_inc(loaded, 16)
                tail = arr[(G - 1) * SC:(G - 1) * SC + TP * CH].rearrange("(p c) -> p c", c=CH)
                sp.dma_start(to[0:TP, G - 1, :], tail).then_inc(loaded, 16)
                rest = arr[E - TR:E].rearrange("(a c) -> a c", a=1)
                sp.dma_start(to[TP:TP + 1, G - 1, 0:TR], rest).then_inc(loaded, 16)
            with nc.allow_non_contiguous_dma(reason="one element per superchunk"):
                sp.dma_start(first_i[0:1, 0:G - 1], dst[0:(G - 1) * SC].rearrange("(a g s) -> a g s", a=1, s=SC)[:, :, 0]).then_inc(loaded, 16)
                sp.dma_start(first_i[0:1, G - 1:G], dst[(G - 1) * SC:(G - 1) * SC + 1].rearrange("(a b) -> a b", a=1)).then_inc(loaded, 16)

        @block.gpsimd
        def _(pool):
            pool.iota(lane_i[:, :], [[0, 1]], base=0, channel_multiplier=1).then_inc(lane_done, 1)

        @block.tensor
        def _(pe):
            pe.wait_ge(first_done, 1)
            pe.matmul(banks[0][:, 0:G], ones_row[:, :], first[:, :], start=True, stop=True).then_inc(start_done, 1)

        @block.vector
        def _(dve):
            n = [0]

            def then(ins):
                n[0] += 1
                ins.then_inc(step, 1)
                dve.wait_ge(step, n[0])

            dve.memset(src_i[:, G - 1, :], NB * P).then_inc(padded, 1)
            dve.memset(dst_i[:, G - 1, :], 0).then_inc(padded, 1)
            dve.memset(weight[:, G - 1, :], 0.0).then_inc(padded, 1)
            dve.memset(tile1[:, G, :], 0.0)
            dve.memset(fields[:, :, G, :], 0.0)
            dve.wait_ge(loaded, 16 * (NL + 1))
            dve.tensor_scalar(first[:, :], first_i[:, :], float(N - P), None, ALU.min).then_inc(first_done, 1)
            then(dve.tensor_scalar(tmp_i[:, :, :], src_i[:, :, :], 7, None, ALU.logical_shift_right))
            then(dve.tensor_copy(bucket[:, :, :], tmp_i[:, :, :]))
            then(dve.tensor_scalar(tmp_i[:, :, :], src_i[:, :, :], P - 1, None, ALU.bitwise_and))
            dve.tensor_copy(fields[:, SRC, 0:G, :], tmp_i[:, :, :])
            dve.tensor_scalar(tile1[:, 0:G, :], bucket[:, :, :], 1.0, None, ALU.add)
            for part in range(3):
                then(dve.tensor_copy(fields[:, W + part, 0:G, :], weight[:, :, :]))
                if part < 2:
                    then(dve.tensor_tensor(weight[:, :, :], weight[:, :, :], fields[:, W + part, 0:G, :], ALU.subtract))
            dve.wait_ge(start_done, 1)
            then(dve.tensor_copy(start[:, :], banks[0][:, 0:G]))
            then(dve.tensor_tensor(off[:, :, :], dst_i[:, :, :], start[:, :].unsqueeze(2).broadcast_to([P, G, CH]), ALU.subtract))
            dve.tensor_copy(fields[:, DST, 0:G, :], off[:, :, :])
            then(dve.tensor_scalar(inside[:, :, :], off[:, :, :], 0.0, None, ALU.is_ge))
            then(dve.scalar_tensor_tensor(out=inside[:, :, :], in0=off[:, :, :], scalar=float(P), in1=inside[:, :, :], op0=ALU.is_lt, op1=ALU.mult))
            then(dve.scalar_tensor_tensor(out=inside[:, :, :], in0=bucket[:, :, :], scalar=float(NB), in1=inside[:, :, :], op0=ALU.is_equal, op1=ALU.max))
            dve.wait_ge(lane_done, 1)
            then(dve.tensor_copy(lane[:, :], lane_i[:, :]))
            then(dve.tensor_scalar(rows_i[:, :], start[:, :], lane[:, 0:1], None, ALU.add))
    return tile1, fields, inside, left, n_left, rows_i


def merge_stats(dve, then, stats, mv, D):
    even, odd = stats[:, :, 1], stats[:, :, 4]
    then(dve.tensor_tensor(mv[:, 1, :], even, odd, ALU.subtract))
    then(dve.tensor_tensor(mv[:, 1, :], mv[:, 1, :], mv[:, 1, :], ALU.mult))
    then(dve.tensor_scalar(mv[:, 1, :], mv[:, 1, :], D / 4.0, None, ALU.mult))
    then(dve.tensor_tensor(mv[:, 0, :], stats[:, :, 2], stats[:, :, 5], ALU.add))
    then(dve.tensor_tensor(mv[:, 1, :], mv[:, 0, :], mv[:, 1, :], ALU.add))
    then(dve.tensor_scalar(mv[:, 1, :], mv[:, 1, :], 1.0 / D, None, ALU.mult))
    then(dve.tensor_tensor(mv[:, 0, :], even, odd, ALU.add))
    then(dve.tensor_scalar(mv[:, 0, :], mv[:, 0, :], 0.5, None, ALU.mult))


def attention(nc, shared, x, node_vec1, wq, wk, wv, wo, bo, kg, kb, vg, vb, xn_dram, NT, TAIL, N, D, H, HD):
    banks, acc, ident, iota, iota1_c, iota_j, ones_row, before = shared
    KV = 2 * D
    HH = 2 * H
    with ExitStack() as ctx:
        def sb(name, shape, dt=F32):
            return ctx.enter_context(nc.sbuf_tensor(name, shape, dt))

        def sem(name):
            return ctx.enter_context(nc.semaphore(name))

        xn = [sb(f"xn{i}", [P, D]) for i in range(2)]
        xT = [sb(f"xT{i}", [P, 2, P]) for i in range(2)]
        xT_all = sb("xT_all", [P, NT, 2, P])
        sq = sb("sq", [P, KV])
        hat = [sb(f"hat{i}", [P, KV]) for i in range(2)]
        kvn = [sb(f"kvn{i}", [P, KV]) for i in range(2)]
        w_nat = sb("w_nat", [P, 4, 2, D])
        wkvT = sb("wkvT", [P, 2, KV])
        woT = sb("woT", [P, 2, D])
        vecs = sb("vecs", [1, D + 4 * HD])
        gain = sb("gain", [P, KV])
        shift = sb("shift", [P, KV])
        bo_b = sb("bo_b", [P, D])
        nv = sb("nv", [P, NT])
        stats = sb("stats", [P, NT, 6])
        mv = sb("mv", [P, 2, NT])
        dev = sb("dev", [P, NT])
        rstd = sb("rstd", [P, NT])
        hsum = sb("hsum", [P, 2, HH])
        ss = sb("ss", [P, HH])
        hdev = sb("hdev", [P, HH])
        hinv = sb("hinv", [P, HH])
        kvT = sb("kvT", [P, 2, P])
        R = sb("R", [P, 2, D])
        M = sb("M", [P, 2, D])
        eps = sb("eps", [P, 1])
        turn_ps, proj_ps, kv_ps, mix_ps = banks[0:2], banks[2:4], banks[4:6], banks[6:8]

        x_in = sem("x_in"); w_in = sem("w_in"); nv_in = sem("nv_in")
        cleared = sem("cleared")
        w_turned = sem("w_turned"); spread = sem("spread"); w_ready = sem("w_ready")
        var_done = sem("var_done"); dev_done = sem("dev_done")
        xn_done = sem("xn_done"); stored = sem("stored"); xn_free = sem("xn_free")
        turned = sem("turned"); xT_done = sem("xT_done"); proj = sem("proj")
        squared = sem("squared"); summed = sem("summed"); rooted = sem("rooted"); inverted = sem("inverted")
        hat_done = sem("hat_done"); gained = sem("gained"); kvn_done = sem("kvn_done"); kv_used = sem("kv_used")
        kvT_done = sem("kvT_done"); R_made = sem("R_made"); R_done = sem("R_done")
        M_made = sem("M_made"); M_done = sem("M_done"); copied = sem("copied")
        xT_back = sem("xT_back"); mixed = sem("mixed"); added = sem("added")
        step = sem("step"); aggr = sem("aggr")
        block = ctx.enter_context(nc.Block())
        NW = 4 + 5
        LAST = NT - 1

        def tiles(eng, one):
            one(0, 0)
            with eng.Fori(0, (NT - 3) // 2) as h:
                one(2 * h + 1, 1)
                one(2 * h + 2, 0)
            one(NT - 2, 1)
            one(NT - 1, 0)

        def pairs(eng, one):
            with eng.Fori(0, NT // 2) as h:
                one(2 * h, 0)
                one(2 * h + 1, 1)
            one(NT - 1, 0)

        @block.sync
        def _(sp):
            sp.wait_ge(cleared, 2)
            for i, w in enumerate((wq, wk, wv, wo)):
                sp.dma_start(w_nat[:, i, :, :], w.rearrange("(m p) d -> p m d", p=P)).then_inc(w_in, 16)
            sp.dma_start(vecs[:, 0:D], bo.rearrange("(a d) -> a d", a=1)).then_inc(w_in, 16)
            for i, v in enumerate((kg, vg, kb, vb)):
                sp.dma_start(vecs[:, D + i * HD:D + (i + 1) * HD], v.rearrange("(a d) -> a d", a=1)).then_inc(w_in, 16)
            sp.dma_start(acc[0:TAIL, LAST, :], x[LAST * P:N, :]).then_inc(x_in, 16)
            sp.dma_start(acc[:, 0:LAST, :], x[0:LAST * P, :].rearrange("(t p) d -> p t d", p=P)).then_inc(x_in, 16)
            with nc.allow_non_contiguous_dma(reason="one value per node"):
                sp.dma_start(nv[:, 0:LAST], node_vec1[0:LAST * P, :].rearrange("(t p) a -> p (t a)", p=P)).then_inc(nv_in, 16)
                sp.dma_start(nv[0:TAIL, LAST:NT], node_vec1[LAST * P:N, :]).then_inc(nv_in, 16)
            sp.sem_inc(xn_free, 2)

            def store(t, i):
                sp.wait_ge(xn_done, t + 1)
                sp.dma_start(xn_dram[bass.ds(t * P, P), :], xn[i][:, :]).then_inc(stored, 16)
                sp.wait_ge(stored, (t + 1) * 16)
                sp.sem_inc(xn_free, 1)

            pairs(sp, store)

        @block.gpsimd
        def _(pool):
            pool.sem_inc(kvn_done, 2)
            pool.wait_ge(w_ready, 1)

            def affine(t, i):
                pool.wait_ge(hat_done, t + 3)
                pool.wait_ge(kv_used, t + 1)
                pool.tensor_tensor(kvn[i][:, :], hat[i][:, :], gain[:, :], ALU.mult).then_inc(gained, 1)
                pool.wait_ge(gained, t + 1)
                pool.tensor_tensor(kvn[i][:, :], kvn[i][:, :], shift[:, :], ALU.add).then_inc(kvn_done, 1)

            pairs(pool, affine)

        @block.scalar
        def _(act):
            act.sem_inc(xT_done, 2)
            act.wait_ge(var_done, 1)
            act.activation(dev[:, :], mv[:, 1, :], ACT.Sqrt, bias=eps[:, 0:1], scale=1.0).then_inc(dev_done, 1)

            def take_xT(t, i):
                act.wait_ge(turned, t + 3)
                act.wait_ge(proj, t + 1)
                act.copy(xT[i][:, :, :], turn_ps[i][:, 0:2 * P].rearrange("p (k c) -> p k c", k=2)).then_inc(xT_done, 1)
                act.wait_ge(xT_done, t + 3)
                act.copy(xT_all[:, bass.ds(t, 1), :, :].rearrange("p a k c -> p (a k) c"), xT[i][:, :, :]).then_inc(copied, 1)

            def heads(t, i):
                act.wait_ge(proj, t + 3)
                act.activation(sq[:, :], proj_ps[i][:, :], ACT.Square).then_inc(squared, 1)
                act.wait_ge(summed, t + 1)
                act.activation(hdev[:, :], ss[:, :], ACT.Sqrt, bias=eps[:, 0:1], scale=1.0 / HD).then_inc(rooted, 1)

            def one(t, i):
                heads(t, i)
                if not isinstance(t, int) or t + 2 < NT:
                    take_xT(t + 2, i)

            take_xT(0, 0)
            take_xT(1, 1)
            tiles(act, one)

            def give_xT(t, i):
                act.wait_ge(mixed, t + 1)
                act.copy(xT[i][:, :, :], xT_all[:, bass.ds(t, 1), :, :].rearrange("p a k c -> p (a k) c")).then_inc(xT_back, 1)

            act.wait_ge(copied, NT)
            act.wait_ge(proj, NT + 2)
            pairs(act, give_xT)

        @block.tensor
        def _(pe):
            pe.sem_inc(turned, 2)
            pe.sem_inc(proj, 2)
            pe.sem_inc(kv_used, 2)
            pe.sem_inc(mixed, 2)
            pe.wait_ge(w_in, 16 * NW)
            for s in range(2):
                for j in range(2):
                    at = D + (2 * s + j) * HD
                    pe.matmul(proj_ps[s][:, j * D:(j + 1) * D], ones_row[:, :],
                              vecs[:, at:at + HD].unsqueeze(1).broadcast_to([1, H, HD]), start=True, stop=True)
            pe.matmul(turn_ps[0][:, 0:D], ones_row[:, :], vecs[:, 0:D], start=True, stop=True).then_inc(spread, 1)
            for k in range(2):
                for m in range(2):
                    pe.transpose(kv_ps[k][:, m * P:(m + 1) * P], w_nat[:, 3, m, k * P:(k + 1) * P], ident[:, :])
                for w in range(2):
                    for m in range(2):
                        last = pe.transpose(mix_ps[k][:, w * D + m * P:w * D + (m + 1) * P],
                                            w_nat[:, 1 + w, m, k * P:(k + 1) * P], ident[:, :])
            last.then_inc(w_turned, 1)
            pe.wait_ge(w_ready, 1)

            def turn(t, i):
                pe.wait_ge(xn_done, t + 1)
                pe.wait_ge(xT_done, t + 1)
                for k in range(2):
                    tr = pe.transpose(turn_ps[i][:, k * P:(k + 1) * P], xn[i][:, k * P:(k + 1) * P], ident[:, :])
                tr.then_inc(turned, 1)

            def project(t, i):
                pe.wait_ge(xT_done, t + 3)
                pe.wait_ge(hat_done, t + 1)
                for k in range(2):
                    mm = pe.matmul(proj_ps[i][:, :], xT[i][:, k, :], wkvT[:, k, :], start=(k == 0), stop=(k == 1))
                mm.then_inc(proj, 1)

            def kv_product(t, i, rows):
                pe.wait_ge(kvn_done, t + 3)
                first = isinstance(t, int) and t == 0
                final = isinstance(t, int) and t == LAST
                for c in range(2):
                    mm = pe.matmul(kv_ps[c][:, 0:P], kvn[i][0:rows, D + c * P:D + (c + 1) * P],
                                   kvn[i][0:rows, c * P:(c + 1) * P], start=first, stop=final, skip_group_check=True)
                mm.then_inc(kv_used, 1)

            def one(t, i):
                fixed = isinstance(t, int)
                if not fixed or t + 2 < NT:
                    turn(t + 2, i)
                if not fixed or t + 1 < NT:
                    project(t + 1, 1 - i)
                if not fixed or t > 0:
                    kv_product(t - 1, 1 - i, P)

            turn(0, 0)
            turn(1, 1)
            project(0, 0)
            one(0, 0)
            one(1, 1)
            with pe.Fori(0, (NT - 5) // 2) as h:
                one(2 * h + 2, 0)
                one(2 * h + 3, 1)
            one(NT - 3, 0)
            one(NT - 2, 1)
            one(NT - 1, 0)
            kv_product(LAST, 0, TAIL)

            pe.wait_ge(kvT_done, 1)
            for c in range(2):
                mm = pe.matmul(mix_ps[c][:, 0:D], kvT[:, c, :], woT[:, c, :], start=True, stop=True)
            mm.then_inc(R_made, 1)
            pe.wait_ge(R_done, 1)
            for m in range(2):
                for c in range(2):
                    mm = pe.matmul(proj_ps[m][:, 0:D], w_nat[:, 0, c, m * P:(m + 1) * P], R[:, c, :], start=(c == 0), stop=(c == 1))
            mm.then_inc(M_made, 1)
            pe.wait_ge(M_done, 1)

            def mix(t, i):
                pe.wait_ge(xT_back, t + 1)
                pe.wait_ge(added, t + 1)
                for k in range(2):
                    mm = pe.matmul(mix_ps[i][:, 0:D], xT[i][:, k, :], M[:, k, :], start=(k == 0), stop=(k == 1))
                mm.then_inc(mixed, 1)

            pairs(pe, mix)

        @block.vector
        def _(dve):
            n = [0]

            def then(ins):
                n[0] += 1
                ins.then_inc(step, 1)
                dve.wait_ge(step, n[0])

            dve.sem_inc(hat_done, 2)
            dve.sem_inc(added, 2)
            dve.memset(acc[:, LAST, :], 0.0).then_inc(cleared, 1)
            dve.memset(nv[:, LAST:NT], 0.0).then_inc(cleared, 1)
            then(dve.memset(kvT[:, :, :], 0.0))
            then(dve.memset(eps[:, :], EPS))
            dve.wait_ge(w_turned, 1)
            for k in range(2):
                heads = mix_ps[k][:, :].rearrange("p (h d) -> p h d", d=HD)
                then(dve.tensor_reduce(hsum[:, k, :], heads, AX.X, ALU.add))
                then(dve.tensor_scalar(hsum[:, k, :], hsum[:, k, :], 1.0 / HD, None, ALU.mult))
                then(dve.tensor_tensor(wkvT[:, k, :].rearrange("p (h d) -> p h d", d=HD), heads,
                                       hsum[:, k, :].unsqueeze(2).broadcast_to([P, HH, HD]), ALU.subtract))
                then(dve.tensor_copy(woT[:, k, :], kv_ps[k][:, 0:D]))
            dve.wait_ge(spread, 1)
            dve.tensor_copy(gain[:, :], proj_ps[0][:, :])
            then(dve.tensor_copy(shift[:, :], proj_ps[1][:, :]))
            then(dve.tensor_copy(bo_b[:, :], turn_ps[0][:, 0:D]))
            dve.wait_ge(x_in, 32)
            with dve.Fori(0, NT) as t:
                dve.bn_stats(stats[:, bass.ds(t, 1), :].rearrange("p a d -> p (a d)"),
                             acc[:, bass.ds(t, 1), :].rearrange("p a d -> p (a d)")).then_inc(aggr, 1)
            dve.wait_ge(aggr, NT)
            merge_stats(dve, then, stats, mv, D)
            dve.sem_inc(var_done, 1)
            dve.wait_ge(dev_done, 1)
            then(dve.reciprocal(rstd[:, :], dev[:, :]))
            dve.wait_ge(nv_in, 32)
            dve.sem_inc(w_ready, 1)

            def normalize(t, i):
                row = acc[:, bass.ds(t, 1), :].rearrange("p a d -> p (a d)")
                dve.wait_ge(xn_free, t + 1)
                dve.wait_ge(turned, t + 1)
                dve.tensor_scalar(xn[i][:, :], row, mv[:, 0, bass.ds(t, 1)], rstd[:, bass.ds(t, 1)],
                                  ALU.subtract, ALU.mult).then_inc(xn_done, 1)
                dve.scalar_tensor_tensor(out=row, in0=row, scalar=nv[:, bass.ds(t, 1)], in1=bo_b[:, :], op0=ALU.add, op1=ALU.add)

            def one(t, i):
                dve.wait_ge(squared, t + 1)
                dve.tensor_reduce(ss[:, :], sq[:, :].rearrange("p (h d) -> p h d", d=HD), AX.X, ALU.add).then_inc(summed, 1)
                if not isinstance(t, int) or t + 2 < NT:
                    normalize(t + 2, i)
                dve.wait_ge(rooted, t + 1)
                dve.reciprocal(hinv[:, :], hdev[:, :]).then_inc(inverted, 1)
                dve.wait_ge(inverted, t + 1)
                dve.wait_ge(kvn_done, t + 1)
                dve.tensor_tensor(hat[i][:, :].rearrange("p (h d) -> p h d", d=HD),
                                  proj_ps[i][:, :].rearrange("p (h d) -> p h d", d=HD),
                                  hinv[:, :].unsqueeze(2).broadcast_to([P, HH, HD]), ALU.mult).then_inc(hat_done, 1)

            normalize(0, 0)
            normalize(1, 1)
            tiles(dve, one)

            dve.wait_ge(kv_used, NT + 2)
            for c in range(2):
                for h in range(2):
                    part = slice(h * HD, (h + 1) * HD)
                    last = dve.tensor_scalar(kvT[part, c, part], kv_ps[c][part, part], 1.0 / N, None, ALU.mult)
            last.then_inc(kvT_done, 1)
            dve.wait_ge(R_made, 1)
            dve.tensor_copy(R[:, 0, :], mix_ps[0][:, 0:D])
            dve.tensor_copy(R[:, 1, :], mix_ps[1][:, 0:D]).then_inc(R_done, 1)
            dve.wait_ge(M_made, 1)
            dve.tensor_copy(M[:, 0, :], proj_ps[0][:, 0:D])
            dve.tensor_copy(M[:, 1, :], proj_ps[1][:, 0:D]).then_inc(M_done, 1)

            def add(t, i):
                row = acc[:, bass.ds(t, 1), :].rearrange("p a d -> p (a d)")
                dve.wait_ge(mixed, t + 3)
                dve.tensor_tensor(row, row, mix_ps[i][:, 0:D], ALU.add).then_inc(added, 1)

            pairs(dve, add)


def edge_sum(nc, shared, edges, xn_dram, G, NG, NT, D):
    banks, acc, ident, iota, iota1_c, iota_j, ones_row, before = shared
    tile1, fields, inside, left, n_left, rows_i = edges
    EARLY_DVE, EARLY_POOL = (0, 1, 2), (3, 4)
    LINKS = 6
    with ExitStack() as ctx:
        def sb(name, shape, dt=F32):
            return ctx.enter_context(nc.sbuf_tensor(name, shape, dt))

        def sem(name):
            return ctx.enter_context(nc.semaphore(name))

        hot_t = sb("hot_t", [P, NB, CH], BF16)
        steps = sb("steps", [P, NB, SW])
        keep = sb("keep", [P, NB, SW], BF16)
        ranks = sb("ranks", [P, NB, SW], BF16)
        rank1 = sb("rank1", [P, CH], BF16)
        far = sb("far", [P, CH], BF16)
        slot = sb("slot", [P, P, CH], BF16)
        vals = sb("vals", [P, FIELDS, NB, CH], BF16)
        table = [sb(f"table{i}", [P, FIELDS, GRP, NB], BF16) for i in range(2)]
        cur = sb("cur", [P, BU + 1, FIELDS, GRP], BF16)
        hot = [sb(f"hot{i}", [P, 2, P, GRP], BF16) for i in range(3)]
        hot_w = [sb(f"hot_w{i}", [P, 3, P, GRP], BF16) for i in range(3)]
        block_sb = [sb(f"block_sb{i}", [P, GRP, P]) for i in range(3)]
        window = [sb(f"window{i}", [P, GRP, D]) for i in range(2)]
        row_of = sb("row_of", [P, 1], I32)
        landing = sb("landing", [P, D])

        def block_ps(i, j):
            return banks[2 * (i % 2) + j // 4][:, (j % 4) * P:(j % 4 + 1) * P]

        sum_ps = [banks[4 + i][:, 0:D] for i in range(2)]
        base_ps = banks[6][:, 0:NB]
        table_ps = banks[7][:, 0:FIELDS * NB].rearrange("p (f b) -> p f b", f=FIELDS)

        keep_set = sem("keep_set"); steps_done = sem("steps_done"); hot_done = sem("hot_done"); tiles_done = sem("tiles_done"); base_done = sem("base_done")
        chain = sem("chain"); slot_done = sem("slot_done"); vals_done = sem("vals_done"); table_made = sem("table_made")
        row_done = sem("row_done"); gathered = sem("gathered"); window_in = sem("window_in"); passed = sem("passed")
        dcur = sem("dcur"); unpacked = sem("unpacked")
        w_done = sem("w_done"); a_done = sem("a_done"); a_copied = sem("a_copied")
        o_done = sem("o_done"); o_added = sem("o_added")
        block = ctx.enter_context(nc.Block())

        def schedule(eng, sort, begin, unit):
            sort(0)
            with eng.Fori(1, GRP) as s:
                sort(s)
            begin()

            def group(g, par, more):
                with eng.Fori(0, GRP - 1) as k:
                    unit(g, k, par, BU, more, True)
                unit(g, GRP - 1, par, BU + 1, more, more)

            with eng.Fori(0, NG // 2) as h:
                group(2 * h, 0, True)
                group(2 * h + 1, 1, True)
            group(NG - 1, 0, False)

        @block.gpsimd
        def _(pool):
            def values(s, parts):
                if not isinstance(s, int):
                    pool.wait_ge(table_made, s)
                pool.wait_ge(tiles_done, s + 1)
                for f in parts:
                    ins = pool.tensor_tensor(vals[:, f, :, :], hot_t[:, :, :],
                                             fields[:, f, bass.ds(s, 1), :].broadcast_to([P, NB, CH]), ALU.mult)
                ins.then_inc(vals_done, 1)

            def fetch(s, k, par):
                pool.tensor_copy(row_of[:, :], rows_i[:, bass.ds(s, 1)]).then_inc(row_done, 1)
                pool.wait_ge(row_done, s + 1)
                pool.sem_inc(passed, 1)
                pool.indirect_dma_start(out=landing[:, :], out_offset=None, in_=xn_dram,
                                        in_offset=bass.IndirectOffsetOnAxis(ap=row_of[:, 0:1], axis=0)).then_inc(gathered, 16)
                pool.wait_ge(gathered, (s + 1) * 16)
                pool.sem_inc(passed, 1)
                pool.tensor_copy(window[par][:, bass.ds(k, 1), :].rearrange("p a d -> p (a d)"), landing[:, :]).then_inc(window_in, 1)

            def sort(s):
                fetch(s, s, 0)
                values(s + 1, EARLY_POOL)

            def unit(g, k, par, n, more, after):
                s = g * GRP + k + GRP
                if more:
                    pool.wait_ge(o_done, g * NT + 2)
                    pool.sem_inc(passed, 1)
                    fetch(s, k, 1 - par)
                    values(s + 1, range(FIELDS))

            values(0, EARLY_POOL)
            schedule(pool, sort, lambda: None, unit)

        @block.tensor
        def _(pe):
            pe.sem_inc(a_done, 2)
            pe.sem_inc(o_done, 2)

            def base(s):
                pe.wait_ge(tiles_done, s + 1)
                for c in range(CH):
                    mm = pe.matmul(base_ps, before[:, :], hot_t[:, :, c], start=(c == 0), stop=(c == CH - 1))
                mm.then_inc(base_done, 1)

            def make_table(s):
                pe.wait_ge(vals_done, s + 1)
                pe.wait_ge(slot_done, s + 1)
                for c in range(CH):
                    mm = pe.matmul(table_ps, slot[:, :, c], vals[:, :, :, c], start=(c == 0), stop=(c == CH - 1))
                mm.then_inc(table_made, 1)

            def sort(s):
                base(s)
                make_table(s)

            def blocks(it, i, first):
                pe.wait_ge(w_done, it + 2)
                pe.wait_ge(a_copied, it + 1 if first else it)
                for j in range(GRP):
                    for part in range(3):
                        mm = pe.matmul(block_ps(i, j), hot[i % 3][:, DST, :, j], hot_w[i % 3][:, part, :, j],
                                       start=(part == 0), stop=(part == 2))
                mm.then_inc(a_done, 1)

            def rows(it, i, par, first):
                pe.wait_ge(a_copied, it + 2)
                pe.wait_ge(o_added, it + 1 if first else it)
                for j in range(GRP):
                    mm = pe.matmul(sum_ps[i % 2], block_sb[i % 3][:, j, :], window[par][:, j, :], start=(j == 0), stop=(j == GRP - 1))
                mm.then_inc(o_done, 1)

            def unit(g, k, par, n, more, after):
                it = g * NT + k * BU
                s = g * GRP + k + GRP
                pe.wait_ge(window_in, (g + 1) * GRP)
                if more:
                    base(s)
                for i in range(n):
                    if i + 1 < n:
                        blocks(it + i + 1, i + 1, False)
                    elif after:
                        blocks(it + n, 0, n > BU)
                    rows(it + i, i, par, i == 0)
                    if more and i == 3:
                        make_table(s)

            schedule(pe, sort, lambda: blocks(0, 0, True), unit)

        @block.scalar
        def _(act):
            act.sem_inc(a_copied, 1)

            def widen(s):
                if not isinstance(s, int):
                    act.wait_ge(slot_done, s)
                act.wait_ge(tiles_done, s + 1)
                act.copy(steps[:, :, 2:SW], hot_t[:, :, :]).then_inc(steps_done, 1)

            def evacuate(it, i):
                act.wait_ge(a_done, it + 3)
                act.wait_ge(o_done, it + 2 if i == 0 else it + 1)
                for half in range(2):
                    ins = act.copy(block_sb[i % 3][:, 4 * half:4 * half + 4, :].rearrange("p m c -> p (m c)"), banks[2 * (i % 2) + half][:, :])
                ins.then_inc(a_copied, 1)

            def unit(g, k, par, n, more, after):
                it = g * NT + k * BU
                for i in range(n):
                    if i + 1 < n:
                        evacuate(it + i + 1, i + 1)
                    elif after:
                        evacuate(it + n, 0)
                    if more and i == 3:
                        widen(g * GRP + k + GRP + 1)

            widen(0)
            schedule(act, lambda s: widen(s + 1), lambda: evacuate(0, 0), unit)

        @block.vector
        def _(dve):
            dve.sem_inc(o_added, 1)
            dve.sem_inc(w_done, 1)
            dve.memset(steps[:, :, 0:2], 0.0).then_inc(keep_set, 1)
            dve.memset(keep[:, :, :], 1.0).then_inc(keep_set, 1)
            dve.wait_ge(keep_set, 2)
            dve.memset(keep[:, :, 0:1], 0.0).then_inc(keep_set, 1)
            dve.wait_ge(keep_set, 3)
            links = [0]

            def link(s, ins):
                links[0] += 1
                ins.then_inc(chain, 1)
                dve.wait_ge(chain, s * LINKS + links[0])

            def hot_tiles(s):
                if not isinstance(s, int):
                    dve.wait_ge(vals_done, s)
                dve.tensor_tensor(hot_t[:, :, :], iota1_c[:, 0:NB, :], tile1[:, bass.ds(s, 1), :].broadcast_to([P, NB, CH]),
                                  ALU.is_equal).then_inc(tiles_done, 1)

            def scan(s):
                links[0] = 0
                dve.wait_ge(steps_done, s + 1)
                dve.wait_ge(base_done, s + 1)
                link(s, dve.tensor_copy(steps[:, :, 0], base_ps))
                flat = lambda a: a.rearrange("p b c -> p (b c)")
                link(s, dve.tensor_tensor_scan(flat(ranks[:, :, :]), flat(keep[:, :, :]), flat(steps[:, :, :]), 0.0, ALU.mult, ALU.add))

            def rank(s):
                link(s, dve.tensor_tensor(ranks[:, :, 2:SW], ranks[:, :, 2:SW], hot_t[:, :, :], ALU.mult))
                if not isinstance(s, int):
                    dve.wait_ge(slot_done, s)
                with nc.allow_low_precision("one value of each sum is not 0"):
                    link(s, dve.tensor_reduce(rank1[:, :], ranks[:, :, 2:SW].rearrange("p b c -> p c b"), AX.X, ALU.add))
                link(s, dve.scalar_tensor_tensor(out=far[:, :], in0=rank1[:, :], scalar=P + 0.5,
                                                 in1=inside[:, bass.ds(s, 1), :].rearrange("p a c -> p (a c)"), op0=ALU.is_lt, op1=ALU.mult))
                out = left[:, bass.ds(s, 1), :].rearrange("p a c -> p (a c)")
                link(s, dve.tensor_scalar(out, far[:, :], 0.5, None, ALU.is_lt))
                dve.tensor_reduce(n_left[:, bass.ds(s, 1)], out, AX.X, ALU.add)

            def slots(s):
                if not isinstance(s, int):
                    dve.wait_ge(table_made, s)
                dve.tensor_tensor(slot[:, :, :], iota1_c[:, :, :], rank1[:, :].unsqueeze(1).broadcast_to([P, P, CH]),
                                  ALU.is_equal).then_inc(slot_done, 1)

            def unpack(s, k, par):
                assert links[0] == LINKS
                dve.wait_ge(table_made, s + 1)
                dve.tensor_copy(table[par][:, :, bass.ds(k, 1), :].rearrange("p f a b -> p f (a b)"), table_ps).then_inc(unpacked, 1)

            def early_values(s):
                if not isinstance(s, int):
                    dve.wait_ge(table_made, s)
                dve.wait_ge(tiles_done, s + 1)
                for f in EARLY_DVE:
                    dve.tensor_tensor(vals[:, f, :, :], hot_t[:, :, :], fields[:, f, bass.ds(s, 1), :].broadcast_to([P, NB, CH]), ALU.mult)

            def sort(s):
                scan(s)
                rank(s)
                slots(s)
                unpack(s, s, 0)
                hot_tiles(s + 1)
                early_values(s + 1)

            def take(unit_no, first_step, from_table, at):
                dve.wait_ge(w_done, first_step + 1)
                dve.tensor_copy(cur[:, :, :, :], from_table[:, :, :, at].rearrange("p f j i -> p i f j")).then_inc(dcur, 1)
                dve.wait_ge(dcur, unit_no + 1)

            def hots(it, i, wait):
                if wait:
                    dve.wait_ge(a_done, it + 2 if i == "first" else it)
                i = 0 if i == "first" else i
                dve.tensor_tensor(hot[i % 3][:, :, :, :], iota_j[:, :, :].unsqueeze(1).broadcast_to([P, 2, P, GRP]),
                                  cur[:, i, 0:2, :].unsqueeze(2).broadcast_to([P, 2, P, GRP]), ALU.is_equal).then_inc(hot_done, 1)
                dve.wait_ge(hot_done, it + 1)
                dve.tensor_tensor(hot_w[i % 3][:, :, :, :], hot[i % 3][:, SRC, :, :].unsqueeze(1).broadcast_to([P, 3, P, GRP]),
                                  cur[:, i, W:W + 3, :].unsqueeze(2).broadcast_to([P, 3, P, GRP]), ALU.mult).then_inc(w_done, 1)

            def begin():
                dve.wait_ge(unpacked, GRP)
                take(0, 0, table[0], slice(0, BU + 1))
                hots(0, 0, False)
                hots(1, 1, False)

            def unit(g, k, par, n, more, after):
                u = g * GRP + k
                s = u + GRP
                it = g * NT + k * BU

                def add(i):
                    row = acc[:, bass.ds(k * BU + i, 1), :].rearrange("p a d -> p (a d)")
                    dve.wait_ge(o_done, it + i + 3)
                    dve.tensor_tensor(row, row, sum_ps[i % 2], ALU.add).then_inc(o_added, 1)

                for i in range(n):
                    if i + 2 < n:
                        hots(it + i + 2, i + 2, True)
                    elif after:
                        if i == n - 2:
                            if more:
                                unpack(s, k, 1 - par)
                            if n == BU:
                                take(u + 1, it + n, table[par], bass.ds((k + 1) * BU, BU + 1))
                            else:
                                dve.wait_ge(unpacked, (g + 2) * GRP)
                                take(u + 1, it + n, table[1 - par], slice(0, BU + 1))
                        hots(it + i + 2, "first" if n > BU and i == n - 2 else i + 2 - n, True)
                    if i > 0:
                        add(i - 1)
                    if more and i == 0:
                        scan(s)
                    if more and i == 1:
                        rank(s)
                    if more and i == 2:
                        slots(s)
                    if more and i == 3:
                        hot_tiles(s + 1)
                add(n - 1)

            hot_tiles(0)
            early_values(0)
            schedule(dve, sort, begin, unit)


def stragglers(nc, shared, edges, src, dst, edge_weight, xn_dram, E, G, TP, TR, NT, D):
    banks, acc, ident, iota, iota1_c, iota_j, ones_row, before = shared
    tile1, fields, inside, left, n_left, rows_i = edges
    SC = CH * P
    with ExitStack() as ctx:
        def sb(name, shape, dt=F32):
            return ctx.enter_context(nc.sbuf_tensor(name, shape, dt))

        def sem(name):
            return ctx.enter_context(nc.semaphore(name))

        ones_col = sb("ones_col", [P, 1])
        count = sb("count", [P, 1])
        total = sb("total", [1, 1], I32)
        src_l = sb("src_l", [P, G * CH], I32)
        dst_l = sb("dst_l", [P, G * CH], I32)
        w_l = sb("w_l", [P, G * CH])
        idx = sb("idx", [P, 1], I32)
        rows = sb("rows", [P, D])
        rel = sb("rel", [P, 1])
        w_one = sb("w_one", [P, 1])
        hot = sb("hot", [P, P])
        left_done = sem("left_done"); total_ps = sem("total_ps"); total_done = sem("total_done")
        padded = sem("padded"); loaded = sem("loaded"); idx_done = sem("idx_done"); rows_in = sem("rows_in")
        rel_done = sem("rel_done"); hot_done = sem("hot_done"); made = sem("made"); added = sem("added")
        passed = sem("passed")
        block = ctx.enter_context(nc.Block())
        Q = G * CH

        def some_left(eng):
            eng.wait_ge(total_done, 1)
            return eng.If(eng.value_load(total[0:1, 0:1], min_val=0, max_val=Q * P) > 0)

        @block.sync
        def _(sp):
            with some_left(sp):
                sp.wait_ge(padded, 3)
                for arr, to in ((dst, dst_l), (src, src_l), (edge_weight, w_l)):
                    at = to[:, :].rearrange("p (g c) -> p g c", c=CH)
                    body = arr[0:(G - 1) * SC].rearrange("(g p c) -> p g c", p=P, c=CH)
                    sp.dma_start(at[:, 0:G - 1, :], body).then_inc(loaded, 16)
                    tail = arr[(G - 1) * SC:(G - 1) * SC + TP * CH].rearrange("(p c) -> p c", c=CH)
                    sp.dma_start(at[0:TP, G - 1, :], tail).then_inc(loaded, 16)
                    rest = arr[E - TR:E].rearrange("(a c) -> a c", a=1)
                    sp.dma_start(at[TP:TP + 1, G - 1, 0:TR], rest).then_inc(loaded, 16)

        @block.gpsimd
        def _(pool):
            with some_left(pool):
                pool.wait_ge(loaded, 9 * 16)
                with pool.Fori(0, Q) as q:
                    pool.tensor_copy(idx[:, :], dst_l[:, bass.ds(q, 1)]).then_inc(idx_done, 1)
                    pool.wait_ge(idx_done, q + 1)
                    pool.wait_ge(made, q * NT + 1)
                    pool.sem_inc(passed, 1)
                    pool.indirect_dma_start(out=rows[:, :], out_offset=None, in_=xn_dram,
                                            in_offset=bass.IndirectOffsetOnAxis(ap=idx[:, 0:1], axis=0)).then_inc(rows_in, 16)
                    pool.wait_ge(rows_in, (q + 1) * 16)

        @block.tensor
        def _(pe):
            pe.sem_inc(made, 1)
            pe.wait_ge(left_done, 2)
            pe.matmul(banks[0][0:1, 0:1], count[:, :], ones_col[:, :], start=True, stop=True).then_inc(total_ps, 1)
            with some_left(pe):
                with pe.Fori(0, Q) as q:
                    pe.wait_ge(rows_in, (q + 1) * 16)
                    pe.sem_inc(passed, 1)
                    with pe.Fori(0, NT) as b:
                        pe.wait_ge(hot_done, q * NT + b + 1)
                        pe.wait_ge(added, q * NT + b + 1)
                        pe.matmul(banks[1][:, 0:D], hot[:, :], rows[:, :], start=True, stop=True).then_inc(made, 1)

        @block.vector
        def _(dve):
            dve.sem_inc(added, 1)
            dve.memset(ones_col[:, :], 1.0).then_inc(left_done, 1)
            dve.tensor_reduce(count[:, :], n_left[:, :], AX.X, ALU.add).then_inc(left_done, 1)
            dve.wait_ge(total_ps, 1)
            dve.tensor_copy(total[:, :], banks[0][0:1, 0:1]).then_inc(total_done, 1)
            with some_left(dve):
                dve.memset(src_l[:, (G - 1) * CH:Q], NB * P).then_inc(padded, 1)
                dve.memset(dst_l[:, (G - 1) * CH:Q], 0).then_inc(padded, 1)
                dve.memset(w_l[:, (G - 1) * CH:Q], 0.0).then_inc(padded, 1)
                dve.wait_ge(loaded, 9 * 16)
                dve.tensor_tensor(w_l[:, :], w_l[:, :], left[:, :, :].rearrange("p g c -> p (g c)"), ALU.mult).then_inc(padded, 1)
                dve.wait_ge(padded, 4)
                with dve.Fori(0, Q) as q:
                    dve.wait_ge(added, q * NT + 1)
                    dve.tensor_copy(rel[:, :], src_l[:, bass.ds(q, 1)]).then_inc(rel_done, 1)
                    dve.tensor_copy(w_one[:, :], w_l[:, bass.ds(q, 1)]).then_inc(rel_done, 1)
                    with dve.Fori(0, NT) as b:
                        dve.wait_ge(rel_done, q * (NT + 2) + b + 2)
                        dve.wait_ge(made, q * NT + b + 1)
                        dve.tensor_scalar(hot[:, :], iota[:, :], rel[:, 0:1], w_one[:, 0:1], ALU.is_equal, ALU.mult).then_inc(hot_done, 1)
                        dve.wait_ge(hot_done, q * NT + b + 1)
                        dve.tensor_scalar(rel[:, :], rel[:, :], float(-P), None, ALU.add).then_inc(rel_done, 1)
                        dve.wait_ge(made, q * NT + b + 2)
                        row = acc[:, bass.ds(b, 1), :].rearrange("p a d -> p (a d)")
                        dve.tensor_tensor(row, row, banks[1][:, 0:D], ALU.add).then_inc(added, 1)


def put_rows(nc, shared, rows_dram, NT):
    acc = shared[1]
    with ExitStack() as ctx:
        rows_out = ctx.enter_context(nc.semaphore("rows_out"))
        block = ctx.enter_context(nc.Block())

        @block.sync
        def _(sp):
            sp.dma_start(rows_dram.rearrange("(t p) d -> p t d", p=P), acc[:, :, :]).then_inc(rows_out, 16)
            sp.wait_ge(rows_out, 16)


def experts(nc, banks, rows_dram, ident, iota, ones_row, Wg, bg, bias, W1, b1, W2, b2, out, NT, TAIL, N, D):
    X, F = W1.shape[0], W1.shape[2]
    FC = F // P
    QG = NT // 2
    TOK = 2 * P
    with ExitStack() as ctx:
        def sb(name, shape, dt=F32):
            return ctx.enter_context(nc.sbuf_tensor(name, shape, dt))

        def sem(name):
            return ctx.enter_context(nc.semaphore(name))

        w1 = [sb(f"w1_{i}", [P, X, 2, F], F32R) for i in range(2)]
        w2 = [sb(f"w2_{i}", [P, X, FC, D], F32R) for i in range(2)]
        wg_f = sb("wg_f", [P, 2, X])
        wg = [sb(f"wg_{i}", [P, 2, X], F32R) for i in range(2)]
        b1_s = sb("b1_s", [P, X, FC])
        b2_s = sb("b2_s", [X, D])
        gb_row = sb("gb_row", [1, 2 * X])
        gb = sb("gb", [P, X])
        eps = sb("eps2", [P, 1])
        r_in = sb("r_in", [P, 2, D])
        res = sb("res", [P, 2, D])
        z = sb("z", [P, 2, D])
        zT = [sb(f"zT{i}", [P, 2, TOK], F32R) for i in range(2)]
        stats = sb("stats2", [P, 2, 6])
        mv = sb("mv2", [P, 2, 2])
        dev = sb("dev2", [P, 2])
        rstd = sb("rstd2", [P, 2])
        logits = sb("logits", [P, 2, X])
        best = sb("best", [P, 2, 8])
        where = sb("where", [P, 2, 8], mybir.dt.uint32)
        where_f = sb("where_f", [P, 2, 2])
        gap = sb("gap", [P, 2])
        ex = sb("ex", [P, 2])
        den = sb("den", [P, 2])
        share = sb("share", [P, 2, 2])
        gate_a = sb("gate_a", [P, 2, X])
        gate = sb("gate", [P, 2, X])
        gateT = sb("gateT", [X, 2, P])
        hf = [sb(f"hf{i}", [P, FC, TOK]) for i in range(2)]
        hh = [sb(f"hh{i}", [P, FC, TOK], F32R) for i in range(2)]
        hl = [sb(f"hl{i}", [P, FC, TOK], F32R) for i in range(2)]

        def hid_ps(e, c):
            return banks[2 * (e % 2) + c // 2][:, (c % 2) * TOK:(c % 2 + 1) * TOK]

        y_ps = banks[4:6]
        turn_ps, small_ps = banks[6], banks[7]

        w_in = [sem(f"w_in{i}") for i in range(2)]
        small_in = sem("small_in"); row_in = sem("row_in"); out_done = sem("out_done")
        w_split = sem("w_split"); gb_ps = sem("gb_ps"); w_ready = sem("w_ready")
        var_done = sem("var_done"); dev_done = sem("dev_done"); z_done = sem("z_done"); z_turned = sem("z_turned")
        zh_done = sem("zh_done"); zl_done = sem("zl_done"); logit_ps = sem("logit_ps")
        gap_done = sem("gap_done"); ex_done = sem("ex_done"); gate_done = sem("gate_done")
        gateT_ps = sem("gateT_ps"); gateT_done = sem("gateT_done"); shift_ps = sem("shift_ps"); res_set = sem("res_set")
        hid = sem("hid"); relu_done = sem("relu_done"); split_done = sem("split_done")
        y_made = sem("y_made"); y_added = sem("y_added"); chain = sem("chain"); hi_done = sem("hi_done"); half_done = sem("half_done"); res_free = sem("res_free"); passed = sem("passed")
        block = ctx.enter_context(nc.Block())
        LINKS = 10

        def groups(eng, group):
            with eng.Fori(0, QG - 1) as q:
                group(q, 2, 2)
            group(QG - 1, 2, 1)
            group(QG, 1, 0)

        @block.sync
        def _(sp):
            for n in range(2 * X):
                if n >= 2:
                    sp.wait_ge(w_split, n - 1)
                e = n % X
                if n < X:
                    sp.dma_start(hf[n % 2][:, :, :].rearrange("p c t -> p (c t)").rearrange("p (k h) -> p k h", k=2),
                                 W1[e].rearrange("(k p) h -> p k h", p=P)).then_inc(w_in[n % 2], 16)
                else:
                    sp.dma_start(hf[n % 2][:, :, :], W2[e].rearrange("(c p) d -> p c d", p=P)).then_inc(w_in[n % 2], 16)

            def load(q, n):
                sp.dma_start(r_in[:, 0:n, :], rows_dram[bass.ds(q * TOK, n * P), :].rearrange("(t p) d -> p t d", p=P)).then_inc(row_in, 16)

            def group(q, n, nxt):
                if nxt:
                    sp.wait_ge(res_set, q + 1)
                    load(q + 1, nxt)
                sp.wait_ge(y_added, q * X + X + 2)
                if n == 2:
                    sp.dma_start(out[bass.ds(q * TOK, TOK), :].rearrange("(t p) d -> p t d", p=P), res[:, :, :]).then_inc(out_done, 16)
                else:
                    sp.dma_start(out[N - TAIL:N, :], res[0:TAIL, 0, :]).then_inc(out_done, 16)
                sp.wait_ge(out_done, (q + 1) * 16)
                sp.sem_inc(res_free, 1)

            sp.sem_inc(res_free, 1)
            groups(sp, group)

        @block.scalar
        def _(act):
            act.sem_inc(relu_done, 2)
            act.dma_start(wg_f[:, :, :], Wg.rearrange("(k p) e -> p k e", p=P)).then_inc(small_in, 16)
            with nc.allow_non_contiguous_dma(reason="bias of each hidden unit on its partition"):
                act.dma_start(b1_s[:, :, :], b1.rearrange("e (c p) -> p e c", p=P)).then_inc(small_in, 16)
            act.dma_start(b2_s[:, :], b2).then_inc(small_in, 16)
            act.dma_start(gb_row[:, 0:X], bg.rearrange("(a e) -> a e", a=1)).then_inc(small_in, 16)
            act.dma_start(gb_row[:, X:2 * X], bias.rearrange("(a e) -> a e", a=1)).then_inc(small_in, 16)
            act.dma_start(r_in[:, :, :], rows_dram[0:TOK, :].rearrange("(t p) d -> p t d", p=P)).then_inc(row_in, 16)
            for n in range(2 * X):
                act.wait_ge(w_in[n % 2], 16 * (n // 2 + 1))
                if n < X:
                    to = w1[0][:, n % X, :, :].rearrange("p k h -> p (k h)")
                else:
                    to = w2[0][:, n % X, :, :].rearrange("p c d -> p (c d)")
                act.copy(to, hf[n % 2][:, :, :].rearrange("p c t -> p (c t)")).then_inc(hi_done, 1)

            def deviation(q, n):
                act.wait_ge(var_done, q + 1)
                act.activation(dev[:, 0:n], mv[:, 0:n, 1], ACT.Sqrt, bias=eps[:, 0:1], scale=1.0).then_inc(dev_done, 1)

            def high_z(q, n):
                act.wait_ge(z_turned, q + 1)
                src = turn_ps[:, :].rearrange("p (k t) -> p k t", k=2)[:, :, 0:n * P]
                act.copy(zT[0][:, :, 0:n * P], src).then_inc(zh_done, 1)

            def exponent(q, n):
                act.wait_ge(gap_done, q + 1)
                act.activation(ex[:, 0:n], gap[:, 0:n], ACT.Exp).then_inc(ex_done, 1)

            def relu(q, e, n):
                act.wait_ge(hid, q * X + e + 1)
                act.wait_ge(split_done, q * X + e + 1)
                for c in range(FC):
                    ins = act.activation(hf[e % 2][:, c, 0:n * P], hid_ps(e, c)[:, 0:n * P], ACT.Relu, bias=b1_s[:, e, c:c + 1])
                ins.then_inc(relu_done, 1)

            def group(q, n, nxt):
                for e in range(X):
                    if e == 4 and nxt:
                        deviation(q + 1, nxt)
                    if e == X - 1 and nxt:
                        act.wait_ge(hid, q * X + X)
                        high_z(q + 1, nxt)
                    relu(q, e, n)
                if nxt:
                    exponent(q + 1, nxt)

            deviation(0, 2)
            high_z(0, 2)
            exponent(0, 2)
            groups(act, group)

        @block.tensor
        def _(pe):
            pe.sem_inc(y_made, 2)
            pe.wait_ge(small_in, 16 * 5)
            pe.matmul(small_ps[:, 0:2 * X], ones_row[:, :], gb_row[:, :], start=True, stop=True).then_inc(gb_ps, 1)

            THREE = ((0, 0), (0, 1), (1, 0))

            def turn(q, n):
                pe.wait_ge(z_done, q + 1)
                for t in range(n):
                    for k in range(2):
                        tr = pe.transpose(turn_ps[:, k * TOK + t * P:k * TOK + (t + 1) * P], z[:, t, k * P:(k + 1) * P], ident[:, :])
                tr.then_inc(z_turned, 1)

            def logit(q, n):
                pe.wait_ge(zh_done, q + 1)
                pe.wait_ge(zl_done, q + 1)
                for t in range(n):
                    m = 0
                    for k in range(2):
                        for a, b in THREE:
                            mm = pe.matmul(small_ps[:, t * X:(t + 1) * X], zT[a][:, k, t * P:(t + 1) * P], wg[b][:, k, :], start=(m == 0), stop=(m == 5))
                            m += 1
                mm.then_inc(logit_ps, 1)

            def turn_gate(q, n):
                pe.wait_ge(gate_done, q + 1)
                for t in range(n):
                    tr = pe.transpose(small_ps[0:X, t * P:(t + 1) * P], gate[:, t, :], ident[:, :])
                tr.then_inc(gateT_ps, 1)

            def shifts(q, n):
                pe.wait_ge(gateT_done, q + 1)
                for t in range(n):
                    mm = pe.matmul(small_ps[:, t * D:(t + 1) * D], gateT[:, t, :], b2_s[:, :], start=True, stop=True)
                mm.then_inc(shift_ps, 1)

            def hidden(q, e, n):
                pe.wait_ge(relu_done, q * X + e + 1)
                for c in range(FC):
                    m = 0
                    for k in range(2):
                        for a, b in THREE:
                            mm = pe.matmul(hid_ps(e, c)[:, 0:n * P], w1[a][:, e, k, c * P:(c + 1) * P], zT[b][:, k, 0:n * P],
                                           start=(m == 0), stop=(m == 5))
                            m += 1
                mm.then_inc(hid, 1)

            def second(q, e, n):
                pe.wait_ge(split_done, q * X + e + 3)
                pe.wait_ge(y_added, q * X + e + 1)
                parts = (hh, hl)
                for t in range(n):
                    m = 0
                    for c in range(FC):
                        for a, b in THREE:
                            mm = pe.matmul(y_ps[e % 2][:, t * D:(t + 1) * D], parts[a][e % 2][:, c, t * P:(t + 1) * P], w2[b][:, e, c, :],
                                           start=(m == 0), stop=(m == 3 * FC - 1))
                            m += 1
                mm.then_inc(y_made, 1)

            def group(q, n, nxt):
                hidden(q, 0, n)
                turn_gate(q, n)
                hidden(q, 1, n)
                shifts(q, n)
                second(q, 0, n)
                for e in range(2, X):
                    hidden(q, e, n)
                    second(q, e - 1, n)
                    if e == 5 and nxt:
                        turn(q + 1, nxt)
                if nxt:
                    logit(q + 1, nxt)
                second(q, X - 1, n)

            turn(0, 2)
            pe.wait_ge(w_ready, 1)
            logit(0, 2)
            groups(pe, group)

        @block.vector
        def _(dve):
            dve.memset(eps[:, :], EPS)
            dve.sem_inc(y_added, 2)
            dve.sem_inc(split_done, 2)
            links = [0]

            def link(q, ins):
                links[0] += 1
                ins.then_inc(chain, 1)
                dve.wait_ge(chain, q * LINKS + links[0])

            def statistics(q, n):
                links[0] = 0
                dve.wait_ge(row_in, (q + 1) * 16)
                for t in range(n):
                    ins = dve.bn_stats(stats[:, t, :], r_in[:, t, :])
                link(q, ins)
                dve.sem_inc(passed, 1)
                for t in range(n):
                    ins = dve.bn_aggr(mv[:, t, :], stats[:, t, :])
                ins.then_inc(var_done, 1)

            def normalize(q, n):
                dve.wait_ge(dev_done, q + 1)
                link(q, dve.reciprocal(rstd[:, 0:n], dev[:, 0:n]))
                for t in range(n):
                    ins = dve.tensor_scalar(z[:, t, :], r_in[:, t, :], mv[:, t, 0:1], rstd[:, t:t + 1], ALU.subtract, ALU.mult)
                ins.then_inc(z_done, 1)

            def low_z(q, n):
                dve.wait_ge(zh_done, q + 1)
                src = turn_ps[:, :].rearrange("p (k t) -> p k t", k=2)[:, :, 0:n * P]
                dve.tensor_tensor(zT[1][:, :, 0:n * P], src, zT[0][:, :, 0:n * P].bitcast(F32), ALU.subtract).then_inc(zl_done, 1)

            def gates(q, n):
                dve.wait_ge(logit_ps, q + 1)
                for t in range(n):
                    ins = dve.tensor_tensor(logits[:, t, :], small_ps[:, t * X:(t + 1) * X], gb[:, :], ALU.add)
                link(q, ins)
                dve.sem_inc(passed, 1)
                for t in range(n):
                    ins = dve.max(best[:, t, :], logits[:, t, :])
                link(q, ins)
                dve.sem_inc(passed, 1)
                for t in range(n):
                    dve.max_index(where[:, t, :], best[:, t, :], logits[:, t, :])
                dve.tensor_tensor(gap[:, 0:n], best[:, 0:n, 1], best[:, 0:n, 0], ALU.subtract).then_inc(gap_done, 1)
                dve.wait_ge(ex_done, q + 1)
                link(q, dve.tensor_copy(where_f[:, 0:n, :], where[:, 0:n, 0:2]))
                link(q, dve.tensor_scalar(den[:, 0:n], ex[:, 0:n], 1.0, None, ALU.add))
                link(q, dve.reciprocal(share[:, 0:n, 0], den[:, 0:n]))
                link(q, dve.tensor_tensor(share[:, 0:n, 1], ex[:, 0:n], share[:, 0:n, 0], ALU.mult))
                for s, to in enumerate((gate_a, gate)):
                    for t in range(n):
                        ins = dve.tensor_scalar(to[:, t, :], iota[:, 0:X], where_f[:, t, s:s + 1], share[:, t, s:s + 1], ALU.is_equal, ALU.mult)
                link(q, ins)
                link(q, dve.tensor_tensor(gate[:, 0:n, :], gate[:, 0:n, :], gate_a[:, 0:n, :], ALU.add))
                assert links[0] == LINKS, links[0]
                dve.sem_inc(gate_done, 1)

            def take_gateT(q, n):
                dve.wait_ge(gateT_ps, q + 1)
                dve.tensor_copy(gateT[:, 0:n, :], small_ps[0:X, 0:n * P].rearrange("p (t c) -> p t c", t=n)).then_inc(gateT_done, 1)

            def set_res(q, n):
                dve.wait_ge(shift_ps, q + 1)
                dve.wait_ge(res_free, q + 1)
                dve.tensor_tensor(res[:, 0:n, :], r_in[:, 0:n, :], small_ps[:, 0:n * D].rearrange("p (t d) -> p t d", t=n), ALU.add).then_inc(res_set, 1)

            def split(q, e, n):
                dve.wait_ge(relu_done, q * X + e + 3)
                dve.wait_ge(y_made, q * X + e + 1)
                dve.tensor_copy(hh[e % 2][:, :, 0:n * P], hf[e % 2][:, :, 0:n * P]).then_inc(half_done, 1)
                dve.wait_ge(half_done, q * X + e + 1)
                dve.tensor_tensor(hl[e % 2][:, :, 0:n * P], hf[e % 2][:, :, 0:n * P], hh[e % 2][:, :, 0:n * P].bitcast(F32), ALU.subtract).then_inc(split_done, 1)

            def add(q, e, n):
                dve.wait_ge(y_added, q * X + e + 2) if e else dve.wait_ge(res_set, q + 1)
                dve.wait_ge(y_made, q * X + e + 3)
                for t in range(n):
                    ins = dve.scalar_tensor_tensor(out=res[:, t, :], in0=y_ps[e % 2][:, t * D:(t + 1) * D], scalar=gate[:, t, e:e + 1],
                                                   in1=res[:, t, :], op0=ALU.mult, op1=ALU.add)
                ins.then_inc(y_added, 1)

            def group(q, n, nxt):
                take_gateT(q, n)
                split(q, 0, n)
                split(q, 1, n)
                set_res(q, n)
                add(q, 0, n)
                for e in range(2, X):
                    split(q, e, n)
                    add(q, e - 1, n)
                    if e == 3 and nxt:
                        statistics(q + 1, nxt)
                    if e == 4 and nxt:
                        normalize(q + 1, nxt)
                if nxt:
                    low_z(q + 1, nxt)
                add(q, X - 1, n)
                if nxt:
                    gates(q + 1, nxt)

            statistics(0, 2)
            for n in range(2 * X):
                dve.wait_ge(hi_done, n + 1)
                if n < X:
                    hi, lo = (w1[i][:, n % X, :, :].rearrange("p k h -> p (k h)") for i in range(2))
                else:
                    hi, lo = (w2[i][:, n % X, :, :].rearrange("p c d -> p (c d)") for i in range(2))
                dve.tensor_tensor(lo, hf[n % 2][:, :, :].rearrange("p c t -> p (c t)"), hi.bitcast(F32), ALU.subtract).then_inc(w_split, 1)
            dve.wait_ge(small_in, 16 * 5)
            dve.tensor_copy(wg[0][:, :, :], wg_f[:, :, :]).then_inc(w_split, 1)
            dve.wait_ge(w_split, 2 * X + 1)
            dve.tensor_tensor(wg[1][:, :, :], wg_f[:, :, :], wg[0][:, :, :].bitcast(F32), ALU.subtract)
            dve.wait_ge(gb_ps, 1)
            dve.tensor_copy(gb[:, :], small_ps[:, 0:X]).then_inc(w_split, 1)
            dve.wait_ge(w_split, 2 * X + 2)
            dve.tensor_tensor(gb[:, :], gb[:, :], small_ps[:, X:2 * X], ALU.add).then_inc(w_ready, 1)
            normalize(0, 2)
            low_z(0, 2)
            gates(0, 2)
            groups(dve, group)


_INS = ['x', 'src', 'dst', 'edge_weight', 'node_vec1', 'L0_mix_wq', 'L0_mix_wk', 'L0_mix_wv', 'L0_mix_wo', 'L0_mix_bo',
        'L0_mix_ln_k_g', 'L0_mix_ln_k_b', 'L0_mix_ln_v_g', 'L0_mix_ln_v_b', 'L0_ffn_Wg', 'L0_ffn_bg', 'L0_ffn_bias',
        'L0_ffn_W1', 'L0_ffn_b1', 'L0_ffn_W2', 'L0_ffn_b2']
_OUTS = [((6250, 256), 'float32')]


def kernel(**inputs):
    import numpy as _np
    import concourse.bacc as _bacc
    from concourse import mybir as _mybir
    from concourse.bass_utils import run_bass_kernel_spmd as _run

    nc = _bacc.Bacc("TRN2", target_bir_lowering=False, num_devices=1)
    arrays, args = {}, []
    for name in _INS:
        a = _np.ascontiguousarray(inputs[name])
        arrays[f"in_{name}_dram"] = a
        args.append(nc.dram_tensor(f"in_{name}_dram", a.shape, _mybir.dt.from_np(a.dtype), kind="ExternalInput").ap())
    for i, (shape, dtype) in enumerate(_OUTS):
        dt = _mybir.dt.from_np(_np.dtype(dtype))
        args.append(nc.dram_tensor(f"out_{i}_dram", shape, dt, kind="ExternalOutput").ap())
    gps_layer(nc, *args)
    r = _run(nc, [arrays], core_ids=[0])
    got = tuple(r.results[0][f"out_{i}_dram"] for i in range(len(_OUTS)))
    return got[0]
```

```python
from contextlib import ExitStack

import numpy as np

import concourse.bass as bass
from concourse import mybir

P = 128
F32 = mybir.dt.float32
F32R = mybir.dt.float32r
I32 = mybir.dt.int32
BF16 = mybir.dt.bfloat16
ALU = mybir.AluOpType
ACT = mybir.ActivationFunctionType
AX = mybir.AxisListType
EPS = 1e-5

CH = 28
SW = CH + 2
GRP = 8
BU = 6
NB = 50
RUN = 6
UNROLL = 7
FIELDS = 5
SRC, DST, W = 0, 1, 2


def gps_layer(nc, x, src, dst, edge_weight, node_vec1, wq, wk, wv, wo, bo, kg, kb, vg, vb,
         Wg, bg, bias, W1, b1, W2, b2, out):
    N, D = x.shape
    E = src.shape[0]
    SC = CH * P
    G = -(-E // SC)
    NT = -(-N // P)
    TAIL = N - (NT - 1) * P
    NG = G // GRP
    assert D == 2 * P and G == NG * GRP and NT == GRP * BU + 1 and NG % 2 == 1 and NB == NT + 1
    HD = kg.shape[0]
    H = D // HD
    FULL = E - (G - 1) * SC
    TP = FULL // CH
    TR = FULL - TP * CH

    xn_dram = nc.dram_tensor("xn_dram", (NT * P, D), F32, kind="Internal").ap()
    rows_dram = nc.dram_tensor("rows_dram", (NT * P, D), F32, kind="Internal").ap()

    with ExitStack() as ctx:
        def sb(name, shape, dt=F32, c=ctx):
            return c.enter_context(nc.sbuf_tensor(name, shape, dt))

        X = Wg.shape[1]
        NJ = (NT * P * 2 + X * (P - 1)) // P
        disp_dram = nc.dram_tensor("disp_dram", (NJ * P, D), F32, kind="Internal").ap()
        y_dram = nc.dram_tensor("y_dram", (NJ * P, D), F32, kind="Internal").ap()
        bias_dram = nc.dram_tensor("bias_dram", (3, X * (W1.shape[2] + D)), BF16, kind="Internal").ap()

        ident = sb("ident", [P, P])
        iota = sb("iota", [P, P])
        ones_row = sb("ones_row", [1, P])
        before = sb("before", [P, P], BF16)
        zeros = sb("zeros", [P, D])
        share = sb("share", [P, NT, 2])
        slot = sb("place", [P, NT, 2], I32)
        tile_e = sb("tile_e", [1, (NJ - 3) // RUN + 1], I32)
        x_in = ctx.enter_context(nc.semaphore("x_in"))
        zeroed = ctx.enter_context(nc.semaphore("zeroed"))
        banks = [ctx.enter_context(nc.psum_tensor(f"bank{i}", [P, 512], F32)) for i in range(8)]
        with ExitStack() as c1:
            acc = sb("acc", [P, NT, D], F32, c1)
            with ExitStack() as c2:
                iota1_c = sb("iota1_c", [P, P, CH], BF16, c2)
                iota_j = sb("iota_j", [P, P, GRP], BF16, c2)
                shared = (banks, acc, ident, iota, iota1_c, iota_j, ones_row, before)
                constants(nc, shared, zeros, NT)
                edges = edge_lists(nc, c2, shared, x, x_in, src, dst, edge_weight, E, G, TP, TR, N, NT, TAIL)
                attention(nc, shared, x_in, node_vec1, wq, wk, wv, wo, bo, kg, kb, vg, vb, xn_dram, NT, TAIL, N, D, H, HD)
                edge_sum(nc, shared, edges, xn_dram, zeros, disp_dram, zeroed, G, NG, NT, NJ, D)
                stragglers(nc, shared, edges, src, dst, edge_weight, xn_dram, E, G, TP, TR, NT, D)
            route(nc, shared, share, slot, tile_e, zeroed, rows_dram, disp_dram, bias_dram, Wg, bg, bias, b1, b2, NT, NJ, D)
        experts(nc, banks, ident, tile_e, disp_dram, y_dram, bias_dram, W1, W2, NJ, D)
        combine(nc, share, slot, rows_dram, y_dram, out, NT, TAIL, N, D)


def constants(nc, shared, zeros, NT):
    banks, acc, ident, iota, iota1_c, iota_j, ones_row, before = shared
    with ExitStack() as ctx:
        ints = ctx.enter_context(nc.sbuf_tensor("ints", [P, 2, P], I32))
        iota_done = ctx.enter_context(nc.semaphore("iota_done"))
        cast_done = ctx.enter_context(nc.semaphore("cast_done"))
        block = ctx.enter_context(nc.Block())

        @block.gpsimd
        def _(pool):
            pool.memset(zeros[:, :], 0.0)
            pool.memset(acc[:, NT - 1, :], 0.0)
            pool.iota(ints[:, 0, :], [[1, P]], base=0, channel_multiplier=0).then_inc(iota_done, 1)
            pool.iota(ints[:, 1, :], [[1, P]], base=0, channel_multiplier=-1).then_inc(iota_done, 1)

        @block.vector
        def _(dve):
            dve.memset(ones_row[:, :], 1.0)
            dve.wait_ge(iota_done, 2)
            dve.tensor_copy(iota[:, :], ints[:, 0, :]).then_inc(cast_done, 1)
            dve.tensor_scalar(ident[:, :], ints[:, 1, :], 0.0, None, ALU.is_equal)
            dve.tensor_scalar(before[:, :], ints[:, 1, :], 0.0, None, ALU.is_gt)
            dve.wait_ge(cast_done, 1)
            dve.tensor_copy(iota_j[:, :, :], iota[:, :].unsqueeze(2).broadcast_to([P, P, GRP]))
            dve.tensor_scalar(iota1_c[:, :, :], iota[:, :].unsqueeze(2).broadcast_to([P, P, CH]), 1.0, None, ALU.add)


def edge_lists(nc, keep, shared, x, x_in, src, dst, edge_weight, E, G, TP, TR, N, NT, TAIL):
    banks, acc, ident, iota, iota1_c, iota_j, ones_row, before = shared
    SC = CH * P

    def kb(name, shape, dt=F32):
        return keep.enter_context(nc.sbuf_tensor(name, shape, dt))

    tile1 = kb("tile1", [P, G + 1, CH], BF16)
    fields = kb("fields", [P, FIELDS, G + 1, CH], BF16)
    inside = kb("inside", [P, G, CH], BF16)
    left = kb("left", [P, G, CH], BF16)
    n_left = kb("n_left", [P, G])
    rows_i = kb("rows_i", [P, G], I32)
    with ExitStack() as ctx:
        def sb(name, shape, dt=F32):
            return ctx.enter_context(nc.sbuf_tensor(name, shape, dt))

        dst_i = sb("dst_i", [P, G, CH], I32)
        weight = sb("weight", [P, G, CH])
        bucket = sb("bucket", [P, G, CH])
        src_i = sb("src_i", [P, G, CH], I32)
        tmp_i = sb("tmp_i", [P, G, CH], I32)
        off = sb("off", [P, G, CH])
        first_i = sb("first_i", [1, G], I32)
        first = sb("first", [1, G])
        start = sb("start", [P, G])
        lane_i = sb("lane_i", [P, 1], I32)
        lane = sb("lane", [P, 1])
        padded = ctx.enter_context(nc.semaphore("padded"))
        loaded = ctx.enter_context(nc.semaphore("loaded"))
        lane_done = ctx.enter_context(nc.semaphore("lane_done"))
        first_done = ctx.enter_context(nc.semaphore("first_done"))
        start_done = ctx.enter_context(nc.semaphore("start_done"))
        step = ctx.enter_context(nc.semaphore("step"))
        block = ctx.enter_context(nc.Block())
        NL = 3 * 3 + 1

        @block.sync
        def _(sp):
            sp.wait_ge(padded, 3)
            for arr, to in ((dst, dst_i), (src, src_i), (edge_weight, weight)):
                body = arr[0:(G - 1) * SC].rearrange("(g p c) -> p g c", p=P, c=CH)
                sp.dma_start(to[:, 0:G - 1, :], body).then_inc(loaded, 16)
                tail = arr[(G - 1) * SC:(G - 1) * SC + TP * CH].rearrange("(p c) -> p c", c=CH)
                sp.dma_start(to[0:TP, G - 1, :], tail).then_inc(loaded, 16)
                rest = arr[E - TR:E].rearrange("(a c) -> a c", a=1)
                sp.dma_start(to[TP:TP + 1, G - 1, 0:TR], rest).then_inc(loaded, 16)
            with nc.allow_non_contiguous_dma(reason="one element per superchunk"):
                sp.dma_start(first_i[0:1, 0:G - 1], dst[0:(G - 1) * SC].rearrange("(a g s) -> a g s", a=1, s=SC)[:, :, 0]).then_inc(loaded, 16)
                sp.dma_start(first_i[0:1, G - 1:G], dst[(G - 1) * SC:(G - 1) * SC + 1].rearrange("(a b) -> a b", a=1)).then_inc(loaded, 16)
            LAST = NT - 1
            sp.dma_start(acc[0:TAIL, LAST, :], x[LAST * P:N, :]).then_inc(x_in, 16)
            sp.dma_start(acc[:, 0:LAST, :], x[0:LAST * P, :].rearrange("(t p) d -> p t d", p=P)).then_inc(x_in, 16)

        @block.gpsimd
        def _(pool):
            pool.iota(lane_i[:, :], [[0, 1]], base=0, channel_multiplier=1).then_inc(lane_done, 1)

        @block.tensor
        def _(pe):
            pe.wait_ge(first_done, 1)
            pe.matmul(banks[0][:, 0:G], ones_row[:, :], first[:, :], start=True, stop=True).then_inc(start_done, 1)

        @block.vector
        def _(dve):
            n = [0]

            def then(ins):
                n[0] += 1
                ins.then_inc(step, 1)
                dve.wait_ge(step, n[0])

            dve.memset(src_i[:, G - 1, :], NB * P).then_inc(padded, 1)
            dve.memset(dst_i[:, G - 1, :], 0).then_inc(padded, 1)
            dve.memset(weight[:, G - 1, :], 0.0).then_inc(padded, 1)
            dve.memset(tile1[:, G, :], 0.0)
            dve.memset(fields[:, :, G, :], 0.0)
            dve.wait_ge(loaded, 16 * (NL + 1))
            dve.tensor_scalar(first[:, :], first_i[:, :], float(N - P), None, ALU.min).then_inc(first_done, 1)
            then(dve.tensor_scalar(tmp_i[:, :, :], src_i[:, :, :], 7, None, ALU.logical_shift_right))
            then(dve.tensor_copy(bucket[:, :, :], tmp_i[:, :, :]))
            then(dve.tensor_scalar(tmp_i[:, :, :], src_i[:, :, :], P - 1, None, ALU.bitwise_and))
            dve.tensor_copy(fields[:, SRC, 0:G, :], tmp_i[:, :, :])
            dve.tensor_scalar(tile1[:, 0:G, :], bucket[:, :, :], 1.0, None, ALU.add)
            for part in range(3):
                then(dve.tensor_copy(fields[:, W + part, 0:G, :], weight[:, :, :]))
                if part < 2:
                    then(dve.tensor_tensor(weight[:, :, :], weight[:, :, :], fields[:, W + part, 0:G, :], ALU.subtract))
            dve.wait_ge(start_done, 1)
            then(dve.tensor_copy(start[:, :], banks[0][:, 0:G]))
            then(dve.tensor_tensor(off[:, :, :], dst_i[:, :, :], start[:, :].unsqueeze(2).broadcast_to([P, G, CH]), ALU.subtract))
            dve.tensor_copy(fields[:, DST, 0:G, :], off[:, :, :])
            then(dve.tensor_scalar(inside[:, :, :], off[:, :, :], 0.0, None, ALU.is_ge))
            then(dve.scalar_tensor_tensor(out=inside[:, :, :], in0=off[:, :, :], scalar=float(P), in1=inside[:, :, :], op0=ALU.is_lt, op1=ALU.mult))
            then(dve.scalar_tensor_tensor(out=inside[:, :, :], in0=bucket[:, :, :], scalar=float(NB), in1=inside[:, :, :], op0=ALU.is_equal, op1=ALU.max))
            dve.wait_ge(lane_done, 1)
            then(dve.tensor_copy(lane[:, :], lane_i[:, :]))
            then(dve.tensor_scalar(rows_i[:, :], start[:, :], lane[:, 0:1], None, ALU.add))
    return tile1, fields, inside, left, n_left, rows_i


def row_statistics(dve, stats, acc, done, NT):
    with dve.Fori(0, NT // UNROLL) as q:
        for i in range(UNROLL):
            t = q * UNROLL + i
            dve.bn_stats(stats[:, bass.ds(t, 1), :].rearrange("p a d -> p (a d)"),
                         acc[:, bass.ds(t, 1), :].rearrange("p a d -> p (a d)")).then_inc(done, 1)
    dve.wait_ge(done, NT)


def merge_stats(dve, then, stats, mv, D):
    even, odd = stats[:, :, 1], stats[:, :, 4]
    then(dve.tensor_tensor(mv[:, 1, :], even, odd, ALU.subtract))
    then(dve.tensor_tensor(mv[:, 1, :], mv[:, 1, :], mv[:, 1, :], ALU.mult))
    then(dve.tensor_scalar(mv[:, 1, :], mv[:, 1, :], D / 4.0, None, ALU.mult))
    then(dve.tensor_tensor(mv[:, 0, :], stats[:, :, 2], stats[:, :, 5], ALU.add))
    then(dve.tensor_tensor(mv[:, 1, :], mv[:, 0, :], mv[:, 1, :], ALU.add))
    then(dve.tensor_scalar(mv[:, 1, :], mv[:, 1, :], 1.0 / D, None, ALU.mult))
    then(dve.tensor_tensor(mv[:, 0, :], even, odd, ALU.add))
    then(dve.tensor_scalar(mv[:, 0, :], mv[:, 0, :], 0.5, None, ALU.mult))


def attention(nc, shared, x_in, node_vec1, wq, wk, wv, wo, bo, kg, kb, vg, vb, xn_dram, NT, TAIL, N, D, H, HD):
    banks, acc, ident, iota, iota1_c, iota_j, ones_row, before = shared
    KV = 2 * D
    HH = 2 * H
    with ExitStack() as ctx:
        def sb(name, shape, dt=F32):
            return ctx.enter_context(nc.sbuf_tensor(name, shape, dt))

        def sem(name):
            return ctx.enter_context(nc.semaphore(name))

        xn = [sb(f"xn{i}", [P, D]) for i in range(2)]
        xT = [sb(f"xT{i}", [P, 2, P]) for i in range(2)]
        xT_all = sb("xT_all", [P, NT, 2, P])
        sq = sb("sq", [P, KV])
        hat = [sb(f"hat{i}", [P, 4, P + 1]) for i in range(2)]
        all_ones = sb("all_ones", [P, P])
        sums = sb("sums", [P, 2, P])
        col = sb("col", [P, 2])
        shift_v = sb("shift_v", [P, 2])
        sv_n = sb("sv_n", [P, 1])
        prod = sb("prod", [P, 2, P])
        w_nat = sb("w_nat", [P, 4, 2, D])
        wkvT = sb("wkvT", [P, 2, KV])
        woT = sb("woT", [P, 2, D])
        vecs = sb("vecs", [1, D + 2 * HD])
        gs_k = sb("gs_k", [P, 2, HD])
        bo_b = sb("bo_b", [P, D])
        nv = sb("nv", [P, NT])
        stats = sb("stats", [P, NT, 6])
        mv = sb("mv", [P, 2, NT])
        rstd = sb("rstd", [P, NT])
        hsum = sb("hsum", [P, 2, HH])
        ss = sb("ss", [P, HH])
        hinv = sb("hinv", [P, HH])
        hvar = sb("hvar", [P, HH])
        power = sb("power", [P, NT])
        kvT = sb("kvT", [P, 2, P])
        R = sb("R", [P, 2, D])
        M = sb("M", [P, 2, D])
        turn_ps, proj_ps, kv_ps, mix_ps = banks[0:2], banks[2:4], banks[4:6], banks[6:8]

        w_in = sem("w_in"); nv_in = sem("nv_in")
        cleared = sem("cleared")
        w_turned = sem("w_turned"); spread = sem("spread"); w_ready = sem("w_ready")
        xn_done = sem("xn_done"); stored = [sem(f"stored{i}") for i in range(2)]
        turned = sem("turned"); xT_done = sem("xT_done"); proj = sem("proj")
        squared = sem("squared"); summed = sem("summed"); hvar_done = sem("hvar_done"); rooted = sem("rooted")
        var_done = sem("var_done"); power_set = sem("power_set"); rstd_done = sem("rstd_done")
        hat_done = sem("hat_done"); kv_used = sem("kv_used")
        kvT_done = sem("kvT_done"); sums_done = sem("sums_done"); sums_made = sem("sums_made"); ones_set = sem("ones_set"); R_made = sem("R_made"); R_done = sem("R_done")
        M_made = sem("M_made"); M_done = sem("M_done"); copied = sem("copied")
        xT_back = sem("xT_back"); mixed = sem("mixed"); added = sem("added")
        step = sem("step"); aggr = sem("aggr")
        block = ctx.enter_context(nc.Block())
        NW = 4 + 3
        NV = 2 + 2 * (P // HD)
        LAST = NT - 1

        def tiles(eng, one):
            one(0, 0)
            with eng.Fori(0, (NT - 3) // 2) as h:
                one(2 * h + 1, 1)
                one(2 * h + 2, 0)
            one(NT - 2, 1)
            one(NT - 1, 0)

        def pairs(eng, one):
            with eng.Fori(0, NT // 2) as h:
                one(2 * h, 0)
                one(2 * h + 1, 1)
            one(NT - 1, 0)

        @block.sync
        def _(sp):
            sp.wait_ge(cleared, 1)
            for i, w in enumerate((wq, wk, wv, wo)):
                sp.dma_start(w_nat[:, i, :, :], w.rearrange("(m p) d -> p m d", p=P)).then_inc(w_in, 16)
            sp.dma_start(vecs[:, 0:D], bo.rearrange("(a d) -> a d", a=1)).then_inc(w_in, 16)
            for i, v in enumerate((kg, kb)):
                sp.dma_start(vecs[:, D + i * HD:D + (i + 1) * HD], v.rearrange("(a d) -> a d", a=1)).then_inc(w_in, 16)
            with nc.allow_non_contiguous_dma(reason="one value per partition"):
                for i, v in enumerate((vg, vb)):
                    for h in range(P // HD):
                        sp.dma_start(col[h * HD:(h + 1) * HD, i:i + 1], v.rearrange("(d a) -> d a", a=1)).then_inc(nv_in, 16)
            with nc.allow_non_contiguous_dma(reason="one value per node"):
                sp.dma_start(nv[:, 0:LAST], node_vec1[0:LAST * P, :].rearrange("(t p) a -> p (t a)", p=P)).then_inc(nv_in, 16)
                sp.dma_start(nv[0:TAIL, LAST:NT], node_vec1[LAST * P:N, :]).then_inc(nv_in, 16)

            def store(t, i):
                sp.wait_ge(xn_done, t + 1)
                sp.dma_start(xn_dram[bass.ds(t * P, P), :], xn[i][:, :]).then_inc(stored[i], 16)

            pairs(sp, store)
            sp.wait_ge(stored[0], 16 * (NT // 2 + 1))
            sp.wait_ge(stored[1], 16 * (NT // 2))

        @block.gpsimd
        def _(pool):
            pool.memset(power[:, :], -0.5).then_inc(power_set, 1)
            pool.wait_ge(power_set, 1)
            pool.wait_ge(var_done, 1)
            pool.tensor_tensor(rstd[:, :], mv[:, 1, :], power[:, :], ALU.pow).then_inc(rstd_done, 1)

            def root(t, i):
                pool.wait_ge(hvar_done, t + 1)
                pool.tensor_tensor(hinv[:, :], hvar[:, :], power[:, 0:HH], ALU.pow).then_inc(rooted, 1)

            pairs(pool, root)

        @block.scalar
        def _(act):
            act.sem_inc(xT_done, 2)

            def take_xT(t, i):
                act.wait_ge(turned, t + 3)
                act.wait_ge(proj, t + 1)
                act.copy(xT[i][:, :, :], turn_ps[i][:, 0:2 * P].rearrange("p (k c) -> p k c", k=2)).then_inc(xT_done, 1)
                act.wait_ge(xT_done, t + 3)
                act.copy(xT_all[:, bass.ds(t, 1), :, :].rearrange("p a k c -> p (a k) c"), xT[i][:, :, :]).then_inc(copied, 1)

            def heads(t, i):
                act.wait_ge(proj, t + 3)
                act.wait_ge(summed, t + 1)
                act.activation(sq[:, :], proj_ps[i][:, :], ACT.Square).then_inc(squared, 1)

            def one(t, i):
                if not isinstance(t, int) or t + 1 < NT:
                    heads(t + 1, 1 - i)
                if not isinstance(t, int) or t + 2 < NT:
                    take_xT(t + 2, i)

            take_xT(0, 0)
            take_xT(1, 1)
            heads(0, 0)
            tiles(act, one)

            def give_xT(t, i):
                act.wait_ge(mixed, t + 1)
                act.copy(xT[i][:, :, :], xT_all[:, bass.ds(t, 1), :, :].rearrange("p a k c -> p (a k) c")).then_inc(xT_back, 1)

            act.wait_ge(copied, NT)
            act.wait_ge(proj, NT + 2)
            pairs(act, give_xT)

        @block.tensor
        def _(pe):
            pe.wait_ge(ones_set, 3)
            pe.sem_inc(turned, 2)
            pe.sem_inc(proj, 2)
            pe.sem_inc(kv_used, 2)
            pe.sem_inc(mixed, 2)
            pe.wait_ge(w_in, 16 * NW)
            pe.matmul(turn_ps[0][:, 0:D + 2 * HD], ones_row[:, :], vecs[:, :], start=True, stop=True).then_inc(spread, 1)
            for k in range(2):
                for m in range(2):
                    pe.transpose(kv_ps[k][:, m * P:(m + 1) * P], w_nat[:, 3, m, k * P:(k + 1) * P], ident[:, :])
                for w in range(2):
                    for m in range(2):
                        last = pe.transpose(mix_ps[k][:, w * D + m * P:w * D + (m + 1) * P],
                                            w_nat[:, 1 + w, m, k * P:(k + 1) * P], ident[:, :])
            last.then_inc(w_turned, 1)
            pe.wait_ge(w_ready, 1)

            def turn(t, i):
                pe.wait_ge(xn_done, t + 1)
                pe.wait_ge(xT_done, t + 1)
                for k in range(2):
                    tr = pe.transpose(turn_ps[i][:, k * P:(k + 1) * P], xn[i][:, k * P:(k + 1) * P], ident[:, :])
                tr.then_inc(turned, 1)

            def project(t, i):
                pe.wait_ge(xT_done, t + 3)
                pe.wait_ge(hat_done, t + 1)
                for k in range(2):
                    mm = pe.matmul(proj_ps[i][:, :], xT[i][:, k, :], wkvT[:, k, :], start=(k == 0), stop=(k == 1))
                mm.then_inc(proj, 1)

            def kv_product(t, i, rows):
                pe.wait_ge(hat_done, t + 3)
                first = isinstance(t, int) and t == 0
                final = isinstance(t, int) and t == LAST
                for c in range(2):
                    pe.matmul(kv_ps[c][:, 0:P + 1], hat[i][0:rows, 2 + c, 0:P], hat[i][0:rows, c, :],
                              start=first, stop=final, skip_group_check=True)
                    mm = pe.matmul(mix_ps[c][:, 0:1], hat[i][0:rows, c, 0:P], hat[i][0:rows, c, P:P + 1],
                                   start=first, stop=final, skip_group_check=True)
                mm.then_inc(kv_used, 1)

            def one(t, i):
                fixed = isinstance(t, int)
                if not fixed or t + 1 < NT:
                    project(t + 1, 1 - i)
                if not fixed or t + 2 < NT:
                    turn(t + 2, i)
                if not fixed or t > 0:
                    kv_product(t - 1, 1 - i, P)

            turn(0, 0)
            turn(1, 1)
            project(0, 0)
            one(0, 0)
            one(1, 1)
            with pe.Fori(0, (NT - 5) // 2) as h:
                one(2 * h + 2, 0)
                one(2 * h + 3, 1)
            one(NT - 3, 0)
            one(NT - 2, 1)
            one(NT - 1, 0)
            kv_product(LAST, 0, TAIL)

            pe.wait_ge(sums_done, 1)
            for c in range(2):
                mm = pe.matmul(proj_ps[c][:, 0:P], all_ones[:, :], sums[:, c, :], start=True, stop=True)
            mm.then_inc(sums_made, 1)
            pe.wait_ge(kvT_done, 1)
            for c in range(2):
                mm = pe.matmul(mix_ps[c][:, 0:D], kvT[:, c, :], woT[:, c, :], start=True, stop=True)
            mm.then_inc(R_made, 1)
            pe.wait_ge(R_done, 1)
            for m in range(2):
                for c in range(2):
                    mm = pe.matmul(proj_ps[m][:, 0:D], w_nat[:, 0, c, m * P:(m + 1) * P], R[:, c, :], start=(c == 0), stop=(c == 1))
            mm.then_inc(M_made, 1)
            pe.wait_ge(M_done, 1)

            def mix(t, i):
                pe.wait_ge(xT_back, t + 1)
                pe.wait_ge(added, t + 1)
                for k in range(2):
                    mm = pe.matmul(mix_ps[i][:, 0:D], xT[i][:, k, :], M[:, k, :], start=(k == 0), stop=(k == 1))
                mm.then_inc(mixed, 1)

            pairs(pe, mix)

        @block.vector
        def _(dve):
            n = [0]

            def then(ins):
                n[0] += 1
                ins.then_inc(step, 1)
                dve.wait_ge(step, n[0])

            dve.sem_inc(hat_done, 2)
            dve.memset(all_ones[:, :], 1.0).then_inc(ones_set, 1)
            for i in range(2):
                dve.memset(hat[i][:, :, P:P + 1], 1.0).then_inc(ones_set, 1)
            dve.sem_inc(summed, 1)
            dve.sem_inc(added, 2)
            dve.memset(nv[:, LAST:NT], 0.0).then_inc(cleared, 1)
            then(dve.memset(kvT[:, :, :], 0.0))
            dve.wait_ge(w_turned, 1)
            for k in range(2):
                heads = mix_ps[k][:, :].rearrange("p (h d) -> p h d", d=HD)
                then(dve.tensor_reduce(hsum[:, k, :], heads, AX.X, ALU.add))
                then(dve.tensor_scalar(hsum[:, k, :], hsum[:, k, :], 1.0 / HD, None, ALU.mult))
                then(dve.tensor_tensor(wkvT[:, k, :].rearrange("p (h d) -> p h d", d=HD), heads,
                                       hsum[:, k, :].unsqueeze(2).broadcast_to([P, HH, HD]), ALU.subtract))
                then(dve.tensor_copy(woT[:, k, :], kv_ps[k][:, 0:D]))
            dve.wait_ge(spread, 1)
            dve.tensor_copy(gs_k[:, :, :].rearrange("p s d -> p (s d)"), turn_ps[0][:, D:D + 2 * HD])
            then(dve.tensor_copy(bo_b[:, :], turn_ps[0][:, 0:D]))
            dve.wait_ge(x_in, 32)
            row_statistics(dve, stats, acc, aggr, NT)
            merge_stats(dve, then, stats, mv, D)
            dve.tensor_scalar(mv[:, 1, :], mv[:, 1, :], EPS, None, ALU.add).then_inc(var_done, 1)
            dve.wait_ge(rstd_done, 1)
            dve.wait_ge(nv_in, 16 * NV)
            dve.sem_inc(w_ready, 1)

            def normalize(t, i, before):
                row = acc[:, bass.ds(t, 1), :].rearrange("p a d -> p (a d)")
                if before is not None:
                    dve.wait_ge(stored[i], 16 * before)
                dve.wait_ge(turned, t + 1)
                dve.tensor_scalar(xn[i][:, :], row, mv[:, 0, bass.ds(t, 1)], rstd[:, bass.ds(t, 1)],
                                  ALU.subtract, ALU.mult).then_inc(xn_done, 1)
                dve.scalar_tensor_tensor(out=row, in0=row, scalar=nv[:, bass.ds(t, 1)], in1=bo_b[:, :], op0=ALU.add, op1=ALU.add)

            def one(t, i, turn):
                dve.wait_ge(squared, t + 1)
                dve.tensor_reduce(ss[:, :], sq[:, :].rearrange("p (h d) -> p h d", d=HD), AX.X, ALU.add).then_inc(summed, 1)
                dve.wait_ge(summed, t + 2)
                dve.tensor_scalar(hvar[:, :], ss[:, :], 1.0 / HD, EPS, ALU.mult, ALU.add).then_inc(hvar_done, 1)
                if not isinstance(t, int) or t + 2 < NT:
                    normalize(t + 2, i, turn)
                dve.wait_ge(rooted, t + 1)
                dve.wait_ge(kv_used, t + 1)
                dve.tensor_tensor(hat[i][:, :, 0:P].rearrange("p b (h d) -> p b h d", d=HD),
                                  proj_ps[i][:, :].rearrange("p (b h d) -> p b h d", b=4, d=HD),
                                  hinv[:, :].rearrange("p (b h) -> p b h", b=4).unsqueeze(3).broadcast_to([P, 4, HH // 4, HD]),
                                  ALU.mult).then_inc(hat_done, 1)

            normalize(0, 0, None)
            normalize(1, 1, None)
            one(0, 0, 1)
            with dve.Fori(0, (NT - 3) // 2) as h:
                one(2 * h + 1, 1, h + 1)
                one(2 * h + 2, 0, h + 2)
            one(NT - 2, 1, None)
            one(NT - 1, 0, None)

            dve.wait_ge(kv_used, NT + 2)
            for c in range(2):
                ins = dve.tensor_scalar(sums[:, c, :], ident[:, :], mix_ps[c][:, 0:1], None, ALU.mult)
            ins.then_inc(sums_done, 1)
            then(dve.tensor_scalar(sv_n[:, :], col[:, 1:2], float(N), None, ALU.mult))
            for c in range(2):
                then(dve.scalar_tensor_tensor(out=shift_v[:, c:c + 1], in0=kv_ps[c][:, P:P + 1], scalar=col[:, 0:1], in1=sv_n[:, :], op0=ALU.mult, op1=ALU.add))
                then(dve.tensor_scalar(prod[:, c, :], kv_ps[c][:, 0:P], col[:, 0:1], None, ALU.mult))
            dve.wait_ge(sums_made, 1)
            gk, sk = (gs_k[:, j, :].unsqueeze(1).broadcast_to([P, P // HD, HD]) for j in range(2))
            for c in range(2):
                heads = prod[:, c, :].rearrange("p (h d) -> p h d", d=HD)
                then(dve.scalar_tensor_tensor(out=prod[:, c, :], in0=proj_ps[c][:, 0:P], scalar=col[:, 1:2], in1=prod[:, c, :], op0=ALU.mult, op1=ALU.add))
                then(dve.tensor_tensor(heads, heads, gk, ALU.mult))
                then(dve.scalar_tensor_tensor(out=heads, in0=sk, scalar=shift_v[:, c:c + 1], in1=heads, op0=ALU.mult, op1=ALU.add))
                for h in range(2):
                    part = slice(h * HD, (h + 1) * HD)
                    last = dve.tensor_scalar(kvT[part, c, part], prod[part, c, part], 1.0 / N, None, ALU.mult)
            last.then_inc(kvT_done, 1)
            dve.wait_ge(R_made, 1)
            dve.tensor_copy(R[:, 0, :], mix_ps[0][:, 0:D])
            dve.tensor_copy(R[:, 1, :], mix_ps[1][:, 0:D]).then_inc(R_done, 1)
            dve.wait_ge(M_made, 1)
            dve.tensor_copy(M[:, 0, :], proj_ps[0][:, 0:D])
            dve.tensor_copy(M[:, 1, :], proj_ps[1][:, 0:D]).then_inc(M_done, 1)

            def add(t, i):
                row = acc[:, bass.ds(t, 1), :].rearrange("p a d -> p (a d)")
                dve.wait_ge(mixed, t + 3)
                dve.tensor_tensor(row, row, mix_ps[i][:, 0:D], ALU.add).then_inc(added, 1)

            pairs(dve, add)


def edge_sum(nc, shared, edges, xn_dram, zeros, disp_dram, zeroed, G, NG, NT, NJ, D):
    banks, acc, ident, iota, iota1_c, iota_j, ones_row, before = shared
    tile1, fields, inside, left, n_left, rows_i = edges
    EARLY_DVE, EARLY_POOL = (0, 1, 2), (3, 4)
    LINKS = 6
    with ExitStack() as ctx:
        def sb(name, shape, dt=F32):
            return ctx.enter_context(nc.sbuf_tensor(name, shape, dt))

        def sem(name):
            return ctx.enter_context(nc.semaphore(name))

        hot_t = sb("hot_t", [P, NB, CH], BF16)
        steps = sb("steps", [P, NB, SW])
        keep = sb("keep", [P, NB, SW], BF16)
        ranks = sb("ranks", [P, NB, SW], BF16)
        rank1 = sb("rank1", [P, CH], BF16)
        far = sb("far", [P, CH], BF16)
        slot = sb("slot", [P, P, CH], BF16)
        vals = sb("vals", [P, FIELDS, NB, CH], BF16)
        table = [sb(f"table{i}", [P, FIELDS, GRP, NB], BF16) for i in range(2)]
        cur = sb("cur", [P, BU + 1, FIELDS, GRP], BF16)
        hot = [sb(f"hot{i}", [P, 2, P, GRP], BF16) for i in range(3)]
        hot_w = [sb(f"hot_w{i}", [P, 3, P, GRP], BF16) for i in range(3)]
        block_sb = [sb(f"block_sb{i}", [P, GRP, P]) for i in range(3)]
        window = [sb(f"window{i}", [P, GRP, D]) for i in range(2)]
        row_of = sb("row_of", [P, 1], I32)
        landing = sb("landing", [P, D])

        def block_ps(i, j):
            return banks[2 * (i % 2) + j // 4][:, (j % 4) * P:(j % 4 + 1) * P]

        sum_ps = [banks[4 + i][:, 0:D] for i in range(2)]
        base_ps = banks[6][:, 0:NB]
        table_ps = banks[7][:, 0:FIELDS * NB].rearrange("p (f b) -> p f b", f=FIELDS)

        keep_set = sem("keep_set"); steps_done = sem("steps_done"); hot_done = sem("hot_done"); tiles_done = sem("tiles_done"); base_done = sem("base_done")
        chain = sem("chain"); slot_done = sem("slot_done"); vals_done = sem("vals_done"); early_done = sem("early_done"); table_made = sem("table_made")
        row_done = sem("row_done"); gathered = sem("gathered"); window_in = sem("window_in"); passed = sem("passed")
        dcur = sem("dcur"); unpacked = sem("unpacked")
        w_done = sem("w_done"); a_done = sem("a_done"); a_copied = sem("a_copied")
        o_done = sem("o_done"); o_added = sem("o_added")
        block = ctx.enter_context(nc.Block())

        def later(s):
            return not (isinstance(s, int) and s == 0)

        def schedule(eng, sort, begin, unit):
            sort(0)
            with eng.Fori(1, GRP) as s:
                sort(s)
            begin()

            def group(g, par, more):
                with eng.Fori(0, GRP - 1) as k:
                    unit(g, k, par, BU, more, True)
                unit(g, GRP - 1, par, BU + 1, more, more)

            with eng.Fori(0, NG // 2) as h:
                group(2 * h, 0, True)
                group(2 * h + 1, 1, True)
            group(NG - 1, 0, False)

        @block.sync
        def _(sp):
            sp.dma_start(disp_dram.rearrange("(p j) d -> p j d", p=P),
                         zeros[:, :].unsqueeze(1).broadcast_to([P, NJ, D])).then_inc(zeroed, 16)

        @block.gpsimd
        def _(pool):
            def values(s, parts):
                if later(s):
                    pool.wait_ge(table_made, s)
                pool.wait_ge(tiles_done, s + 1)
                for f in parts:
                    ins = pool.tensor_tensor(vals[:, f, :, :], hot_t[:, :, :],
                                             fields[:, f, bass.ds(s, 1), :].broadcast_to([P, NB, CH]), ALU.mult)
                ins.then_inc(vals_done, 1)

            def fetch(s, k, par):
                pool.tensor_copy(row_of[:, :], rows_i[:, bass.ds(s, 1)]).then_inc(row_done, 1)
                pool.wait_ge(row_done, s + 1)
                pool.sem_inc(passed, 1)
                pool.indirect_dma_start(out=landing[:, :], out_offset=None, in_=xn_dram,
                                        in_offset=bass.IndirectOffsetOnAxis(ap=row_of[:, 0:1], axis=0)).then_inc(gathered, 16)
                pool.wait_ge(gathered, (s + 1) * 16)
                pool.sem_inc(passed, 1)
                pool.tensor_copy(window[par][:, bass.ds(k, 1), :].rearrange("p a d -> p (a d)"), landing[:, :]).then_inc(window_in, 1)

            def sort(s):
                fetch(s, s, 0)
                values(s + 1, EARLY_POOL)

            def unit(g, k, par, n, more, after):
                s = g * GRP + k + GRP
                if more:
                    pool.wait_ge(o_done, g * NT + 2)
                    pool.sem_inc(passed, 1)
                    fetch(s, k, 1 - par)
                    values(s + 1, range(FIELDS))

            values(0, EARLY_POOL)
            schedule(pool, sort, lambda: None, unit)

        @block.tensor
        def _(pe):
            pe.sem_inc(a_done, 2)
            pe.sem_inc(o_done, 2)

            def base(s):
                pe.wait_ge(tiles_done, s + 1)
                for c in range(CH):
                    mm = pe.matmul(base_ps, before[:, :], hot_t[:, :, c], start=(c == 0), stop=(c == CH - 1))
                mm.then_inc(base_done, 1)

            def make_table(s):
                pe.wait_ge(vals_done, s + 1)
                pe.wait_ge(slot_done, s + 1)
                for c in range(CH):
                    mm = pe.matmul(table_ps, slot[:, :, c], vals[:, :, :, c], start=(c == 0), stop=(c == CH - 1))
                mm.then_inc(table_made, 1)

            def sort(s):
                base(s)
                if later(s):
                    make_table(s - 1)

            def begin():
                make_table(GRP - 1)
                blocks(0, 0, True)

            def blocks(it, i, first):
                pe.wait_ge(w_done, it + 2)
                pe.wait_ge(a_copied, it + 1 if first else it)
                for j in range(GRP):
                    for part in range(3):
                        mm = pe.matmul(block_ps(i, j), hot[i % 3][:, DST, :, j], hot_w[i % 3][:, part, :, j],
                                       start=(part == 0), stop=(part == 2))
                mm.then_inc(a_done, 1)

            def rows(it, i, par, first):
                pe.wait_ge(a_copied, it + 2)
                pe.wait_ge(o_added, it + 1 if first else it)
                for j in range(GRP):
                    mm = pe.matmul(sum_ps[i % 2], block_sb[i % 3][:, j, :], window[par][:, j, :], start=(j == 0), stop=(j == GRP - 1))
                mm.then_inc(o_done, 1)

            def unit(g, k, par, n, more, after):
                it = g * NT + k * BU
                s = g * GRP + k + GRP
                pe.wait_ge(window_in, (g + 1) * GRP)
                if more:
                    base(s)
                for i in range(n):
                    if i + 1 < n:
                        blocks(it + i + 1, i + 1, False)
                    elif after:
                        blocks(it + n, 0, n > BU)
                    rows(it + i, i, par, i == 0)
                    if more and i == 3:
                        make_table(s)

            schedule(pe, sort, begin, unit)

        @block.scalar
        def _(act):
            act.sem_inc(a_copied, 1)

            def widen(s):
                if later(s):
                    act.wait_ge(slot_done, s)
                act.wait_ge(tiles_done, s + 1)
                act.copy(steps[:, :, 2:SW], hot_t[:, :, :]).then_inc(steps_done, 1)

            def evacuate(it, i):
                act.wait_ge(a_done, it + 3)
                act.wait_ge(o_done, it + 2 if i == 0 else it + 1)
                for half in range(2):
                    ins = act.copy(block_sb[i % 3][:, 4 * half:4 * half + 4, :].rearrange("p m c -> p (m c)"), banks[2 * (i % 2) + half][:, :])
                ins.then_inc(a_copied, 1)

            def unit(g, k, par, n, more, after):
                it = g * NT + k * BU
                for i in range(n):
                    if i + 1 < n:
                        evacuate(it + i + 1, i + 1)
                    elif after:
                        evacuate(it + n, 0)
                    if more and i == 3:
                        widen(g * GRP + k + GRP + 1)

            widen(0)
            schedule(act, lambda s: widen(s + 1), lambda: evacuate(0, 0), unit)

        @block.vector
        def _(dve):
            dve.sem_inc(o_added, 1)
            dve.sem_inc(w_done, 1)
            dve.memset(steps[:, :, 0:2], 0.0).then_inc(keep_set, 1)
            dve.memset(keep[:, :, :], 1.0).then_inc(keep_set, 1)
            dve.wait_ge(keep_set, 2)
            dve.memset(keep[:, :, 0:1], 0.0).then_inc(keep_set, 1)
            dve.wait_ge(keep_set, 3)
            links = [0]

            def link(s, ins):
                links[0] += 1
                ins.then_inc(chain, 1)
                dve.wait_ge(chain, s * LINKS + links[0])

            def hot_tiles(s):
                if later(s):
                    dve.wait_ge(vals_done, s)
                dve.tensor_tensor(hot_t[:, :, :], iota1_c[:, 0:NB, :], tile1[:, bass.ds(s, 1), :].broadcast_to([P, NB, CH]),
                                  ALU.is_equal).then_inc(tiles_done, 1)

            def scan(s):
                links[0] = 0
                dve.wait_ge(steps_done, s + 1)
                dve.wait_ge(base_done, s + 1)
                link(s, dve.tensor_copy(steps[:, :, 0], base_ps))
                flat = lambda a: a.rearrange("p b c -> p (b c)")
                link(s, dve.tensor_tensor_scan(flat(ranks[:, :, :]), flat(keep[:, :, :]), flat(steps[:, :, :]), 0.0, ALU.mult, ALU.add))

            def rank(s):
                link(s, dve.tensor_tensor(ranks[:, :, 2:SW], ranks[:, :, 2:SW], hot_t[:, :, :], ALU.mult))
                if later(s):
                    dve.wait_ge(slot_done, s)
                with nc.allow_low_precision("one value of each sum is not 0"):
                    link(s, dve.tensor_reduce(rank1[:, :], ranks[:, :, 2:SW].rearrange("p b c -> p c b"), AX.X, ALU.add))
                link(s, dve.scalar_tensor_tensor(out=far[:, :], in0=rank1[:, :], scalar=P + 0.5,
                                                 in1=inside[:, bass.ds(s, 1), :].rearrange("p a c -> p (a c)"), op0=ALU.is_lt, op1=ALU.mult))
                out = left[:, bass.ds(s, 1), :].rearrange("p a c -> p (a c)")
                link(s, dve.tensor_scalar(out, far[:, :], 0.5, None, ALU.is_lt))
                dve.tensor_reduce(n_left[:, bass.ds(s, 1)], out, AX.X, ALU.add)

            def slots(s):
                if later(s):
                    dve.wait_ge(table_made, s)
                dve.tensor_tensor(slot[:, :, :], iota1_c[:, :, :], rank1[:, :].unsqueeze(1).broadcast_to([P, P, CH]),
                                  ALU.is_equal).then_inc(slot_done, 1)

            def unpack(s, k, par):
                assert links[0] == LINKS
                dve.wait_ge(table_made, s + 1)
                dve.tensor_copy(table[par][:, :, bass.ds(k, 1), :].rearrange("p f a b -> p f (a b)"), table_ps).then_inc(unpacked, 1)

            def early_values(s):
                if later(s):
                    dve.wait_ge(table_made, s)
                dve.wait_ge(tiles_done, s + 1)
                for f in EARLY_DVE:
                    ins = dve.tensor_tensor(vals[:, f, :, :], hot_t[:, :, :], fields[:, f, bass.ds(s, 1), :].broadcast_to([P, NB, CH]), ALU.mult)
                ins.then_inc(early_done, 1)

            def sort(s):
                scan(s)
                rank(s)
                if later(s):
                    unpack(s - 1, s - 1, 0)
                    early_values(s)
                slots(s)
                dve.wait_ge(early_done, s + 1)
                hot_tiles(s + 1)

            def take(unit_no, first_step, from_table, at):
                dve.wait_ge(w_done, first_step + 1)
                dve.tensor_copy(cur[:, :, :, :], from_table[:, :, :, at].rearrange("p f j i -> p i f j")).then_inc(dcur, 1)
                dve.wait_ge(dcur, unit_no + 1)

            def hots(it, i, wait):
                if wait:
                    dve.wait_ge(a_done, it + 2 if i == "first" else it)
                i = 0 if i == "first" else i
                dve.tensor_tensor(hot[i % 3][:, :, :, :], iota_j[:, :, :].unsqueeze(1).broadcast_to([P, 2, P, GRP]),
                                  cur[:, i, 0:2, :].unsqueeze(2).broadcast_to([P, 2, P, GRP]), ALU.is_equal).then_inc(hot_done, 1)
                dve.wait_ge(hot_done, it + 1)
                dve.tensor_tensor(hot_w[i % 3][:, :, :, :], hot[i % 3][:, SRC, :, :].unsqueeze(1).broadcast_to([P, 3, P, GRP]),
                                  cur[:, i, W:W + 3, :].unsqueeze(2).broadcast_to([P, 3, P, GRP]), ALU.mult).then_inc(w_done, 1)

            def begin():
                unpack(GRP - 1, GRP - 1, 0)
                early_values(GRP)
                dve.wait_ge(unpacked, GRP)
                take(0, 0, table[0], slice(0, BU + 1))
                hots(0, 0, False)
                hots(1, 1, False)

            def unit(g, k, par, n, more, after):
                u = g * GRP + k
                s = u + GRP
                it = g * NT + k * BU

                def add(i):
                    row = acc[:, bass.ds(k * BU + i, 1), :].rearrange("p a d -> p (a d)")
                    dve.wait_ge(o_done, it + i + 3)
                    dve.tensor_tensor(row, row, sum_ps[i % 2], ALU.add).then_inc(o_added, 1)

                for i in range(n):
                    if i + 2 < n:
                        hots(it + i + 2, i + 2, True)
                    elif after:
                        if i == n - 2:
                            if more:
                                unpack(s, k, 1 - par)
                            if n == BU:
                                take(u + 1, it + n, table[par], bass.ds((k + 1) * BU, BU + 1))
                            else:
                                dve.wait_ge(unpacked, (g + 2) * GRP)
                                take(u + 1, it + n, table[1 - par], slice(0, BU + 1))
                        hots(it + i + 2, "first" if n > BU and i == n - 2 else i + 2 - n, True)
                    if i > 0:
                        add(i - 1)
                    if more and i == 0:
                        scan(s)
                    if more and i == 1:
                        rank(s)
                    if more and i == 2:
                        slots(s)
                    if more and i == 3:
                        hot_tiles(s + 1)
                add(n - 1)

            hot_tiles(0)
            early_values(0)
            schedule(dve, sort, begin, unit)


def stragglers(nc, shared, edges, src, dst, edge_weight, xn_dram, E, G, TP, TR, NT, D):
    banks, acc, ident, iota, iota1_c, iota_j, ones_row, before = shared
    tile1, fields, inside, left, n_left, rows_i = edges
    SC = CH * P
    with ExitStack() as ctx:
        def sb(name, shape, dt=F32):
            return ctx.enter_context(nc.sbuf_tensor(name, shape, dt))

        def sem(name):
            return ctx.enter_context(nc.semaphore(name))

        ones_col = sb("ones_col", [P, 1])
        count = sb("count", [P, 1])
        total = sb("total", [1, 1], I32)
        src_l = sb("src_l", [P, G * CH], I32)
        dst_l = sb("dst_l", [P, G * CH], I32)
        w_l = sb("w_l", [P, G * CH])
        idx = sb("idx", [P, 1], I32)
        rows = sb("rows", [P, D])
        rel = sb("rel", [P, 1])
        w_one = sb("w_one", [P, 1])
        hot = sb("hot", [P, P])
        left_done = sem("left_done"); total_ps = sem("total_ps"); total_done = sem("total_done")
        padded = sem("padded"); loaded = sem("loaded"); idx_done = sem("idx_done"); rows_in = sem("rows_in")
        rel_done = sem("rel_done"); hot_done = sem("hot_done"); made = sem("made"); added = sem("added")
        passed = sem("passed")
        block = ctx.enter_context(nc.Block())
        Q = G * CH

        def some_left(eng):
            eng.wait_ge(total_done, 1)
            return eng.If(eng.value_load(total[0:1, 0:1], min_val=0, max_val=Q * P) > 0)

        @block.sync
        def _(sp):
            with some_left(sp):
                sp.wait_ge(padded, 3)
                for arr, to in ((dst, dst_l), (src, src_l), (edge_weight, w_l)):
                    at = to[:, :].rearrange("p (g c) -> p g c", c=CH)
                    body = arr[0:(G - 1) * SC].rearrange("(g p c) -> p g c", p=P, c=CH)
                    sp.dma_start(at[:, 0:G - 1, :], body).then_inc(loaded, 16)
                    tail = arr[(G - 1) * SC:(G - 1) * SC + TP * CH].rearrange("(p c) -> p c", c=CH)
                    sp.dma_start(at[0:TP, G - 1, :], tail).then_inc(loaded, 16)
                    rest = arr[E - TR:E].rearrange("(a c) -> a c", a=1)
                    sp.dma_start(at[TP:TP + 1, G - 1, 0:TR], rest).then_inc(loaded, 16)

        @block.gpsimd
        def _(pool):
            with some_left(pool):
                pool.wait_ge(loaded, 9 * 16)
                with pool.Fori(0, Q) as q:
                    pool.tensor_copy(idx[:, :], dst_l[:, bass.ds(q, 1)]).then_inc(idx_done, 1)
                    pool.wait_ge(idx_done, q + 1)
                    pool.wait_ge(made, q * NT + 1)
                    pool.sem_inc(passed, 1)
                    pool.indirect_dma_start(out=rows[:, :], out_offset=None, in_=xn_dram,
                                            in_offset=bass.IndirectOffsetOnAxis(ap=idx[:, 0:1], axis=0)).then_inc(rows_in, 16)
                    pool.wait_ge(rows_in, (q + 1) * 16)

        @block.tensor
        def _(pe):
            pe.sem_inc(made, 1)
            pe.wait_ge(left_done, 2)
            pe.matmul(banks[0][0:1, 0:1], count[:, :], ones_col[:, :], start=True, stop=True).then_inc(total_ps, 1)
            with some_left(pe):
                with pe.Fori(0, Q) as q:
                    pe.wait_ge(rows_in, (q + 1) * 16)
                    pe.sem_inc(passed, 1)
                    with pe.Fori(0, NT) as b:
                        pe.wait_ge(hot_done, q * NT + b + 1)
                        pe.wait_ge(added, q * NT + b + 1)
                        pe.matmul(banks[1][:, 0:D], hot[:, :], rows[:, :], start=True, stop=True).then_inc(made, 1)

        @block.vector
        def _(dve):
            dve.sem_inc(added, 1)
            dve.memset(ones_col[:, :], 1.0).then_inc(left_done, 1)
            dve.tensor_reduce(count[:, :], n_left[:, :], AX.X, ALU.add).then_inc(left_done, 1)
            dve.wait_ge(total_ps, 1)
            dve.tensor_copy(total[:, :], banks[0][0:1, 0:1]).then_inc(total_done, 1)
            with some_left(dve):
                dve.memset(src_l[:, (G - 1) * CH:Q], NB * P).then_inc(padded, 1)
                dve.memset(dst_l[:, (G - 1) * CH:Q], 0).then_inc(padded, 1)
                dve.memset(w_l[:, (G - 1) * CH:Q], 0.0).then_inc(padded, 1)
                dve.wait_ge(loaded, 9 * 16)
                dve.tensor_tensor(w_l[:, :], w_l[:, :], left[:, :, :].rearrange("p g c -> p (g c)"), ALU.mult).then_inc(padded, 1)
                dve.wait_ge(padded, 4)
                with dve.Fori(0, Q) as q:
                    dve.wait_ge(added, q * NT + 1)
                    dve.tensor_copy(rel[:, :], src_l[:, bass.ds(q, 1)]).then_inc(rel_done, 1)
                    dve.tensor_copy(w_one[:, :], w_l[:, bass.ds(q, 1)]).then_inc(rel_done, 1)
                    with dve.Fori(0, NT) as b:
                        dve.wait_ge(rel_done, q * (NT + 2) + b + 2)
                        dve.wait_ge(made, q * NT + b + 1)
                        dve.tensor_scalar(hot[:, :], iota[:, :], rel[:, 0:1], w_one[:, 0:1], ALU.is_equal, ALU.mult).then_inc(hot_done, 1)
                        dve.wait_ge(hot_done, q * NT + b + 1)
                        dve.tensor_scalar(rel[:, :], rel[:, :], float(-P), None, ALU.add).then_inc(rel_done, 1)
                        dve.wait_ge(made, q * NT + b + 2)
                        row = acc[:, bass.ds(b, 1), :].rearrange("p a d -> p (a d)")
                        dve.tensor_tensor(row, row, banks[1][:, 0:D], ALU.add).then_inc(added, 1)

def route(nc, shared, share, slot, tile_e, zeroed, rows_dram, disp_dram, bias_dram, Wg, bg, bias, b1, b2, NT, NJ, D):
    banks, acc, ident, iota, iota1_c, iota_j, ones_row, before = shared
    X = Wg.shape[1]
    NS = NT * 2
    B1, B2 = b1.shape[0] * b1.shape[1], b2.shape[0] * b2.shape[1]
    BC = (B1 + B2) // P
    NU = NT // 2
    NR = tile_e.shape[1]
    assert X ** (RUN + 1) <= 1 << 24 and NR * RUN >= NJ - 1
    assert NU % 2 == 0 and NT % UNROLL == 0
    with ExitStack() as ctx:
        def sb(name, shape, dt=F32):
            return ctx.enter_context(nc.sbuf_tensor(name, shape, dt))

        def sem(name):
            return ctx.enter_context(nc.semaphore(name))

        wg = sb("wg", [P, 2, X])
        gb_row = sb("gb_row", [1, 2 * X])
        gb = sb("gb", [P, X])
        b_all = sb("b_all", [P, BC])
        b_part = sb("b_part", [P, 3, BC], BF16)
        stats = sb("stats2", [P, NT, 6])
        mv = sb("mv2", [P, 2, NT])
        dev = sb("dev2", [P, NT])
        rstd = sb("rstd2", [P, NT])
        zT = [sb(f"rzT{i}", [P, 2, 2, P]) for i in range(2)]
        eps = sb("eps2", [P, 1])
        ones = sb("ones", [P, P], BF16)
        back = sb("back", [P, X])
        logits = sb("logits", [P, NT, X])
        hits = sb("hits", [P, NT, X])
        best = sb("best", [P, 2, NT])
        which = sb("which", [P, 2, NT])
        hot = sb("chosen", [P, NT, 2, X])
        scan = [sb(f"scan{i}", [P, NS, X]) for i in range(2)]
        rows_of = sb("rows_of", [P, X], BF16)
        ahead = sb("ahead", [P, X])
        tiles_i = sb("tiles_i", [P, X], I32)
        tiles = sb("tiles", [P, X])
        upto = sb("upto", [P, X])
        start = sb("start2", [P, X])
        slot_f = sb("slot_f", [P, NS])
        gap = sb("gap", [P, NT])
        ex = sb("ex", [P, NT])
        den = sb("den", [P, NT])
        later = sb("later", [1, NJ, X])
        tile_f = sb("tile_f", [1, (NR + 1) * RUN])
        packed = sb("packed", [1, NR])
        turn_ps, logit_ps, small_ps = banks[0:2], banks[2], banks[3]

        small_in = sem("small_in"); rows_out = sem("rows_out"); parts_done = sem("parts_done"); parts_out = sem("parts_out")
        var_done = sem("var_done"); dev_done = sem("dev_done"); z_done = sem("z_done"); turned = sem("turned")
        zT_done = sem("zT_done"); logit = sem("logit"); gb_made = sem("gb_made"); gap_done = sem("gap_done"); ex_done = sem("ex_done")
        counted = sem("counted"); ranked = sem("ranked"); slots_done = sem("slots_done"); sent = sem("sent")
        aggr = sem("aggr"); step = sem("step"); eps_set = sem("eps_set")
        block = ctx.enter_context(nc.Block())

        @block.sync
        def _(sp):
            sp.dma_start(rows_dram.rearrange("(t p) d -> p t d", p=P), acc[:, :, :]).then_inc(rows_out, 16)
            sp.dma_start(wg[:, :, :], Wg.rearrange("(k p) e -> p k e", p=P)).then_inc(small_in, 16)
            sp.dma_start(gb_row[:, 0:X], bg.rearrange("(a e) -> a e", a=1)).then_inc(small_in, 16)
            sp.dma_start(gb_row[:, X:2 * X], bias.rearrange("(a e) -> a e", a=1)).then_inc(small_in, 16)
            flat1 = b1.rearrange("e f -> (e f)")
            flat2 = b2.rearrange("e f -> (e f)")
            whole = B1 // BC
            cut = B1 - whole * BC
            sp.dma_start(b_all[0:whole, :], flat1[0:whole * BC].rearrange("(p c) -> p c", c=BC)).then_inc(small_in, 16)
            sp.dma_start(b_all[whole:whole + 1, 0:cut], flat1[whole * BC:B1].rearrange("(a c) -> a c", a=1)).then_inc(small_in, 16)
            sp.dma_start(b_all[whole:whole + 1, cut:BC], flat2[0:BC - cut].rearrange("(a c) -> a c", a=1)).then_inc(small_in, 16)
            sp.dma_start(b_all[whole + 1:P, :], flat2[BC - cut:B2].rearrange("(p c) -> p c", c=BC)).then_inc(small_in, 16)
            sp.wait_ge(parts_done, 1)
            sp.dma_start(bias_dram.rearrange("s (p c) -> p s c", p=P), b_part[:, :, :]).then_inc(parts_out, 16)
            sp.wait_ge(parts_out, 16)

        @block.gpsimd
        def _(pool):
            pool.memset(ones[:, :], 1.0)
            pool.memset(eps[:, :], EPS).then_inc(eps_set, 1)
            pool.wait_ge(zeroed, 16)
            pool.wait_ge(slots_done, 1)
            for t in range(NT):
                for s in range(2):
                    pool.indirect_dma_start(out=disp_dram, out_offset=bass.IndirectOffsetOnAxis(ap=slot[:, t, s:s + 1], axis=0),
                                            in_=acc[:, t, :], in_offset=None).then_inc(sent, 16)
            pool.wait_ge(sent, NS * 16)

        @block.scalar
        def _(act):
            act.wait_ge(eps_set, 1)
            act.wait_ge(var_done, 1)
            act.activation(dev[:, :], mv[:, 1, :], ACT.Sqrt, bias=eps[:, 0:1]).then_inc(dev_done, 1)

            def take(u, i, n):
                act.wait_ge(turned, u + 1)
                act.wait_ge(logit, u + 1)
                act.copy(zT[i][:, 0:n, :, :].rearrange("p t k c -> p (t k c)"), turn_ps[i][:, 0:n * 2 * P]).then_inc(zT_done, 1)

            with act.Fori(0, NU // 2) as h:
                take(2 * h, 0, 2)
                take(2 * h + 1, 1, 2)
            take(NU, 0, 1)
            act.wait_ge(gap_done, 1)
            act.activation(ex[:, :], gap[:, :], ACT.Exp).then_inc(ex_done, 1)

        @block.tensor
        def _(pe):
            pe.wait_ge(small_in, 7 * 16)
            pe.matmul(small_ps[:, 0:2 * X], ones_row[:, :], gb_row[:, :], start=True, stop=True).then_inc(gb_made, 1)
            pe.sem_inc(logit, 2)
            pe.sem_inc(zT_done, 2)

            def turn(u, i, n):
                pe.wait_ge(z_done, 2 * u + n)
                pe.wait_ge(zT_done, u + 1)
                for t in range(n):
                    for k in range(2):
                        tr = pe.transpose(turn_ps[i][:, (2 * t + k) * P:(2 * t + k + 1) * P],
                                          acc[:, 2 * u + t, k * P:(k + 1) * P], ident[:, :])
                tr.then_inc(turned, 1)

            def product(u, i, n):
                pe.wait_ge(zT_done, u + 3)
                for t in range(n):
                    at = (2 * u + t) * X
                    for k in range(2):
                        mm = pe.matmul(logit_ps[:, at:at + X], zT[i][:, t, k, :], wg[:, k, :], start=(k == 0), stop=(k == 1))
                mm.then_inc(logit, 1)

            turn(0, 0, 2)
            for u in range(NU + 1):
                if u < NU:
                    turn(u + 1, (u + 1) % 2, 2 if u + 1 < NU else 1)
                product(u, u % 2, 2 if u < NU else 1)
            pe.wait_ge(counted, 1)
            pe.matmul(small_ps[:, 0:X], before[:, :], rows_of[:, :], start=True, stop=True)
            pe.matmul(small_ps[:, X:2 * X], ones[:, :], rows_of[:, :], start=True, stop=True).then_inc(ranked, 1)

        @block.vector
        def _(dve):
            n = [0]

            def then(ins):
                n[0] += 1
                ins.then_inc(step, 1)
                dve.wait_ge(step, n[0])

            row_statistics(dve, stats, acc, aggr, NT)
            merge_stats(dve, then, stats, mv, D)
            dve.sem_inc(var_done, 1)
            dve.wait_ge(dev_done, 1)
            then(dve.reciprocal(rstd[:, :], dev[:, :]))
            dve.wait_ge(rows_out, 16)
            with dve.Fori(0, NT // UNROLL) as q:
                for i in range(UNROLL):
                    t = q * UNROLL + i
                    row = acc[:, bass.ds(t, 1), :].rearrange("p a d -> p (a d)")
                    ins = dve.tensor_scalar(row, row, mv[:, 0, bass.ds(t, 1)], rstd[:, bass.ds(t, 1)], ALU.subtract, ALU.mult)
                    ins.then_inc(z_done, 1)
            dve.wait_ge(small_in, 7 * 16)
            for part in range(3):
                then(dve.tensor_copy(b_part[:, part, :], b_all[:, :]))
                if part < 2:
                    then(dve.tensor_tensor(b_all[:, :], b_all[:, :], b_part[:, part, :], ALU.subtract))
            dve.sem_inc(parts_done, 1)
            then(dve.tensor_scalar(back[:, :], iota[:, 0:X], float(-X), None, ALU.add))
            dve.wait_ge(gb_made, 1)
            then(dve.tensor_copy(gb[:, :], small_ps[:, 0:X]))
            then(dve.tensor_tensor(gb[:, :], gb[:, :], small_ps[:, X:2 * X], ALU.add))
            dve.wait_ge(logit, NU + 1 + 2)
            then(dve.tensor_tensor(logits[:, :, :], logit_ps[:, 0:NT * X].rearrange("p (t e) -> p t e", e=X),
                                   gb[:, :].unsqueeze(1).broadcast_to([P, NT, X]), ALU.add))
            for s in range(2):
                then(dve.tensor_reduce(best[:, s, :], logits[:, :, :], AX.X, ALU.max))
                then(dve.tensor_tensor(hits[:, :, :], logits[:, :, :], best[:, s, :].unsqueeze(2).broadcast_to([P, NT, X]), ALU.is_equal))
                then(dve.tensor_tensor(hits[:, :, :], hits[:, :, :], back[:, :].unsqueeze(1).broadcast_to([P, NT, X]), ALU.mult))
                then(dve.tensor_reduce(which[:, s, :], hits[:, :, :], AX.X, ALU.min))
                then(dve.tensor_tensor(hot[:, :, s, :], back[:, :].unsqueeze(1).broadcast_to([P, NT, X]),
                                       which[:, s, :].unsqueeze(2).broadcast_to([P, NT, X]), ALU.is_equal))
                if s == 0:
                    then(dve.scalar_tensor_tensor(out=logits[:, :, :], in0=hot[:, :, 0, :], scalar=-3e38, in1=logits[:, :, :], op0=ALU.mult, op1=ALU.add))
            dve.tensor_tensor(gap[:, :], best[:, 1, :], best[:, 0, :], ALU.subtract).then_inc(gap_done, 1)
            now = hot[:, :, :, :].rearrange("p t s e -> p (t s) e")
            k, i = 1, 0
            while k < NS:
                nxt = scan[i][:, :, :]
                dve.tensor_copy(nxt[:, 0:k, :], now[:, 0:k, :])
                then(dve.tensor_tensor(nxt[:, k:NS, :], now[:, k:NS, :], now[:, 0:NS - k, :], ALU.add))
                now, k, i = nxt, 2 * k, 1 - i
            then(dve.tensor_copy(rows_of[:, :], now[:, NS - 1, :]))
            dve.sem_inc(counted, 1)
            dve.wait_ge(ranked, 1)
            then(dve.tensor_copy(ahead[:, :], small_ps[:, 0:X]))
            then(dve.tensor_scalar(tiles[:, :], small_ps[:, X:2 * X], float(P - 1), None, ALU.add))
            then(dve.tensor_copy(tiles_i[:, :], tiles[:, :]))
            then(dve.tensor_scalar(tiles_i[:, :], tiles_i[:, :], 7, None, ALU.logical_shift_right))
            then(dve.tensor_copy(tiles[:, :], tiles_i[:, :]))
            then(dve.tensor_copy(upto[:, :], tiles[:, :]))
            for e in range(1, X):
                then(dve.tensor_tensor(upto[:, e:e + 1], upto[:, e - 1:e], tiles[:, e:e + 1], ALU.add))
            then(dve.tensor_tensor(start[:, :], upto[:, :], tiles[:, :], ALU.subtract))
            then(dve.scalar_tensor_tensor(out=ahead[:, :], in0=start[:, :], scalar=float(P), in1=ahead[:, :], op0=ALU.mult, op1=ALU.add))
            then(dve.tensor_tensor(now, now, ahead[:, :].unsqueeze(1).broadcast_to([P, NS, X]), ALU.add))
            then(dve.tensor_tensor(now, now, hot[:, :, :, :].rearrange("p t s e -> p (t s) e"), ALU.mult))
            then(dve.tensor_reduce(slot_f[:, :], now, AX.X, ALU.add))
            dve.tensor_scalar(slot[:, :, :].rearrange("p t s -> p (t s)"), slot_f[:, :], -1.0, None, ALU.add).then_inc(slots_done, 1)
            then(dve.tensor_tensor(later[:, :, 0:X - 1], iota[0:1, 0:NJ].unsqueeze(2).broadcast_to([1, NJ, X - 1]),
                                   upto[0:1, 0:X - 1].unsqueeze(1).broadcast_to([1, NJ, X - 1]), ALU.is_ge))
            then(dve.memset(tile_f[:, :], 0.0))
            then(dve.tensor_reduce(tile_f[:, 0:NJ], later[:, :, 0:X - 1], AX.X, ALU.add))
            then(dve.tensor_copy(packed[:, :], tile_f[:, 0:NR * RUN].rearrange("a (q s) -> a q s", s=RUN)[:, :, 0]))
            for i in range(1, RUN + 1):
                digit = tile_f[:, i // RUN * RUN:i // RUN * RUN + NR * RUN].rearrange("a (q s) -> a q s", s=RUN)[:, :, i % RUN]
                then(dve.scalar_tensor_tensor(out=packed[:, :], in0=digit, scalar=float(X ** i), in1=packed[:, :], op0=ALU.mult, op1=ALU.add))
            dve.tensor_copy(tile_e[:, :], packed[:, :])
            dve.wait_ge(ex_done, 1)
            then(dve.tensor_scalar(den[:, :], ex[:, :], 1.0, None, ALU.add))
            then(dve.reciprocal(den[:, :], den[:, :]))
            dve.tensor_copy(share[:, :, 0], den[:, :])
            dve.tensor_tensor(share[:, :, 1], ex[:, :], den[:, :], ALU.mult)


def experts(nc, banks, ident, tile_e, disp_dram, y_dram, bias_dram, W1, W2, NJ, D):
    X, F = W1.shape[0], W1.shape[2]
    FC = F // P
    with ExitStack() as ctx:
        def sb(name, shape, dt=F32):
            return ctx.enter_context(nc.sbuf_tensor(name, shape, dt))

        def sem(name):
            return ctx.enter_context(nc.semaphore(name))

        w1 = [sb(f"w1_{i}", [P, X, 2 * F], F32R) for i in range(2)]
        w2 = [sb(f"w2_{i}", [P, X, FC * D], F32R) for i in range(2)]
        bx = sb("bx", [3, X * (F + D)], BF16)
        ones3 = sb("ones3", [3, P], BF16)
        stage = [sb(f"stage{i}", [P, FC * D]) for i in range(2)]
        zin = [sb(f"zin{i}", [P, D]) for i in range(2)]
        zh = [sb(f"zh{i}", [P, 2, P], F32R) for i in range(2)]
        zl = [sb(f"zl{i}", [P, 2, P], F32R) for i in range(2)]
        h = [sb(f"h{i}", [P, F]) for i in range(2)]
        hh = [sb(f"hh{i}", [P, FC, P], F32R) for i in range(2)]
        hl = [sb(f"hl{i}", [P, FC, P], F32R) for i in range(2)]
        y = [sb(f"y{i}", [P, D]) for i in range(2)]
        zt_ps, hid_ps, ht_ps, y_ps = banks[0:2], banks[2:4], banks[4:6], banks[6:8]

        w_in = [sem(f"w_in{i}") for i in range(2)]
        bias_in = sem("bias_in"); hi_done = sem("hi_done"); w_split = sem("w_split"); ones_set = sem("ones_set")
        z_in = [sem(f"z_in{i}") for i in range(2)]
        y_out = [sem(f"y_out{i}") for i in range(2)]
        z_turned = sem("z_turned"); zh_done = sem("zh_done"); zl_done = sem("zl_done"); hid = sem("hid"); relu_done = sem("relu_done")
        h_turned = sem("h_turned"); hh_done = sem("hh_done"); hl_done = sem("hl_done"); y_made = sem("y_made"); y_done = sem("y_done")
        block = ctx.enter_context(nc.Block())
        LAST = NJ - 1
        EARLY = 2
        assert NJ % 2 == 1 and (NJ - 3) % RUN == 0 and RUN % 2 == 0

        @block.sync
        def _(sp):
            def load(j, i):
                sp.wait_ge(z_turned, j + 1)
                sp.dma_start(zin[i][:, :], disp_dram[bass.ds(j * P, P), :]).then_inc(z_in[i], 16)

            def store(j, i):
                sp.wait_ge(y_done, j + 3)
                sp.dma_start(y_dram[bass.ds(j * P, P), :], y[i][:, :]).then_inc(y_out[i], 16)

            for j in range(3):
                load(j, j % 2)
            with sp.Fori(0, (NJ - 3) // 2) as q:
                load(2 * q + 3, 1)
                store(2 * q, 0)
                load(2 * q + 4, 0)
                store(2 * q + 1, 1)
            for j in range(NJ - 3, NJ):
                store(j, j % 2)
            sp.wait_ge(y_out[0], 16 * (NJ // 2 + 1))
            sp.wait_ge(y_out[1], 16 * (NJ // 2))

        @block.gpsimd
        def _(pool):
            pool.memset(ones3[:, :], 1.0).then_inc(ones_set, 1)

            def split(n):
                hi, lo = (w[:, n // 2, :] for w in (w2 if n % 2 else w1))
                pool.wait_ge(w_in[n % 2], 16 * (n // 2 + 1))
                pool.tensor_copy(hi, stage[n % 2][:, :]).then_inc(hi_done, 1)
                pool.wait_ge(hi_done, n + 1)
                pool.tensor_tensor(lo, stage[n % 2][:, :], hi.bitcast(F32), ALU.subtract).then_inc(w_split, 1)


            for n in range(2 * X):
                e = n // 2
                if n >= 2:
                    pool.wait_ge(w_split, n - 1)
                if n % 2 == 0:
                    pool.dma_start(stage[0][:, :].rearrange("p (k h) -> p k h", k=2), W1[e].rearrange("(k p) h -> p k h", p=P)).then_inc(w_in[0], 16)
                else:
                    pool.dma_start(stage[1][:, :].rearrange("p (c d) -> p c d", c=FC), W2[e].rearrange("(c p) d -> p c d", p=P)).then_inc(w_in[1], 16)
                if n > EARLY:
                    split(n - 1)
            split(2 * X - 1)

        @block.scalar
        def _(act):
            act.dma_start(bx[:, :], bias_dram).then_inc(bias_in, 16)

            for n in range(EARLY):
                act.wait_ge(w_in[n % 2], 16 * (n // 2 + 1))
                act.copy((w2 if n % 2 else w1)[0][:, n // 2, :], stage[n % 2][:, :]).then_inc(hi_done, 1)

            def high_z(j, i):
                act.wait_ge(z_turned, j + 3)
                act.wait_ge(hid, j + 1)
                act.copy(zh[i][:, :, :], zt_ps[i][:, 0:2 * P].rearrange("p (k c) -> p k c", k=2)).then_inc(zh_done, 1)

            def relu(j, i):
                act.wait_ge(hid, j + 3)
                act.wait_ge(h_turned, j + 1)
                act.activation(h[i][:, :], hid_ps[i][:, :], ACT.Relu).then_inc(relu_done, 1)

            def high_h(j, i):
                act.wait_ge(h_turned, j + 3)
                act.wait_ge(y_made, j + 1)
                act.copy(hh[i][:, :, :], ht_ps[i][:, :].rearrange("p (c t) -> p c t", c=FC)).then_inc(hh_done, 1)

            def one(j, i):
                high_h(j, i)
                high_z(j + 2, i)
                relu(j + 1, 1 - i)

            high_z(0, 0)
            high_z(1, 1)
            relu(0, 0)
            with act.Fori(0, (NJ - 3) // 2) as q:
                one(2 * q, 0)
                one(2 * q + 1, 1)
            one(NJ - 3, 0)
            high_h(NJ - 2, 1)
            relu(NJ - 1, 0)
            high_h(NJ - 1, 0)

        @block.tensor
        def _(pe):
            for s in (z_turned, hid, h_turned, y_made):
                pe.sem_inc(s, 2)
            THREE = ((0, 0), (0, 1), (1, 0))
            bits = X.bit_length() - 1
            assert X == 1 << bits

            def run_experts(q):
                packed = pe.value_load(tile_e[0:1, bass.ds(q, 1)], min_val=0, max_val=X ** (RUN + 1) - 1)
                return [(packed >> (bits * i)) & (X - 1) for i in range(RUN + 1)]

            def turn_z(j, i, pair):
                pe.wait_ge(z_in[i], 16 * (pair + 1))
                pe.wait_ge(zl_done, j + 1)
                for k in range(2):
                    tr = pe.transpose(zt_ps[i][:, k * P:(k + 1) * P], zin[i][:, k * P:(k + 1) * P], ident[:, :])
                tr.then_inc(z_turned, 1)

            def hidden(j, i, e):
                pe.wait_ge(w_split, e * 2 + 2)
                pe.wait_ge(zl_done, j + 3)
                pe.wait_ge(relu_done, j + 1)
                pe.matmul(hid_ps[i][:, :], ones3[:, :], bx[:, bass.ds(e * F, F)], start=True, stop=False)
                zz = (zh[i], zl[i])
                for m, (k, (a, b)) in enumerate((k, ab) for k in range(2) for ab in THREE):
                    w = w1[b][:, bass.ds(e, 1), k * F:(k + 1) * F].rearrange("p a f -> p (a f)")
                    mm = pe.matmul(hid_ps[i][:, :], zz[a][:, k, :], w, start=False, stop=(m == 5))
                mm.then_inc(hid, 1)

            def turn_h(j, i):
                pe.wait_ge(relu_done, j + 3)
                pe.wait_ge(hl_done, j + 1)
                for c in range(FC):
                    tr = pe.transpose(ht_ps[i][:, c * P:(c + 1) * P], h[i][:, c * P:(c + 1) * P], ident[:, :])
                tr.then_inc(h_turned, 1)

            def second(j, i, e):
                pe.wait_ge(hl_done, j + 3)
                pe.wait_ge(y_done, j + 1)
                pe.matmul(y_ps[i][:, 0:D], ones3[:, :], bx[:, bass.ds(e * D + X * F, D)], start=True, stop=False)
                parts = (hh[i], hl[i])
                for m, (c, (a, b)) in enumerate((c, ab) for c in range(FC) for ab in THREE):
                    w = w2[b][:, bass.ds(e, 1), c * D:(c + 1) * D].rearrange("p a d -> p (a d)")
                    mm = pe.matmul(y_ps[i][:, 0:D], parts[a][:, c, :], w, start=False, stop=(m == 3 * FC - 1))
                mm.then_inc(y_made, 1)

            def turns(j, i, pair):
                turn_h(j, i)
                turn_z(j + 2, i, pair)

            turn_z(0, 0, 0)
            turn_z(1, 1, 0)
            pe.wait_ge(bias_in, 16)
            pe.wait_ge(ones_set, 1)
            hidden(0, 0, run_experts(0)[0])
            RUNS = (NJ - 3) // RUN
            with pe.Fori(0, RUNS) as q:
                for i in range(RUN):
                    j = RUN * q + i
                    turns(j, i % 2, q * (RUN // 2) + i // 2 + 1)
                    if i == 0:
                        e = run_experts(q)
                    hidden(j + 1, (i + 1) % 2, e[i + 1])
                    second(j, i % 2, e[i])
            turns(NJ - 3, 0, NJ // 2)
            e = run_experts(RUNS)
            hidden(NJ - 2, 1, e[1])
            second(NJ - 3, 0, e[0])
            turn_h(NJ - 2, 1)
            hidden(NJ - 1, 0, e[2])
            second(NJ - 2, 1, e[1])
            turn_h(NJ - 1, 0)
            second(NJ - 1, 0, e[2])

        @block.vector
        def _(dve):
            dve.sem_inc(relu_done, 2)
            dve.sem_inc(zl_done, 2)
            dve.sem_inc(hl_done, 2)
            dve.sem_inc(y_done, 2)
            for n in range(EARLY):
                dve.wait_ge(hi_done, n + 1)
                hi, lo = (w[:, n // 2, :] for w in (w2 if n % 2 else w1))
                dve.tensor_tensor(lo, stage[n % 2][:, :], hi.bitcast(F32), ALU.subtract).then_inc(w_split, 1)

            def low_z(j, i):
                dve.wait_ge(zh_done, j + 1)
                dve.tensor_tensor(zl[i][:, :, :], zt_ps[i][:, 0:2 * P].rearrange("p (k c) -> p k c", k=2),
                                  zh[i][:, :, :].bitcast(F32), ALU.subtract).then_inc(zl_done, 1)

            def low_h(j, i):
                dve.wait_ge(hh_done, j + 1)
                dve.tensor_tensor(hl[i][:, :, :], ht_ps[i][:, :].rearrange("p (c t) -> p c t", c=FC),
                                  hh[i][:, :, :].bitcast(F32), ALU.subtract).then_inc(hl_done, 1)

            def take_y(j, i, q):
                dve.wait_ge(y_made, j + 3)
                if not (isinstance(q, int) and q == 0):
                    dve.wait_ge(y_out[i], 16 * q)
                dve.tensor_copy(y[i][:, :], y_ps[i][:, 0:D]).then_inc(y_done, 1)

            def one(j, i, q):
                low_h(j, i)
                low_z(j + 2, i)
                take_y(j, i, q)

            low_z(0, 0)
            low_z(1, 1)
            one(0, 0, 0)
            one(1, 1, 0)
            with dve.Fori(1, (NJ - 3) // 2) as q:
                one(2 * q, 0, q)
                one(2 * q + 1, 1, q)
            one(NJ - 3, 0, NJ // 2 - 1)
            low_h(NJ - 2, 1)
            take_y(NJ - 2, 1, NJ // 2 - 1)
            low_h(NJ - 1, 0)
            take_y(NJ - 1, 0, NJ // 2)


def combine(nc, share, slot, rows_dram, y_dram, out, NT, TAIL, N, D):
    LAST = NT - 1
    B = 4
    with ExitStack() as ctx:
        def sb(name, shape, dt=F32):
            return ctx.enter_context(nc.sbuf_tensor(name, shape, dt))

        def sem(name):
            return ctx.enter_context(nc.semaphore(name))

        rows = sb("c_rows", [P, B, D])
        picked = sb("picked", [P, B, 2, D])
        part = sb("part", [P, B, D])
        row_in = [sem(f"row_in{i}") for i in range(B)]
        y_in = [sem(f"y_in{i}") for i in range(B)]
        out_done = [sem(f"out_done{i}") for i in range(B)]
        halved = sem("halved"); added = sem("added")
        block = ctx.enter_context(nc.Block())
        assert NT % B == 1

        def fours(eng, one):
            with eng.Fori(0, NT // B) as q:
                for i in range(B):
                    one(B * q + i, i, q + 1)
            one(LAST, 0, NT // B + 1)

        @block.gpsimd
        def _(pool):
            pool.sem_inc(added, B)
            for t in range(NT):
                pool.wait_ge(added, t + 1)
                for s in range(2):
                    pool.indirect_dma_start(out=picked[:, t % B, s, :], out_offset=None, in_=y_dram,
                                            in_offset=bass.IndirectOffsetOnAxis(ap=slot[:, t, s:s + 1], axis=0)).then_inc(y_in[t % B], 16)

        @block.scalar
        def _(act):
            act.sem_inc(halved, B)

            def load(t, i, turn):
                act.wait_ge(halved, t + 1)
                act.dma_start(rows[:, i, :], rows_dram[bass.ds(t * P, P), :]).then_inc(row_in[i], 16)

            fours(act, load)

        @block.vector
        def _(dve):
            for i in range(B):
                dve.sem_inc(out_done[i], 16)

            def add(t, i, turn):
                dve.wait_ge(row_in[i], 16 * turn)
                dve.wait_ge(y_in[i], 32 * turn)
                dve.wait_ge(out_done[i], 16 * turn)
                dve.scalar_tensor_tensor(out=part[:, i, :], in0=picked[:, i, 0, :], scalar=share[:, bass.ds(t, 1), 0],
                                         in1=rows[:, i, :], op0=ALU.mult, op1=ALU.add).then_inc(halved, 1)
                dve.wait_ge(halved, t + B + 1)
                dve.scalar_tensor_tensor(out=part[:, i, :], in0=picked[:, i, 1, :], scalar=share[:, bass.ds(t, 1), 1],
                                         in1=part[:, i, :], op0=ALU.mult, op1=ALU.add).then_inc(added, 1)

            fours(dve, add)

        @block.sync
        def _(sp):
            def store(t, i, turn):
                sp.wait_ge(added, t + B + 1)
                if isinstance(t, int):
                    sp.dma_start(out[N - TAIL:N, :], part[0:TAIL, i, :]).then_inc(out_done[i], 16)
                else:
                    sp.dma_start(out[bass.ds(t * P, P), :], part[:, i, :]).then_inc(out_done[i], 16)

            fours(sp, store)
            for i in range(B):
                sp.wait_ge(out_done[i], 16 * (NT // B + 1 + (i == 0)))


_INS = ['x', 'src', 'dst', 'edge_weight', 'node_vec1', 'L0_mix_wq', 'L0_mix_wk', 'L0_mix_wv', 'L0_mix_wo', 'L0_mix_bo',
        'L0_mix_ln_k_g', 'L0_mix_ln_k_b', 'L0_mix_ln_v_g', 'L0_mix_ln_v_b', 'L0_ffn_Wg', 'L0_ffn_bg', 'L0_ffn_bias',
        'L0_ffn_W1', 'L0_ffn_b1', 'L0_ffn_W2', 'L0_ffn_b2']
_OUTS = [((6250, 256), 'float32')]


def kernel(**inputs):
    import numpy as _np
    import concourse.bacc as _bacc
    from concourse import mybir as _mybir
    from concourse.bass_utils import run_bass_kernel_spmd as _run

    nc = _bacc.Bacc("TRN2", target_bir_lowering=False, num_devices=1)
    arrays, args = {}, []
    for name in _INS:
        a = _np.ascontiguousarray(inputs[name])
        arrays[f"in_{name}_dram"] = a
        args.append(nc.dram_tensor(f"in_{name}_dram", a.shape, _mybir.dt.from_np(a.dtype), kind="ExternalInput").ap())
    for i, (shape, dtype) in enumerate(_OUTS):
        dt = _mybir.dt.from_np(_np.dtype(dtype))
        args.append(nc.dram_tensor(f"out_{i}_dram", shape, dt, kind="ExternalOutput").ap())
    gps_layer(nc, *args)
    r = _run(nc, [arrays], core_ids=[0])
    got = tuple(r.results[0][f"out_{i}_dram"] for i in range(len(_OUTS)))
    return got[0]
```
